# Optimizing a Trainium2 kernel written in Bass

```python
import numpy as np
import jax
import jax.numpy as jnp

def _softmax(x, axis=-1):
    return jax.nn.softmax(x, axis=axis)

def _gelu(x):
    return jax.nn.gelu(x, approximate=True)

def _silu(x):
    return jax.nn.silu(x)

def _sigmoid(x):
    return jax.nn.sigmoid(x)

def _layernorm(x, axis=-1, eps=1e-05):
    m = jnp.mean(x, axis=axis, keepdims=True)
    v = jnp.var(x, axis=axis, keepdims=True)
    return (x - m) / jnp.sqrt(v + eps)

def _scatter_add(tgt, idx, src, axis=0):
    return tgt.at[idx].add(src)

def _segment_sum(src, seg, n):
    return jax.ops.segment_sum(src, seg, n)
kernel_name = 'mk_seq_preln_d2_jaxref_r8_b7c2e4'

def setup_inputs(seed: int=0):
    np.random.seed(seed)
    _w = jnp.asarray

    def _L0_attn_setup():
        import jax, jax.numpy as jnp
        import numpy as np
        B, T = (4, 256)
        D_MODEL = 128
        N_HEADS = 8
        HEAD_DIM = 32
        KV_LRANK = 64

        def _orthogonalize_per_head(w):
            chunks = w.reshape(N_HEADS, HEAD_DIM, D_MODEL)

            def ns(m):
                A = m @ m.T
                Bm = 1.5 * jnp.eye(HEAD_DIM, dtype=m.dtype) - 0.5 * A
                return Bm @ m
            return jax.vmap(ns)(chunks).reshape(w.shape)
        key = jax.random.key(seed)
        ks = jax.random.split(key, 6)

        def lin(k, out_dim, in_dim):
            bound = 1.0 / np.sqrt(in_dim)
            return jax.random.uniform(k, (out_dim, in_dim), jnp.float32, -bound, bound)
        Wq = _orthogonalize_per_head(lin(ks[0], N_HEADS * HEAD_DIM, D_MODEL))
        return {'x': jax.random.normal(ks[1], (B, T, D_MODEL), jnp.float32), 'Wq': Wq, 'Wkv_down': lin(ks[2], KV_LRANK, D_MODEL), 'Wk_up': lin(ks[3], N_HEADS * HEAD_DIM, KV_LRANK), 'Wv_up': lin(ks[4], N_HEADS * HEAD_DIM, KV_LRANK), 'Wo': lin(ks[5], D_MODEL, N_HEADS * HEAD_DIM)}
    _L0_attn_in = _L0_attn_setup()

    def _L0_ffn_setup():
        import jax, jax.numpy as jnp
        import numpy as np
        B, S, D, E, F = (2, 128, 128, 14, 256)
        key = jax.random.key(seed)
        k0, k1, k2, k3 = jax.random.split(key, 4)
        h = jax.random.normal(k0, (B, S, D), jnp.float32)
        gate_w = jax.random.normal(k1, (E, D), jnp.float32) * 0.02
        w1 = jax.random.normal(k2, (E, D, F), jnp.float32) * (1.0 / np.sqrt(D).astype(np.float32))
        b1 = jnp.zeros((E, F), jnp.float32)
        w2 = jax.random.normal(k3, (E, F, D), jnp.float32) * (1.0 / np.sqrt(F).astype(np.float32))
        b2 = jnp.zeros((E, D), jnp.float32)
        return {'h': h, 'gate_w': gate_w, 'w1': w1, 'b1': b1, 'w2': w2, 'b2': b2}
    _L0_ffn_in = _L0_ffn_setup()

    def _L1_attn_setup():
        import jax, jax.numpy as jnp
        import numpy as np
        D_MODEL = 128
        N_HEADS = 16
        HEAD_DIM = D_MODEL // N_HEADS
        EPS = 1e-06

        def _feature_map(t):
            return jax.nn.relu(t) + EPS
        key = jax.random.key(seed)
        ks = jax.random.split(key, 5)
        b, s = (2, 256)
        x = jax.random.normal(ks[0], (b, s, D_MODEL), dtype=jnp.float32)
        scale = 1.0 / np.sqrt(D_MODEL)
        Wq = jax.random.normal(ks[1], (D_MODEL, D_MODEL), dtype=jnp.float32) * scale
        Wk = jax.random.normal(ks[2], (D_MODEL, D_MODEL), dtype=jnp.float32) * scale
        Wv = jax.random.normal(ks[3], (D_MODEL, D_MODEL), dtype=jnp.float32) * scale
        Wo = jax.random.normal(ks[4], (D_MODEL, D_MODEL), dtype=jnp.float32) * scale
        return {'x': x, 'Wq': Wq, 'Wk': Wk, 'Wv': Wv, 'Wo': Wo}
    _L1_attn_in = _L1_attn_setup()

    def _L1_ffn_setup():
        import math
        import jax, jax.numpy as jnp
        import numpy as np
        D_MODEL = 128
        D_FF = 512
        N_EXPERTS = 8
        CAPACITY_FACTOR = 1.25
        L, B = (64, 8)

        def _route(tokens, router_w):
            T = tokens.shape[0]
            E = router_w.shape[0]
            capacity = int(math.ceil(T / E * CAPACITY_FACTOR))
            logits = tokens @ router_w.T
            probs = jax.nn.softmax(logits, axis=-1)
            top1_idx = jnp.argmax(probs, axis=-1)
            top1_prob = jnp.max(probs, axis=-1)
            order = jnp.lexsort((-top1_prob, top1_idx))
            sorted_e = top1_idx[order]
            counts = jnp.bincount(top1_idx, length=E)
            start = jnp.cumsum(counts) - counts
            pos_in_group = jnp.arange(T) - start[sorted_e]
            keep_sorted = pos_in_group < capacity
            keep = jnp.zeros((T,), bool).at[order].set(keep_sorted)
            return jnp.where(keep, top1_idx, 0).astype(jnp.int32)
        key = jax.random.key(seed)
        ks = jax.random.split(key, 6)
        s_in = 1.0 / math.sqrt(D_MODEL)
        s_ff = 1.0 / math.sqrt(D_FF)
        return {'x': jax.random.normal(ks[0], (L, B, D_MODEL), dtype=jnp.float32), 'router_w': jax.random.uniform(ks[1], (N_EXPERTS, D_MODEL), minval=-s_in, maxval=s_in), 'W1': jax.random.uniform(ks[2], (N_EXPERTS, D_MODEL, D_FF), minval=-s_in, maxval=s_in), 'b1': jax.random.uniform(ks[3], (N_EXPERTS, D_FF), minval=-s_in, maxval=s_in), 'W2': jax.random.uniform(ks[4], (N_EXPERTS, D_FF, D_MODEL), minval=-s_ff, maxval=s_ff), 'b2': jax.random.uniform(ks[5], (N_EXPERTS, D_MODEL), minval=-s_ff, maxval=s_ff)}
    _L1_ffn_in = _L1_ffn_setup()
    _d = {'L0_attn_x': _L0_attn_in['x'], 'L0_attn_Wq': _L0_attn_in['Wq'], 'L0_attn_Wkv_down': _L0_attn_in['Wkv_down'], 'L0_attn_Wk_up': _L0_attn_in['Wk_up'], 'L0_attn_Wv_up': _L0_attn_in['Wv_up'], 'L0_attn_Wo': _L0_attn_in['Wo'], 'L0_ffn_gate_w': _L0_ffn_in['gate_w'], 'L0_ffn_w1': _L0_ffn_in['w1'], 'L0_ffn_b1': _L0_ffn_in['b1'], 'L0_ffn_w2': _L0_ffn_in['w2'], 'L0_ffn_b2': _L0_ffn_in['b2'], 'L1_attn_Wq': _L1_attn_in['Wq'], 'L1_attn_Wk': _L1_attn_in['Wk'], 'L1_attn_Wv': _L1_attn_in['Wv'], 'L1_attn_Wo': _L1_attn_in['Wo'], 'L1_ffn_router_w': _L1_ffn_in['router_w'], 'L1_ffn_W1': _L1_ffn_in['W1'], 'L1_ffn_b1': _L1_ffn_in['b1'], 'L1_ffn_W2': _L1_ffn_in['W2'], 'L1_ffn_b2': _L1_ffn_in['b2']}
    _x0 = _d['L0_attn_x']
    _d['L0_attn_x'] = jax.random.normal(jax.random.fold_in(jax.random.key(seed), 1), (8, 1024, 128), dtype=_x0.dtype)
    del _x0
    return _d

def reference(L0_attn_x, L0_attn_Wq, L0_attn_Wkv_down, L0_attn_Wk_up, L0_attn_Wv_up, L0_attn_Wo, L0_ffn_gate_w, L0_ffn_w1, L0_ffn_b1, L0_ffn_w2, L0_ffn_b2, L1_attn_Wq, L1_attn_Wk, L1_attn_Wv, L1_attn_Wo, L1_ffn_router_w, L1_ffn_W1, L1_ffn_b1, L1_ffn_W2, L1_ffn_b2):

    def _L0_attn_ref(x, Wq, Wkv_down, Wk_up, Wv_up, Wo):
        import jax, jax.numpy as jnp
        import numpy as np
        B, T = (4, 256)
        D_MODEL = 128
        N_HEADS = 8
        HEAD_DIM = 32
        KV_LRANK = 64

        def _orthogonalize_per_head(w):
            chunks = w.reshape(N_HEADS, HEAD_DIM, D_MODEL)

            def ns(m):
                A = m @ m.T
                Bm = 1.5 * jnp.eye(HEAD_DIM, dtype=m.dtype) - 0.5 * A
                return Bm @ m
            return jax.vmap(ns)(chunks).reshape(w.shape)
        b, t, _ = x.shape
        q = (x @ Wq.T).reshape(b, t, N_HEADS, HEAD_DIM)
        kv_latent = x @ Wkv_down.T
        k = (kv_latent @ Wk_up.T).reshape(b, t, N_HEADS, HEAD_DIM)
        v = (kv_latent @ Wv_up.T).reshape(b, t, N_HEADS, HEAD_DIM)
        scale = HEAD_DIM ** (-0.5)
        scores = jnp.einsum('bqhd,bkhd->bhqk', q, k) * scale
        attn = jax.nn.softmax(scores, axis=-1)
        out = jnp.einsum('bhqk,bkhd->bqhd', attn, v)
        out = out.reshape(b, t, N_HEADS * HEAD_DIM)
        return out @ Wo.T

    def _L0_ffn_ref(h, gate_w, w1, b1, w2, b2):
        import jax, jax.numpy as jnp
        import numpy as np
        B, S, D, E, F = (2, 128, 128, 14, 256)
        Bb, Ss, Dd = h.shape
        x = h.reshape(Bb * Ss, Dd)
        logits = x @ gate_w.T
        probs = jax.nn.softmax(logits, axis=-1)
        top2_p, top2_i = jax.lax.top_k(probs, 2)
        w = top2_p / jnp.maximum(top2_p.sum(-1, keepdims=True), 1e-10)
        hh = jnp.einsum('nd,edf->nef', x, w1) + b1
        hh = jax.nn.gelu(hh, approximate=False)
        all_out = jnp.einsum('nef,efd->ned', hh, w2) + b2
        n = jnp.arange(x.shape[0])
        out0 = all_out[n, top2_i[:, 0]]
        out1 = all_out[n, top2_i[:, 1]]
        moe_out = w[:, 0:1] * out0 + w[:, 1:2] * out1
        result = jnp.clip(x + moe_out, -100.0, 100.0).reshape(Bb, Ss, Dd)
        return result

    def _L1_attn_ref(x, Wq, Wk, Wv, Wo):
        import jax, jax.numpy as jnp
        import numpy as np
        D_MODEL = 128
        N_HEADS = 16
        HEAD_DIM = D_MODEL // N_HEADS
        EPS = 1e-06

        def _feature_map(t):
            return jax.nn.relu(t) + EPS
        b, s, _ = x.shape
        q = (x @ Wq.T).reshape(b, s, N_HEADS, HEAD_DIM)
        k = (x @ Wk.T).reshape(b, s, N_HEADS, HEAD_DIM)
        v = (x @ Wv.T).reshape(b, s, N_HEADS, HEAD_DIM)
        q = _feature_map(q).transpose(0, 2, 1, 3)
        k = _feature_map(k).transpose(0, 2, 1, 3)
        v = v.transpose(0, 2, 1, 3)
        kv = jnp.einsum('bhsd,bhsm->bhsdm', k, v)
        kv_cum = jnp.cumsum(kv, axis=2)
        out = jnp.einsum('bhsd,bhsdm->bhsm', q, kv_cum)
        k_cum = jnp.cumsum(k, axis=2)
        z = 1.0 / (jnp.einsum('bhsd,bhsd->bhs', q, k_cum) + EPS)
        out = out * z[..., None]
        out = out.transpose(0, 2, 1, 3).reshape(b, s, D_MODEL)
        return out @ Wo.T

    def _L1_ffn_ref(x, router_w, W1, b1, W2, b2):
        import math
        import jax, jax.numpy as jnp
        import numpy as np
        D_MODEL = 128
        D_FF = 512
        N_EXPERTS = 8
        CAPACITY_FACTOR = 1.25
        L, B = (64, 8)

        def _route(tokens, router_w):
            T = tokens.shape[0]
            E = router_w.shape[0]
            capacity = int(math.ceil(T / E * CAPACITY_FACTOR))
            logits = tokens @ router_w.T
            probs = jax.nn.softmax(logits, axis=-1)
            top1_idx = jnp.argmax(probs, axis=-1)
            top1_prob = jnp.max(probs, axis=-1)
            order = jnp.lexsort((-top1_prob, top1_idx))
            sorted_e = top1_idx[order]
            counts = jnp.bincount(top1_idx, length=E)
            start = jnp.cumsum(counts) - counts
            pos_in_group = jnp.arange(T) - start[sorted_e]
            keep_sorted = pos_in_group < capacity
            keep = jnp.zeros((T,), bool).at[order].set(keep_sorted)
            return jnp.where(keep, top1_idx, 0).astype(jnp.int32)
        Lx, Bx, D = x.shape
        T = Lx * Bx
        E = router_w.shape[0]
        tokens = x.reshape(T, D)
        final_e = _route(tokens, router_w)
        out = jnp.zeros_like(tokens)
        for e in range(E):
            h = jax.nn.relu(tokens @ W1[e] + b1[e])
            y = h @ W2[e] + b2[e]
            out = out + jnp.where((final_e == e)[:, None], y, 0.0)
        return out.reshape(Lx, Bx, D)
    x = L0_attn_x
    x = x + _L0_attn_ref(_layernorm(x, axis=-1), L0_attn_Wq, L0_attn_Wkv_down, L0_attn_Wk_up, L0_attn_Wv_up, L0_attn_Wo)
    x = x + _L0_ffn_ref(_layernorm(x, axis=-1), L0_ffn_gate_w, L0_ffn_w1, L0_ffn_b1, L0_ffn_w2, L0_ffn_b2)
    x = x + _L1_attn_ref(_layernorm(x, axis=-1), L1_attn_Wq, L1_attn_Wk, L1_attn_Wv, L1_attn_Wo)
    x = x + _L1_ffn_ref(_layernorm(x, axis=-1), L1_ffn_router_w, L1_ffn_W1, L1_ffn_b1, L1_ffn_W2, L1_ffn_b2)
    return x

_drawn_inputs = setup_inputs


def setup_inputs(seed=0):
    import zlib

    import numpy as np

    out = dict(_drawn_inputs(seed))
    spreads = {'L0_ffn_b1': (0.0, 0.1), 'L0_ffn_b2': (0.0, 0.1)}
    factors = {'L1_ffn_b1': 5.535, 'L1_ffn_b2': 4.466}
    for name, (base, spread) in spreads.items():
        noise = np.random.default_rng([zlib.crc32(name.encode()), seed]).standard_normal(out[name].shape)
        drawn = base * np.exp(spread * noise) if base else spread * noise
        out[name] = jnp.asarray(drawn.astype(out[name].dtype))
    for name, factor in factors.items():
        out[name] = (out[name] * factor).astype(out[name].dtype)
    return out
```

```python
from contextlib import ExitStack

import concourse.bass as bass
from concourse import mybir

F32 = mybir.dt.float32
BF16 = mybir.dt.bfloat16
I32 = mybir.dt.int32
U32 = mybir.dt.uint32
ALU = mybir.AluOpType
ACT = mybir.ActivationFunctionType
AX = mybir.AxisListType

P = 128
B, T, D = 8, 1024, 128
NTOK = B * T
TILES = NTOK // P
G = 4
GT = G * P
GROUPS = TILES // G
H0, DH0, LR = 8, 32, 64
HW0 = H0 * DH0
UNITS = B * H0
KT = T // P
HALF = 512
SCALE = float(DH0) ** -0.5
H1, DH1 = 16, 8
KV1 = H1 * DH1 * DH1
E0, F0 = 14, 256
E1, F1 = 8, 512
BT = 256
REGION = NTOK + BT
LN_EPS = 1e-5
FEAT_EPS = 1e-6
CAP1 = -(-NTOK // E1 * 5 // 4)
assert CAP1 == 1280


def surplus_of(choices, experts):
    return blocks_of(choices, experts) - choices * NTOK // BT


def blocks_of(choices, experts):
    n = choices * NTOK // BT + experts - 1
    return n + n % 2


def apart(eng, sem, value, passed):
    eng.wait_ge(sem, value)
    eng.sem_inc(passed, 1)


def layer_norm(nc, dve, passed, act_done, x, xn, stats, mv, rstd, stats_done, var_done, rstd_done, xn_done, n):
    for t in range(G):
        last = nc.vector.bn_stats(stats[:, t, :], x[:, t, :])
    last.then_inc(stats_done, 1)
    apart(dve, stats_done, 2 * n + 1, passed)
    for t in range(G):
        last = nc.vector.bn_aggr(mv[:, t, :], stats[:, t, :])
    last.then_inc(stats_done, 1)
    dve.wait_ge(stats_done, 2 * n + 2)
    nc.vector.tensor_scalar(rstd[:, :], mv[:, :, 1], LN_EPS, None, ALU.add).then_inc(var_done, 1)
    dve.wait_ge(act_done, n + 1)
    nc.vector.reciprocal(rstd[:, :], rstd[:, :]).then_inc(rstd_done, 1)
    dve.wait_ge(rstd_done, n + 1)
    for t in range(G):
        last = nc.vector.tensor_scalar(xn[:, t, :], x[:, t, :], mv[:, t, 0:1], rstd[:, t:t + 1],
                                       ALU.subtract, ALU.mult)
    last.then_inc(xn_done, 1)


def constants(nc, c):
    with nc.semaphore("c_fill") as fill, nc.semaphore("c_done") as done, nc.Block() as block:
        @block.gpsimd
        def _(pool):
            nc.gpsimd.memset(c["ident"][:, :], 0.0).then_inc(fill, 1)
            nc.gpsimd.memset(c["tri"][:, :], 1.0).then_inc(fill, 1)
            nc.gpsimd.memset(c["stri"][:, :], 1.0).then_inc(fill, 1)
            nc.gpsimd.memset(c["ones"][:, :], 1.0).then_inc(fill, 1)
            pool.wait_ge(fill, 4)
            nc.gpsimd.affine_select(out=c["ident"][:, :], in_=c["ident"][:, :], compare_op=ALU.not_equal,
                                    fill=1.0, base=0, pattern=[[-1, P]], channel_multiplier=1).then_inc(done, 1)
            nc.gpsimd.affine_select(out=c["tri"][:, :], in_=c["tri"][:, :], compare_op=ALU.is_ge,
                                    fill=0.0, base=0, pattern=[[1, P]], channel_multiplier=-1).then_inc(done, 1)
            nc.gpsimd.affine_select(out=c["stri"][:, :], in_=c["stri"][:, :], compare_op=ALU.is_gt,
                                    fill=0.0, base=0, pattern=[[1, P]], channel_multiplier=-1).then_inc(done, 1)
            nc.gpsimd.iota(c["iota"][:, :], pattern=[[1, 128]], base=0, channel_multiplier=0,
                           allow_small_or_imprecise_dtypes=True).then_inc(done, 1)
            pool.wait_ge(done, 4)


def project(nc, c, X, x_in, w, q3, k3, v0):
    with ExitStack() as ctx:
        def sb(name, shape, dt=F32):
            return ctx.enter_context(nc.sbuf_tensor(name, shape, dt))

        def sem(name):
            return ctx.enter_context(nc.semaphore(name))

        wq, wd = sb("wq", [P, HW0]), sb("wd", [P, LR])
        wku, wvu = sb("wku", [LR, HW0]), sb("wvu", [LR, HW0])
        stats, mv, rstd = sb("pj_stats", [P, G, 6]), sb("pj_mv", [P, G, 2]), sb("pj_rstd", [P, G])
        xn = sb("pj_xn", [P, G, D])
        xT = sb("pj_xT", [P, GT])
        lat = sb("pj_lat", [LR, GT])
        hi, mid, lo = (sb(f"pj_{n}", [P, 4, GT], BF16) for n in ("hi", "mid", "lo"))
        rest = sb("pj_rest", [P, 4, GT])
        vs = sb("pj_v", [P, H0, KT, DH0])
        p_xT = ctx.enter_context(nc.psum_tensor("pj_pxT", [P, GT], F32))
        p_lat = ctx.enter_context(nc.psum_tensor("pj_plat", [P, GT], F32))
        p_qk = ctx.enter_context(nc.psum_tensor("pj_pqk", [P, 4, GT], F32))
        p_v = ctx.enter_context(nc.psum_tensor("pj_pv", [P, G, HW0], F32))
        (x_in_s, w_in, stats_d, var_d, root_d, rstd_d, xn_d, pxT_d, xT_d, plat_d, lat_d, pqk_d, hi_d,
         rest_d, mid_d, lo_d, pv_d, v_d, hi_out, mid_out, lo_out, v_out, passed) = (
            sem(f"pj_{n}") for n in ("x_in0", "w_in", "stats", "var", "root", "rstd", "xn", "pxT", "xT",
                                     "plat", "lat", "pqk", "hi_d", "rest_d", "mid_d", "lo_d", "pv",
                                     "v_d", "hi_out", "mid_out", "lo_out", "v_out", "passed"))
        x_in_s = [x_in_s, sem("pj_x_in1")]
        block = ctx.enter_context(nc.Block())
        x_v = x_in.rearrange("b t d -> (b t) d").rearrange("(g t p) d -> p g t d", p=P, t=G)
        X_g = X[:, :].rearrange("p (g t d) -> p g t d", g=GROUPS, t=G)

        def batch(sp, b, more):
            for half in range(2):
                g = b * 2 + half
                if more:
                    apart(sp, xn_d, g + 1, passed)
                    sp.dma_start(X_g[:, bass.ds(g + 2, 1)].rearrange("p o t d -> p (o t) d"),
                                 x_v[:, bass.ds(g + 2, 1)].rearrange("p o t d -> p (o t) d")).then_inc(x_in_s[half], 16)
                for part, plane, ready, sent in ((0, hi, hi_d, hi_out), (1, mid, mid_d, mid_out), (2, lo, lo_d, lo_out)):
                    apart(sp, ready, g + 1, passed)
                    for s, dram in ((0, q3), (2, k3)):
                        for cc in range(2):
                            dst = dram[part, bass.ds(b * H0 + cc * 4, 4), :, half * GT:(half + 1) * GT]
                            sp.dma_start(dst.rearrange("h d t -> (h d) t"), plane[:, s + cc, :]).then_inc(sent, 16)
            apart(sp, v_d, b * 2 + 2, passed)
            sp.dma_start(v0[bass.ds(b * H0, H0)].rearrange("h p x -> p h x"),
                         vs[:, :, :, :].rearrange("p h k d -> p h (k d)")).then_inc(v_out, 16)

        @block.sync
        def _(sp):
            for dst, src in ((wq, w["WqT"]), (wd, w["WdT"]), (wku, w["WkuT"]), (wvu, w["WvuT"])):
                sp.dma_start(dst[:, :], src).then_inc(w_in, 16)
            for g in range(2):
                sp.dma_start(X_g[:, g], x_v[:, g]).then_inc(x_in_s[g], 16)
            with sp.Fori(0, B - 1) as b:
                batch(sp, b, True)
            batch(sp, B - 1, False)
            sp.wait_ge(hi_out, GROUPS * 64)
            sp.wait_ge(mid_out, GROUPS * 64)
            sp.wait_ge(lo_out, GROUPS * 64)
            sp.wait_ge(v_out, B * 16)

        @block.tensor
        def _(pe):
            pe.wait_ge(w_in, 64)
            with pe.Fori(0, B) as b:
                for half in range(2):
                    g = b * 2 + half
                    pe.wait_ge(xn_d, g + 1)
                    for t in range(G):
                        mm = nc.tensor.transpose(p_xT[:, t * P:(t + 1) * P], xn[:, t, :], c["ident"][:, :])
                    mm.then_inc(pxT_d, 1)
                    pe.wait_ge(xT_d, g + 1)
                    nc.tensor.matmul(p_lat[0:LR, :], wd[:, :], xT[:, :], start=True, stop=True).then_inc(plat_d, 1)
                    pe.wait_ge(hi_d, g)
                    pe.wait_ge(rest_d, g)
                    for cc in range(2):
                        nc.tensor.matmul(p_qk[:, cc, :], wq[:, cc * P:(cc + 1) * P], xT[:, :], start=True, stop=True)
                    pe.wait_ge(lat_d, g + 1)
                    for cc in range(2):
                        mm = nc.tensor.matmul(p_qk[:, 2 + cc, :], wku[:, cc * P:(cc + 1) * P], lat[:, :], start=True, stop=True)
                    mm.then_inc(pqk_d, 1)
                    pe.wait_ge(v_d, g)
                    for t in range(G):
                        mm = nc.tensor.matmul(p_v[:, t, :], lat[:, t * P:(t + 1) * P], wvu[:, :], start=True, stop=True)
                    mm.then_inc(pv_d, 1)

        @block.scalar
        def _(act):
            with act.Fori(0, B) as b:
                for half in range(2):
                    g = b * 2 + half
                    act.wait_ge(var_d, g + 1)
                    nc.scalar.activation(rstd[:, :], rstd[:, :], ACT.Sqrt).then_inc(root_d, 1)
                    act.wait_ge(pxT_d, g + 1)
                    act.wait_ge(pqk_d, g)
                    nc.scalar.copy(xT[:, :], p_xT[:, :]).then_inc(xT_d, 1)
                    act.wait_ge(plat_d, g + 1)
                    act.wait_ge(pv_d, g)
                    nc.scalar.copy(lat[:, :], p_lat[0:LR, :]).then_inc(lat_d, 1)
                    act.wait_ge(pqk_d, g + 1)
                    act.wait_ge(hi_out, g * 64)
                    nc.scalar.copy(hi[:, :, :], p_qk[:, :, :]).then_inc(hi_d, 1)
                    act.wait_ge(rest_d, g + 1)
                    act.wait_ge(mid_out, g * 64)
                    nc.scalar.copy(mid[:, :, :], rest[:, :, :]).then_inc(mid_d, 1)

        @block.vector
        def _(dve):
            with dve.Fori(0, B) as b:
                for half in range(2):
                    g = b * 2 + half
                    dve.wait_ge(x_in_s[half], (b + 1) * 16)
                    dve.wait_ge(pxT_d, g)
                    layer_norm(nc, dve, passed, root_d, X[:, bass.ds(g * GT, GT)].rearrange("p (t d) -> p t d", t=G),
                               xn[:, :, :], stats, mv, rstd, stats_d, var_d, rstd_d, xn_d, g)
                    dve.wait_ge(hi_d, g + 1)
                    dve.wait_ge(lo_d, g)
                    nc.vector.tensor_tensor(rest[:, :, :], p_qk[:, :, :], hi[:, :, :], ALU.subtract).then_inc(rest_d, 1)
                    dve.wait_ge(pv_d, g + 1)
                    if half == 0:
                        dve.wait_ge(v_out, b * 16)
                    nc.vector.tensor_copy(vs[:, :, half * G:(half + 1) * G, :].rearrange("p h k d -> p k h d"),
                                          p_v[:, :, :].rearrange("p k (h d) -> p k h d", h=H0)).then_inc(v_d, 1)

        @block.gpsimd
        def _(pool):
            with pool.Fori(0, B) as b:
                for half in range(2):
                    g = b * 2 + half
                    pool.wait_ge(mid_d, g + 1)
                    pool.wait_ge(lo_out, g * 64)
                    nc.gpsimd.tensor_tensor(lo[:, :, :], rest[:, :, :], mid[:, :, :], ALU.subtract).then_inc(lo_d, 1)


SLOTS = 4
PROBS = 4
MAX_PLAN = (4, 4, 2, 2, 2, 2, 0, 0)


def attend(nc, c, q3, k3, v0, o0):
    with ExitStack() as ctx:
        def sb(name, shape, dt=F32):
            return ctx.enter_context(nc.sbuf_tensor(name, shape, dt))

        def sem(name):
            return ctx.enter_context(nc.semaphore(name))

        qa = [sb(f"qa{s}", [P, T], BF16) for s in range(SLOTS)]
        ka = [sb(f"ka{s}", [P, T], BF16) for s in range(SLOTS)]
        KB = 2 * DH0 + 2
        qb = [sb(f"qb{s}", [KB, T], BF16) for s in range(SLOTS)]
        kb = [sb(f"kb{s}", [KB, T], BF16) for s in range(SLOTS)]
        v = [sb(f"vh{s}", [P, KT, DH0]) for s in range(SLOTS)]
        probs = [sb(f"probs{i}", [P, T]) for i in range(PROBS)]
        halfmax, rowmax = sb("halfmax", [P, 2, KT]), sb("rowmax", [P, KT])
        max_hi, max_lo = (sb(n, [KT, P], BF16) for n in ("max_hi", "max_lo"))
        inv = sb("inv", [P, T // 4])
        ot = [sb(f"ot{i}", [P, T // 4]) for i in range(2)]
        p_s = [ctx.enter_context(nc.psum_tensor(f"p_s{i}", [P, T], F32)) for i in range(2)]
        p_m = [ctx.enter_context(nc.psum_tensor(f"p_m{i}", [P, HALF], F32)) for i in range(2)]
        p_o = [ctx.enter_context(nc.psum_tensor(f"p_o{i}", [P, 2, T // 4], F32)) for i in range(2)]
        operands_in = [sem(f"at_operands_in{s}") for s in range(SLOTS)]
        o_out = [sem(f"at_o_out{i}") for i in range(2)]
        (ones_d, max_scores, max_read, max_row, max_T, max_parts, max_hi_d, max_in, scores,
         probs_d, pv_d, inv_d, o_d, passed) = (
            sem(f"at_{n}") for n in ("ones", "max_scores", "max_read", "max_row", "max_T",
                                     "max_parts", "max_hi_d", "max_in", "scores", "probs", "pv", "inv",
                                     "o", "passed"))
        PV0, O0 = SLOTS * KT, 2
        LAST = UNITS // SLOTS - 1
        block = ctx.enter_context(nc.Block())

        @block.sync
        def _(sp):
            with sp.Fori(0, UNITS // SLOTS) as r:
                for s in range(SLOTS):
                    u = r * SLOTS + s
                    apart(sp, pv_d, PV0 + (u - SLOTS + 1) * KT, passed)
                    for i, (qp, kp) in enumerate(((0, 0), (0, 1), (1, 0), (1, 1))):
                        rows = slice(i * DH0, (i + 1) * DH0)
                        sp.dma_start(qa[s][rows, :], q3[qp, bass.ds(u, 1)].rearrange("o d t -> (o d) t")).then_inc(operands_in[s], 16)
                        sp.dma_start(ka[s][rows, :], k3[kp, bass.ds(u, 1)].rearrange("o d t -> (o d) t")).then_inc(operands_in[s], 16)
                    for i, (qp, kp) in enumerate(((0, 2), (2, 0))):
                        rows = slice(i * DH0, (i + 1) * DH0)
                        sp.dma_start(qb[s][rows, :], q3[qp, bass.ds(u, 1)].rearrange("o d t -> (o d) t")).then_inc(operands_in[s], 16)
                        sp.dma_start(kb[s][rows, :], k3[kp, bass.ds(u, 1)].rearrange("o d t -> (o d) t")).then_inc(operands_in[s], 16)
                    sp.dma_start(v[s][:, :, :].rearrange("p k d -> p (k d)"),
                                 v0[bass.ds(u, 1)].rearrange("o p x -> (o p) x")).then_inc(operands_in[s], 16)

        LOADS = 13

        def after(r, s):
            return (r, s + 1) if s + 1 < SLOTS else (r + 1, 0)

        def rows_of_maxima(pool, r, s):
            apart(pool, max_parts, r * SLOTS + s + 1, passed)
            pool.dma_start(qb[s][2 * DH0:2 * DH0 + 1, :], max_hi[:, :]).then_inc(max_in, 16)
            pool.dma_start(qb[s][2 * DH0 + 1:KB, :], max_lo[:, :]).then_inc(max_in, 16)

        def store(pool, r, s):
            u = r * SLOTS + s
            apart(pool, o_d, O0 + u + 1, passed)
            for j in range(4):
                pool.dma_start(o0[bass.ds(u, 1), :, j * (T // 4):(j + 1) * (T // 4)].rearrange("o d t -> (o d) t"),
                               ot[s % 2][j * DH0:(j + 1) * DH0, :]).then_inc(o_out[s % 2], 16)

        @block.gpsimd
        def _(pool):
            for s in range(SLOTS):
                nc.gpsimd.memset(kb[s][2 * DH0:KB, :], 1.0).then_inc(ones_d, 1)
            rows_of_maxima(pool, 0, 0)
            with pool.Fori(0, UNITS // SLOTS - 1) as r:
                for s in range(SLOTS):
                    rows_of_maxima(pool, *after(r, s))
                    store(pool, r, s)
            for s in range(SLOTS):
                if s + 1 < SLOTS:
                    rows_of_maxima(pool, LAST, s + 1)
                store(pool, LAST, s)
            for out_s in o_out:
                pool.wait_ge(out_s, UNITS // 2 * 64)

        def max_half(pe, r, s, n):
            u = r * SLOTS + s
            if n == 0:
                pe.wait_ge(operands_in[s], (r + 1) * LOADS * 16)
                pe.wait_ge(max_parts, u)
            if n >= 2:
                pe.wait_ge(max_read, u * 16 + n - 1)
            nc.tensor.matmul(p_m[n % 2][:, :], qa[s][:, (n // 2) * P:(n // 2 + 1) * P],
                             ka[s][:, (n % 2) * HALF:(n % 2 + 1) * HALF], start=True, stop=True).then_inc(max_scores, 1)

        def max_turn(pe, r, s):
            u = r * SLOTS + s
            pe.wait_ge(max_row, u + 1)
            nc.tensor.transpose(p_m[0][0:KT, 0:P], rowmax[:, :], c["ident"][:, :]).then_inc(max_T, 1)

        def score(pe, r, s, k):
            u = r * SLOTS + s
            if k == 0:
                pe.wait_ge(max_in, (u + 1) * 32)
            g = u * KT + k
            if not (isinstance(g, int) and g < 2):
                pe.wait_ge(probs_d, g - 1)
            for h in range(2):
                cols, q = slice(k * P, (k + 1) * P), slice(h * HALF, (h + 1) * HALF)
                nc.tensor.matmul(p_s[k % 2][:, q], ka[s][:, cols], qa[s][:, q], start=True, stop=False)
                mm = nc.tensor.matmul(p_s[k % 2][:, q], kb[s][:, cols], qb[s][:, q], start=False, stop=True)
            mm.then_inc(scores, 1)

        def values(pe, r, s, k):
            u = r * SLOTS + s
            g = u * KT + k
            pe.wait_ge(probs_d, g + 1)
            if k == 0:
                pe.wait_ge(o_d, O0 + u - 1)
            Q = T // 4
            for col, lhs in ((0, v[s][:, k, :]), (1, c["ones"][:, 0:DH0])):
                for j in range(4):
                    mm = nc.tensor.matmul(p_o[s % 2][j * DH0:(j + 1) * DH0, col, :], lhs, probs[g_slot(k)][:, j * Q:(j + 1) * Q],
                                          start=(k == 0 and col == 0), stop=(k == KT - 1), skip_group_check=True,
                                          tile_position=(0, j * DH0))
            mm.then_inc(pv_d, 1)

        def g_slot(k):
            return k % PROBS

        def head(pe, r, s, last):
            for k in range(KT):
                if not last:
                    for n in range(sum(MAX_PLAN[:k]), sum(MAX_PLAN[:k + 1])):
                        max_half(pe, *after(r, s), n)
                    if k == KT - 2:
                        max_turn(pe, *after(r, s))
                if k + 1 < KT:
                    score(pe, r, s, k + 1)
                elif not last:
                    score(pe, *after(r, s), 0)
                values(pe, r, s, k)

        @block.tensor
        def _(pe):
            pe.sem_inc(pv_d, PV0)
            pe.wait_ge(ones_d, SLOTS)
            for n in range(2 * KT):
                max_half(pe, 0, 0, n)
            max_turn(pe, 0, 0)
            score(pe, 0, 0, 0)
            with pe.Fori(0, LAST) as r:
                for s in range(SLOTS):
                    head(pe, r, s, False)
            for s in range(SLOTS):
                head(pe, LAST, s, s == SLOTS - 1)

        @block.scalar
        def _(act):
            with act.Fori(0, UNITS // SLOTS) as r:
                for s in range(SLOTS):
                    for k in range(KT):
                        g = (r * SLOTS + s) * KT + k
                        act.wait_ge(scores, g + 1)
                        act.wait_ge(pv_d, PV0 + g - PROBS + 1)
                        nc.scalar.activation(probs[g_slot(k)][:, :], p_s[k % 2][:, :], ACT.Exp, scale=SCALE).then_inc(probs_d, 1)

        def maxima(dve, r, s):
            u = r * SLOTS + s
            for n in range(2 * KT):
                dve.wait_ge(max_scores, u * 2 * KT + n + 1)
                if n == 0:
                    dve.wait_ge(max_row, u)
                nc.vector.reduce_max(halfmax[:, n % 2, n // 2:n // 2 + 1], p_m[n % 2][:, :], AX.X).then_inc(max_read, 1)
            dve.wait_ge(max_read, (u + 1) * 2 * KT)
            nc.vector.tensor_tensor(rowmax[:, :], halfmax[:, 0, :], halfmax[:, 1, :], ALU.max).then_inc(max_row, 1)
            dve.wait_ge(max_T, u + 1)
            dve.wait_ge(max_in, u * 32)
            nc.vector.tensor_scalar(max_hi[:, :], p_m[0][0:KT, 0:P], -1.0, None, ALU.mult).then_inc(max_hi_d, 1)
            dve.wait_ge(max_hi_d, u + 1)
            nc.vector.scalar_tensor_tensor(out=max_lo[:, :], in0=p_m[0][0:KT, 0:P], scalar=-1.0,
                                           in1=max_hi[:, :], op0=ALU.mult, op1=ALU.subtract).then_inc(max_parts, 1)

        def normalise(dve, r, s):
            u = r * SLOTS + s
            dve.wait_ge(pv_d, PV0 + (u + 1) * KT)
            dve.wait_ge(o_d, O0 + u)
            nc.vector.reciprocal(inv[:, :], p_o[s % 2][:, 1, :]).then_inc(inv_d, 1)
            dve.wait_ge(inv_d, u + 1)
            dve.wait_ge(o_out[s % 2], (r * (SLOTS // 2) + s // 2) * 64)
            nc.vector.tensor_tensor(ot[s % 2][:, :], p_o[s % 2][:, 0, :], inv[:, :], ALU.mult).then_inc(o_d, 1)

        @block.vector
        def _(dve):
            dve.sem_inc(o_d, O0)
            maxima(dve, 0, 0)
            with dve.Fori(0, LAST) as r:
                for s in range(SLOTS):
                    maxima(dve, *after(r, s))
                    normalise(dve, r, s)
            for s in range(SLOTS):
                if s + 1 < SLOTS:
                    maxima(dve, LAST, s + 1)
                normalise(dve, LAST, s)


def block_table(nc, dve, c, count, experts, blocks, tabs, SLOT, done, n0):
    n = [n0]

    def step(ins):
        ins.then_inc(done, 1)
        n[0] += 1
        dve.wait_ge(done, n[0])

    R = NTOK // BT
    cmp, used, upto, zero = tabs["cmp"], tabs["used"], tabs["upto"], tabs["zero"]
    ge, past, first, live = tabs["ge"], tabs["past"], tabs["first"], tabs["live"]
    step(nc.vector.memset(zero[:, :], 0.0))
    step(nc.vector.tensor_scalar(cmp[:, 0:R], c["iota"][:, 0:R], float(BT), None, ALU.mult))
    step(nc.vector.tensor_tensor(ge[:, 0:experts * R].rearrange("p (e r) -> p e r", r=R),
                                 count.unsqueeze(2).broadcast_to([P, experts, R]),
                                 cmp[:, 0:R].unsqueeze(1).broadcast_to([P, experts, R]), ALU.is_gt))
    step(nc.vector.tensor_reduce(used[:, :], ge[:, 0:experts * R].rearrange("p (e r) -> p e r", r=R), AX.X, ALU.add))
    step(nc.vector.tensor_tensor_scan(upto[:, :], used[:, :], zero[:, :], 0.0, ALU.add, ALU.add))
    je = ge[:, 0:blocks * experts].rearrange("p (j e) -> p j e", e=experts)
    shape = [P, blocks, experts]
    step(nc.vector.tensor_tensor(je, c["iota"][:, 0:blocks].unsqueeze(2).broadcast_to(shape),
                                 upto[:, :].unsqueeze(1).broadcast_to(shape), ALU.is_ge))
    step(nc.vector.tensor_reduce(past[:, :], je, AX.X, ALU.add))
    step(nc.vector.tensor_tensor(je, je, used[:, :].unsqueeze(1).broadcast_to(shape), ALU.mult))
    step(nc.vector.tensor_reduce(first[:, :], je, AX.X, ALU.add))
    step(nc.vector.tensor_tensor(first[:, :], c["iota"][:, 0:blocks], first[:, :], ALU.subtract))
    step(nc.vector.tensor_scalar(first[:, :], first[:, :], float(BT), None, ALU.mult))
    step(nc.vector.tensor_scalar(live[:, :], past[:, :], float(REGION), None, ALU.mult))
    step(nc.vector.tensor_tensor(tabs["row"][:, :], first[:, :], live[:, :], ALU.add))
    step(nc.vector.tensor_scalar(tabs["expert"][:, :], past[:, :], float(experts - 1), None, ALU.min))
    step(nc.vector.tensor_scalar(cmp[:, 0:experts], c["iota"][:, 0:experts], float(REGION), None, ALU.mult))
    step(nc.vector.tensor_tensor(tabs["tail"][:, :], cmp[:, 0:experts], count, ALU.add))
    slotf, over, jump = tabs["slotf"], tabs["over"], tabs["jump"]
    step(nc.vector.tensor_tensor(upto[:, :], upto[:, :], used[:, :], ALU.subtract))
    step(nc.vector.scalar_tensor_tensor(out=upto[:, :], in0=upto[:, :], scalar=float(BT), in1=cmp[:, 0:experts],
                                        op0=ALU.mult, op1=ALU.subtract))
    step(nc.vector.tensor_tensor(jump[:, :], upto[:, 1:experts], upto[:, 0:experts - 1], ALU.subtract))
    step(nc.vector.tensor_copy(slotf[:, :], SLOT))
    shape = [P, slotf.shape[1], experts - 1]
    step(nc.vector.tensor_tensor(over[:, :, :], slotf[:, :].unsqueeze(2).broadcast_to(shape),
                                 cmp[:, 1:experts].unsqueeze(1).broadcast_to(shape), ALU.is_ge))
    step(nc.vector.tensor_tensor(over[:, :, :], over[:, :, :], jump[:, :].unsqueeze(1).broadcast_to(shape), ALU.mult))
    step(nc.vector.tensor_reduce(tabs["moved"][:, :], over[:, :, :], AX.X, ALU.add))
    step(nc.vector.tensor_tensor(slotf[:, :], slotf[:, :], tabs["moved"][:, :], ALU.add))
    step(nc.vector.tensor_copy(SLOT, slotf[:, :]))


TABLE_STEPS = 17


def tables(ctx, nc, name, choices, experts):
    blocks, slots = blocks_of(choices, experts), choices * TILES
    wide = {"cmp": 128, "used": experts, "upto": experts, "zero": experts, "past": blocks, "first": blocks,
            "ge": max(blocks, NTOK // BT) * experts, "live": blocks, "jump": experts - 1, "slotf": slots,
            "moved": slots}
    tabs = {n: ctx.enter_context(nc.sbuf_tensor(f"{name}_{n}", [P, w], F32)) for n, w in wide.items()}
    tabs["over"] = ctx.enter_context(nc.sbuf_tensor(f"{name}_over", [P, slots, experts - 1], F32))
    for n, w in (("row", blocks), ("expert", blocks), ("tail", experts)):
        tabs[n] = ctx.enter_context(nc.sbuf_tensor(f"{name}_{n}", [P, w], I32))
    return tabs


def zero_tails(nc, sp, xs, zeros, tabs, experts, surplus, out):
    for e in range(experts):
        row = sp.value_load(tabs["tail"][0:1, e:e + 1], min_val=0, max_val=experts * REGION - BT)
        sp.dma_start(xs[bass.ds(row, BT), :].rearrange("(t p) d -> p t d", p=P), zeros[:, :, :]).then_inc(out, 16)
    for n in range(surplus):
        rows = slice(experts * REGION + n * BT, experts * REGION + (n + 1) * BT)
        sp.dma_start(xs[rows, :].rearrange("(t p) d -> p t d", p=P), zeros[:, :, :]).then_inc(out, 16)
    sp.wait_ge(out, (experts + surplus) * 16)


def route2(nc, c, X, XN, GATE, SLOT, tabs, w, o0, xs):
    with ExitStack() as ctx:
        def sb(name, shape, dt=F32):
            return ctx.enter_context(nc.sbuf_tensor(f"r2_{name}", shape, dt))

        def sem(name):
            return ctx.enter_context(nc.semaphore(f"r2_{name}"))

        def ps(name, shape):
            return ctx.enter_context(nc.psum_tensor(f"r2_{name}", shape, F32))

        wo, wg = sb("wo", [P, 2, D]), sb("wg", [P, E0])
        oT = [sb(f"oT{i}", [P, 2, GT]) for i in range(2)]
        xn = [sb(f"xn{i}", [P, G, D]) for i in range(2)]
        slot = [sb(f"slot{i}", [P, G * 2], I32) for i in range(2)]
        stats, mv, rstd = sb("stats", [P, G, 6]), sb("mv", [P, G, 2]), sb("rstd", [P, G])
        xT = sb("xT", [P, GT])
        top, total = sb("top", [P, G]), sb("total", [P, G])
        prob = sb("prob", [P, G, E0])
        best, at = sb("best", [P, G, 8]), sb("at", [P, G, 8], U32)
        atf = sb("atf", [P, G, 2])
        hot, both = sb("hot", [P, G, 2, E0]), sb("both", [P, G, E0])
        seen, now = sb("seen", [P, E0]), sb("now", [P, E0])
        start = sb("start", [P, E0])
        place, placed = sb("place", [P, G, E0]), sb("placed", [P, G, 2, E0])
        zeros = sb("zeros", [P, BT // P, D])
        p_y, p_xT = ps("p_y", [P, G, D]), ps("p_xT", [P, GT])
        p_g, p_pos = ps("p_g", [P, 512]), ps("p_pos", [P, 512])
        gate_ps = p_g[:, 0:G * E0].rearrange("p (t e) -> p t e", e=E0)
        pos_ps = p_pos[:, 0:G * E0].rearrange("p (t e) -> p t e", e=E0)
        (w_in, y_d, x_d, stats_d, var_d, root_d, rstd_d, xn_d, pxT_d, xT_d, kept_d, gate_d, shift_d, exp_d,
         own, hot_done, hot_d, pos_d, slot_d, count_d, tabs_d, zeros_d, tails_out, passed) = (
            sem(n) for n in ("w_in", "y", "x", "stats", "var", "root", "rstd", "xn", "pxT", "xT", "kept", "gate",
                             "shift", "exp", "own", "hot_done", "hot", "pos", "slot", "count", "tabs", "zeros", "tails_out",
                             "passed"))
        oT_in = [sem(f"oT_in{i}") for i in range(2)]
        rows_out = [sem(f"rows_out{i}") for i in range(2)]
        OWN = 13
        block = ctx.enter_context(nc.Block())

        @block.sync
        def _(sp):
            for cc in range(2):
                sp.dma_start(wo[:, cc, :], w["WoT"][cc * P:(cc + 1) * P, :]).then_inc(w_in, 16)
            sp.dma_start(wg[:, :], w["gateT"]).then_inc(w_in, 16)
            with sp.Fori(0, B) as b:
                for i in range(2):
                    apart(sp, y_d, b * 2 + i + 1, passed)
                    for cc in range(2):
                        sp.dma_start(oT[i][:, cc, :], o0[bass.ds(b * H0 + cc * 4, 4), :, i * GT:(i + 1) * GT]
                                     .rearrange("h d t -> (h d) t")).then_inc(oT_in[i], 16)
            sp.wait_ge(zeros_d, 1)
            sp.wait_ge(tabs_d, 1 + TABLE_STEPS)
            zero_tails(nc, sp, xs, zeros, tabs, E0, surplus_of(2, E0), tails_out)

        @block.tensor
        def _(pe):
            pe.sem_inc(y_d, 2)
            pe.wait_ge(w_in, 48)
            with pe.Fori(0, B) as b:
                for i in range(2):
                    g = b * 2 + i
                    pe.wait_ge(oT_in[i], (b + 1) * 32)
                    pe.wait_ge(x_d, g)
                    for t in range(G):
                        for cc in range(2):
                            mm = nc.tensor.matmul(p_y[:, t, :], oT[i][:, cc, t * P:(t + 1) * P], wo[:, cc, :],
                                                  start=(cc == 0), stop=(cc == 1))
                    mm.then_inc(y_d, 1)
                    pe.wait_ge(xn_d, g + 1)
                    for t in range(G):
                        mm = nc.tensor.transpose(p_xT[:, t * P:(t + 1) * P], xn[i][:, t, :], c["ident"][:, :])
                    mm.then_inc(pxT_d, 1)
                    pe.wait_ge(xT_d, g + 1)
                    for t in range(G):
                        mm = nc.tensor.matmul(gate_ps[:, t, :], xT[:, t * P:(t + 1) * P], wg[:, :], start=True, stop=True)
                    mm.then_inc(gate_d, 1)
                    pe.wait_ge(hot_d, g + 1)
                    for t in range(G):
                        nc.tensor.matmul(pos_ps[:, t, :], c["stri"][:, :], both[:, t, :], start=True, stop=False)
                        for t2 in range(t):
                            nc.tensor.matmul(pos_ps[:, t, :], c["ones"][:, :], both[:, t2, :], start=False, stop=False)
                        mm = nc.tensor.matmul(pos_ps[:, t, :], c["ones"][:, :], seen[:, :], start=False, stop=True)
                    mm.then_inc(pos_d, 1)
            pe.wait_ge(own, GROUPS * OWN)
            nc.tensor.matmul(p_pos[:, 0:E0], c["ones"][:, :], seen[:, :], start=True, stop=True).then_inc(count_d, 1)

        @block.scalar
        def _(act):
            with act.Fori(0, B) as b:
                for i in range(2):
                    g = b * 2 + i
                    act.wait_ge(var_d, g + 1)
                    nc.scalar.activation(rstd[:, :], rstd[:, :], ACT.Sqrt).then_inc(root_d, 1)
                    act.wait_ge(pxT_d, g + 1)
                    act.wait_ge(gate_d, g)
                    nc.scalar.copy(xT[:, :], p_xT[:, :]).then_inc(xT_d, 1)
                    nc.scalar.copy(XN[:, bass.ds(g * GT, GT)].rearrange("p (t d) -> p t d", t=G), xn[i][:, :, :]).then_inc(kept_d, 1)
                    act.wait_ge(shift_d, g + 1)
                    nc.scalar.activation(prob[:, :, :], prob[:, :, :], ACT.Exp).then_inc(exp_d, 1)

        @block.vector
        def _(dve):
            nc.vector.tensor_scalar(start[:, :], c["iota"][:, 0:E0], float(REGION), None, ALU.mult).then_inc(zeros_d, 1)
            nc.vector.memset(zeros[:, :, :], 0.0).then_inc(zeros_d, 1)
            nc.vector.memset(seen[:, :], 0.0).then_inc(zeros_d, 1)
            dve.wait_ge(zeros_d, 3)
            with dve.Fori(0, B) as b:
                for i in range(2):
                    g = b * 2 + i
                    n = [0]

                    def step(ins):
                        n[0] += 1
                        ins.then_inc(own, 1)
                        dve.wait_ge(own, g * OWN + n[0])

                    Xg = X[:, bass.ds(g * GT, GT)].rearrange("p (t d) -> p t d", t=G)
                    dve.wait_ge(y_d, g + 3)
                    nc.vector.tensor_tensor(Xg, Xg, p_y[:, :, :], ALU.add).then_inc(x_d, 1)
                    dve.wait_ge(x_d, g + 1)
                    dve.wait_ge(rows_out[i], b * 2 * G * 16)
                    apart(dve, kept_d, g, passed)
                    layer_norm(nc, dve, passed, root_d, Xg, xn[i][:, :, :], stats, mv, rstd, stats_d, var_d, rstd_d, xn_d, g)
                    dve.wait_ge(gate_d, g + 1)
                    step(nc.vector.tensor_reduce(top[:, :], gate_ps, AX.X, ALU.max))
                    nc.vector.tensor_tensor(prob[:, :, :], gate_ps, top[:, :].unsqueeze(2).broadcast_to([P, G, E0]),
                                            ALU.subtract).then_inc(shift_d, 1)
                    dve.wait_ge(exp_d, g + 1)
                    step(nc.vector.tensor_reduce(total[:, :], prob[:, :, :], AX.X, ALU.add))
                    step(nc.vector.reciprocal(total[:, :], total[:, :]))
                    step(nc.vector.tensor_tensor(prob[:, :, :], prob[:, :, :], total[:, :].unsqueeze(2).broadcast_to([P, G, E0]), ALU.mult))
                    dve.sem_inc(passed, 1)
                    for t in range(G):
                        last = nc.vector.max(best[:, t, :], prob[:, t, :])
                    step(last)
                    dve.sem_inc(passed, 1)
                    for t in range(G):
                        last = nc.vector.max_index(at[:, t, :], best[:, t, :], prob[:, t, :])
                    step(last)
                    step(nc.vector.tensor_copy(atf[:, :, :], at[:, :, 0:2]))
                    step(nc.vector.tensor_tensor(hot[:, :, :, :], c["iota"][:, 0:E0].unsqueeze(1).unsqueeze(1).broadcast_to([P, G, 2, E0]),
                                                 atf[:, :, :].unsqueeze(3).broadcast_to([P, G, 2, E0]), ALU.is_equal))
                    nc.vector.tensor_tensor(both[:, :, :], hot[:, :, 0, :], hot[:, :, 1, :], ALU.add).then_inc(hot_d, 1)
                    step(nc.vector.tensor_tensor(total[:, :], best[:, :, 0], best[:, :, 1], ALU.add))
                    step(nc.vector.tensor_scalar(total[:, :], total[:, :], 1e-10, None, ALU.max))
                    step(nc.vector.reciprocal(total[:, :], total[:, :]))
                    step(nc.vector.tensor_tensor(GATE[:, bass.ds(g * G * 2, G * 2)].rearrange("p (t k) -> p t k", k=2), best[:, :, 0:2],
                                                 total[:, :].unsqueeze(2).broadcast_to([P, G, 2]), ALU.mult))
                    dve.wait_ge(hot_d, g + 1)
                    nc.vector.tensor_reduce(now[:, :], both[:, :, :].rearrange("p t e -> p e t"), AX.X, ALU.add).then_inc(hot_done, 1)
                    dve.wait_ge(pos_d, g + 1)
                    dve.wait_ge(hot_done, g * 4 + 1)
                    nc.vector.tensor_tensor(place[:, :, :], pos_ps, start[:, :].unsqueeze(1).broadcast_to([P, G, E0]), ALU.add).then_inc(hot_done, 1)
                    dve.wait_ge(hot_done, g * 4 + 2)
                    nc.vector.tensor_tensor(placed[:, :, :, :], hot[:, :, :, :], place[:, :, :].unsqueeze(2).broadcast_to([P, G, 2, E0]), ALU.mult).then_inc(hot_done, 1)
                    dve.wait_ge(hot_done, g * 4 + 3)
                    nc.vector.tensor_reduce(atf[:, :, :], placed[:, :, :, :], AX.X, ALU.add).then_inc(hot_done, 1)
                    dve.wait_ge(hot_done, g * 4 + 4)
                    nc.vector.tensor_copy(slot[i][:, :], atf[:, :, :].rearrange("p t k -> p (t k)")).then_inc(slot_d, 1)
                    nc.vector.tensor_copy(SLOT[:, bass.ds(g * G * 2, G * 2)], atf[:, :, :].rearrange("p t k -> p (t k)")).then_inc(slot_d, 1)
                    step(nc.vector.tensor_tensor(seen[:, :], seen[:, :], now[:, :], ALU.add))
                    assert n[0] == OWN
            dve.wait_ge(count_d, 1)
            nc.vector.tensor_copy(now[:, :], p_pos[:, 0:E0]).then_inc(tabs_d, 1)
            dve.wait_ge(tabs_d, 1)
            block_table(nc, dve, c, now[:, :], E0, blocks_of(2, E0), tabs, SLOT[:, :], tabs_d, 1)

        @block.gpsimd
        def _(pool):
            with pool.Fori(0, B) as b:
                for i in range(2):
                    g = b * 2 + i
                    apart(pool, slot_d, g * 2 + 1, passed)
                    for t in range(G):
                        for k in range(2):
                            pool.indirect_dma_start(xs[:, :], bass.IndirectOffsetOnAxis(ap=slot[i][:, t * 2 + k:t * 2 + k + 1], axis=0),
                                                    xn[i][:, t, :], None).then_inc(rows_out[i], 16)
            for i in range(2):
                pool.wait_ge(rows_out[i], B * 2 * G * 16)


def experts(nc, c, name, E, F, act_fn, tabs, blocks, surplus, w, xs, ys):
    with ExitStack() as ctx:
        def sb(n, shape, dt=F32):
            return ctx.enter_context(nc.sbuf_tensor(f"{name}_{n}", shape, dt))

        def sem(n):
            return ctx.enter_context(nc.semaphore(f"{name}_{n}"))

        def ps(n, shape):
            return ctx.enter_context(nc.psum_tensor(f"{name}_{n}", shape, F32))

        NF, NT = F // P, BT // P
        w1 = [sb(f"w1_{i}", [P, F]) for i in range(2)]
        b1 = [sb(f"b1_{i}", [P, NF]) for i in range(2)]
        w2 = [sb(f"w2_{i}", [P, NF, D]) for i in range(2)]
        b2 = [sb(f"b2_{i}", [P, D]) for i in range(2)]
        xb = [sb(f"xb{i}", [P, NT, D]) for i in range(2)]
        xT = [sb(f"xT{i}", [P, BT]) for i in range(2)]
        h = [sb(f"h{i}", [P, NF, BT]) for i in range(2)]
        y = [sb(f"y{i}", [P, NT, D]) for i in range(2)]
        p_xT = [ps(f"p_xT{i}", [P, 512]) for i in range(2)]
        p_h = [ps(f"p_h{i}", [P, max(NF, 2), BT]) for i in range(2)]
        p_y = [ps(f"p_y{i}", [P, 512]) for i in range(2)]
        rows_in = [sem(f"rows_in{i}") for i in range(2)]
        weights_in = [sem(f"weights_in{i}") for i in range(2)]
        y_out = [sem(f"y_out{i}") for i in range(2)]
        pxT_d, xT_d, ph_d, h_d, py_d, y_d, passed = (sem(n) for n in ("pxT", "xT", "ph", "h", "py", "y", "passed"))
        PY0 = Y0 = 2
        block = ctx.enter_context(nc.Block())

        def turn(pe, j, i, q):
            pe.wait_ge(rows_in[i], (q + 1) * 16)
            for t in range(NT):
                mm = nc.tensor.transpose(p_xT[i][:, t * P:(t + 1) * P], xb[i][:, t, :], c["ident"][:, :])
            mm.then_inc(pxT_d, 1)

        def hidden(pe, j, i, q):
            pe.wait_ge(weights_in[i], (q + 1) * 64)
            pe.wait_ge(xT_d, j + 1)
            for f in range(NF):
                mm = nc.tensor.matmul(p_h[i][:, f, :], w1[i][:, f * P:(f + 1) * P], xT[i][:, :], start=True, stop=True)
            mm.then_inc(ph_d, 1)

        def outputs(pe, j, i, q):
            pe.wait_ge(h_d, j + 1)
            pe.wait_ge(y_d, Y0 + j - 1)
            for t in range(NT):
                for f in range(NF):
                    mm = nc.tensor.matmul(p_y[i][:, t * P:(t + 1) * P], h[i][:, f, t * P:(t + 1) * P], w2[i][:, f, :],
                                          start=(f == 0), stop=(f == NF - 1))
            mm.then_inc(py_d, 1)

        def copy_turned(dve, j, i, q):
            dve.wait_ge(pxT_d, j + 1)
            if not (isinstance(j, int) and j < 2):
                dve.wait_ge(ph_d, j - 1)
            nc.vector.tensor_copy(xT[i][:, :], p_xT[i][:, 0:BT]).then_inc(xT_d, 1)

        def add_bias(dve, j, i, q):
            dve.wait_ge(py_d, PY0 + j + 1)
            dve.wait_ge(y_out[i], q * 16)
            nc.vector.tensor_tensor(y[i][:, :, :], p_y[i][:, 0:BT].rearrange("p (t d) -> p t d", t=NT),
                                    b2[i][:, :].unsqueeze(1).broadcast_to([P, NT, D]), ALU.add).then_inc(y_d, 1)

        def pipeline(eng, ahead, mid, behind):
            ahead(eng, 0, 0, 0)
            mid(eng, 0, 0, 0)
            ahead(eng, 1, 1, 0)
            with eng.Fori(0, (blocks - 2) // 2) as r:
                mid(eng, r * 2 + 1, 1, r)
                ahead(eng, r * 2 + 2, 0, r + 1)
                behind(eng, r * 2, 0, r)
                mid(eng, r * 2 + 2, 0, r + 1)
                ahead(eng, r * 2 + 3, 1, r + 1)
                behind(eng, r * 2 + 1, 1, r)
            q = blocks // 2 - 1
            mid(eng, blocks - 1, 1, q)
            behind(eng, blocks - 2, 0, q)
            behind(eng, blocks - 1, 1, q)

        def load_rows(sp, j, i):
            row = sp.value_load(tabs["row"][0:1, bass.ds(j, 1)], min_val=0, max_val=E * REGION + surplus * BT - BT)
            if not (isinstance(j, int) and j < 2):
                apart(sp, pxT_d, j - 1, passed)
            sp.dma_start(xb[i][:, :, :], xs[bass.ds(row, BT), :].rearrange("(t p) d -> p t d", p=P)).then_inc(rows_in[i], 16)

        def load_weights(sp, j, i):
            e = sp.value_load(tabs["expert"][0:1, bass.ds(j, 1)], min_val=0, max_val=E - 1)
            apart(sp, py_d, PY0 + j - 1, passed)
            apart(sp, y_d, Y0 + j - 1, passed)
            sp.dma_start(w1[i][:, :], w["W1"][bass.ds(e, 1)].rearrange("o d f -> (o d) f")).then_inc(weights_in[i], 16)
            sp.dma_start(b1[i][:, :], w["b1"][bass.ds(e, 1)].rearrange("o p f -> (o p) f")).then_inc(weights_in[i], 16)
            sp.dma_start(w2[i][:, :, :], w["W2"][bass.ds(e, 1)].rearrange("o (f p) d -> p (o f) d", p=P)).then_inc(weights_in[i], 16)
            sp.dma_start(b2[i][:, :], w["b2"][bass.ds(e, 1), :].broadcast_to([P, D])).then_inc(weights_in[i], 16)

        @block.sync
        def _(sp):
            load_rows(sp, 0, 0)
            load_rows(sp, 1, 1)
            with sp.Fori(0, blocks // 2 - 1) as r:
                load_weights(sp, r * 2, 0)
                load_rows(sp, r * 2 + 2, 0)
                load_weights(sp, r * 2 + 1, 1)
                load_rows(sp, r * 2 + 3, 1)
            load_weights(sp, blocks - 2, 0)
            load_weights(sp, blocks - 1, 1)

        @block.tensor
        def _(pe):
            pe.sem_inc(py_d, PY0)
            pipeline(pe, turn, hidden, outputs)

        @block.scalar
        def _(act):
            with act.Fori(0, blocks // 2) as r:
                for i in range(2):
                    j = r * 2 + i
                    act.wait_ge(ph_d, j + 1)
                    act.wait_ge(py_d, PY0 + j - 1)
                    for f in range(NF):
                        last = nc.scalar.activation(h[i][:, f, :], p_h[i][:, f, :], act_fn, bias=b1[i][:, f:f + 1])
                    last.then_inc(h_d, 1)

        @block.vector
        def _(dve):
            dve.sem_inc(y_d, Y0)
            pipeline(dve, copy_turned, lambda *a: None, add_bias)

        @block.gpsimd
        def _(pool):
            with pool.Fori(0, blocks // 2) as r:
                for i in range(2):
                    j = r * 2 + i
                    apart(pool, y_d, Y0 + j + 1, passed)
                    pool.dma_start(ys[bass.ds(j * BT, BT), :].rearrange("(t p) d -> p t d", p=P), y[i][:, :, :]).then_inc(y_out[i], 16)
            for i in range(2):
                pool.wait_ge(y_out[i], blocks // 2 * 16)


def linear(nc, c, X, XN, GATE, SLOT, BESTP, HOT, w, ys):
    with ExitStack() as ctx:
        def sb(name, shape, dt=F32):
            return ctx.enter_context(nc.sbuf_tensor(f"ln_{name}", shape, dt))

        def sem(name):
            return ctx.enter_context(nc.semaphore(f"ln_{name}"))

        def ps(name, shape):
            return ctx.enter_context(nc.psum_tensor(f"ln_{name}", shape, F32))

        wqkv, wo, wr = sb("wqkv", [P, 3 * D]), sb("wo", [P, D]), sb("wr", [P, E1])
        slot = [sb(f"slot{i}", [P, G * 2], I32) for i in range(2)]
        rows = [sb(f"rows{i}", [P, G * 2, D]) for i in range(2)]
        moe = sb("moe", [P, G, D])
        stats, mv, rstd = sb("stats", [P, G, 6]), sb("mv", [P, G, 2]), sb("rstd", [P, G])
        xn, xT = sb("xn", [P, G, D]), sb("xT", [P, GT])
        qk = [sb(f"qk{i}", [P, 2 * D]) for i in range(2)]
        v1 = [sb(f"v1_{i}", [P, D + 1]) for i in range(2)]
        qT = [sb(f"qT{i}", [P, P]) for i in range(2)]
        kv = [sb(f"kv{i}", [P, KV1 + D]) for i in range(2)]
        state = sb("state", [P, D + H1])
        own_head = sb("own_head", [P, D + H1])
        prod = sb("prod", [P, KV1 + D])
        num, den = sb("num", [P, D]), sb("den", [P, H1])
        o, oT = sb("o", [P, G, D]), sb("oT", [P, GT])
        top, total = sb("top", [P, G]), sb("total", [P, G])
        prob, best, at = sb("prob", [P, G, E1]), sb("best", [P, G, 8]), sb("at", [P, G, 8], U32)
        atf = sb("atf", [P, G])
        p_T, p_qkv = ps("p_T", [P, 512]), ps("p_qkv", [P, 512])
        p_cum = ps("p_cum", [P, 3, 512])
        p_prev, p_st, p_y = ps("p_prev", [P, 512]), ps("p_st", [P, 512]), ps("p_y", [P, G, D])
        names = ("w_in", "ones", "mask", "x", "stats", "var", "root", "rstd", "xn", "pxT", "xT", "qkv", "qk",
                 "v", "pqT", "qT", "kc", "kv", "st", "state", "cum", "prev", "prod", "o", "own", "poT", "oT",
                 "y", "kept", "logits", "shift", "exp", "passed", "moe", "chain", "slots", "router")
        S = {n: sem(n) for n in names}
        rows_in = [sem(f"rows_in{i}") for i in range(2)]
        OWN, CHAIN = 8, 4
        block = ctx.enter_context(nc.Block())

        @block.sync
        def _(sp):
            for dst, src in ((wqkv, w["WqkvT"]), (wo, w["Wo1T"]), (wr, w["routerT"])):
                sp.dma_start(dst[:, :], src).then_inc(S["w_in"], 16)
            sp.wait_ge(S["w_in"], 48)

        @block.gpsimd
        def _(pool):
            def masked(out, keys, reps):
                nc.gpsimd.memset(out, 1.0).then_inc(S["mask"], 1)
                pool.wait_ge(S["mask"], keys + 1)
                nc.gpsimd.affine_select(out=out, in_=out, compare_op=ALU.is_ge, fill=0.0, base=0,
                                        pattern=[[-DH1, H1], [0, reps]], channel_multiplier=1).then_inc(S["mask"], 1)
                pool.wait_ge(S["mask"], keys + 2)
                nc.gpsimd.affine_select(out=out, in_=out, compare_op=ALU.is_ge, fill=0.0, base=DH1 - 1,
                                        pattern=[[DH1, H1], [0, reps]], channel_multiplier=-1).then_inc(S["mask"], 1)

            masked(own_head[:, 0:D].rearrange("p (h m) -> p h m", h=H1), 0, DH1)
            masked(own_head[:, D:D + H1].rearrange("p (h m) -> p h m", h=H1), 3, 1)
            for i in range(2):
                nc.gpsimd.memset(v1[i][:, D:D + 1], 1.0).then_inc(S["ones"], 1)

            def gather(b, i):
                g = b * 2 + i
                apart(pool, S["moe"], 1 + (g - 1), S["passed"])
                nc.gpsimd.tensor_copy(slot[i][:, :], SLOT[:, bass.ds(g * G * 2, G * 2)]).then_inc(S["slots"], 1)
                apart(pool, S["slots"], g + 1, S["passed"])
                for n in range(G * 2):
                    pool.indirect_dma_start(rows[i][:, n, :], None, ys[:, :],
                                            bass.IndirectOffsetOnAxis(ap=slot[i][:, n:n + 1], axis=0)).then_inc(rows_in[i], 16)

            def outer(g, t):
                n = g * G + t
                pool.wait_ge(S["v"], n + 1)
                pool.wait_ge(S["cum"], 2 + n - 1)
                shape = [P, H1, DH1, DH1]
                k = qk[t % 2][:, D:2 * D].rearrange("p (h d) -> p h d", h=H1)
                v = v1[t % 2][:, 0:D].rearrange("p (h m) -> p h m", h=H1)
                nc.gpsimd.tensor_tensor(kv[t % 2][:, 0:KV1].rearrange("p (h d m) -> p h d m", h=H1, d=DH1),
                                        k.unsqueeze(3).broadcast_to(shape), v.unsqueeze(2).broadcast_to(shape),
                                        ALU.mult).then_inc(S["kv"], 1)

            gather(0, 0)
            with pool.Fori(0, B - 1) as b:
                gather(b, 1)
                for t in range(G):
                    outer(b * 2, t)
                gather(b + 1, 0)
                for t in range(G):
                    outer(b * 2 + 1, t)
            gather(B - 1, 1)
            for i in range(2):
                for t in range(G):
                    outer(B * 2 - 2 + i, t)

        @block.tensor
        def _(pe):
            pe.sem_inc(S["cum"], 2)
            pe.wait_ge(S["w_in"], 48)
            pe.wait_ge(S["ones"], 2)
            with pe.Fori(0, B) as b:
                for i in range(2):
                    g = b * 2 + i

                    def turned(src, done):
                        for t in range(G):
                            mm = nc.tensor.transpose(p_T[:, t * P:(t + 1) * P], src[:, t, :], c["ident"][:, :])
                        mm.then_inc(done, 1)

                    def qkv(t):
                        nc.tensor.matmul(p_qkv[:, 0:3 * D], xT[:, t * P:(t + 1) * P], wqkv[:, :], start=True,
                                         stop=True).then_inc(S["qkv"], 1)

                    pe.wait_ge(S["xn"], 2 * g + 1)
                    turned(xn, S["pxT"])
                    pe.wait_ge(S["xT"], 2 * g + 1)
                    pe.wait_ge(S["v"], g * G)
                    qkv(0)
                    for t in range(G):
                        n, tb, s = g * G + t, i * G + t, t % 2
                        pe.wait_ge(S["v"], n + 1)
                        nc.tensor.transpose(p_T[:, 0:P], qk[s][:, 0:D], c["ident"][:, :]).then_inc(S["pqT"], 1)
                        pe.wait_ge(S["state"], 2 * n)
                        nc.tensor.matmul(p_st[:, 0:D + 1], qk[s][:, D:2 * D], v1[s][:, :], start=(tb == 0),
                                         stop=(tb == KT - 1), skip_group_check=True).then_inc(S["st"], 1)
                        if t + 1 < G:
                            qkv(t + 1)
                        if tb > 0:
                            pe.wait_ge(S["qT"], n + 1)
                            pe.wait_ge(S["o"], n)
                            nc.tensor.matmul(p_prev[:, 0:D + H1], qT[s][:, :], state[:, :], start=True,
                                             stop=True).then_inc(S["prev"], 1)
                        pe.wait_ge(S["kv"], n + 1)
                        pe.wait_ge(S["kc"], n + 1)
                        pe.wait_ge(S["prod"], 2 * n)
                        for a in range(3):
                            z = min(512, KV1 + D - a * 512)
                            mm = nc.tensor.matmul(p_cum[:, a, 0:z], c["tri"][:, :], kv[s][:, a * 512:a * 512 + z],
                                                  start=True, stop=True)
                        mm.then_inc(S["cum"], 1)
                        pe.wait_ge(S["qT"], n + 1)
                    pe.wait_ge(S["o"], g * G + G)
                    turned(o, S["poT"])
                    pe.wait_ge(S["oT"], g + 1)
                    for t in range(G):
                        mm = nc.tensor.matmul(p_y[:, t, :], oT[:, t * P:(t + 1) * P], wo[:, :], start=True, stop=True)
                    mm.then_inc(S["y"], 1)
                    pe.wait_ge(S["xn"], 2 * g + 2)
                    turned(xn, S["pxT"])
                    pe.wait_ge(S["xT"], 2 * g + 2)
                    for t in range(G):
                        mm = nc.tensor.matmul(p_y[:, 0, t * E1:(t + 1) * E1], xT[:, t * P:(t + 1) * P], wr[:, :], start=True, stop=True)
                    mm.then_inc(S["logits"], 1)

        @block.scalar
        def _(act):
            with act.Fori(0, B) as b:
                for i in range(2):
                    g = b * 2 + i

                    def root_and_turn(m):
                        act.wait_ge(S["var"], m + 1)
                        nc.scalar.activation(rstd[:, :], rstd[:, :], ACT.Sqrt).then_inc(S["root"], 1)
                        act.wait_ge(S["pxT"], m + 1)
                        act.wait_ge(S["logits"], g)
                        nc.scalar.copy(xT[:, :], p_T[:, :]).then_inc(S["xT"], 1)

                    root_and_turn(2 * g)
                    for t in range(G):
                        n, s = g * G + t, t % 2
                        act.wait_ge(S["v"], n + 1)
                        act.wait_ge(S["cum"], 2 + n - 1)
                        nc.scalar.copy(kv[s][:, KV1:KV1 + D], qk[s][:, D:2 * D]).then_inc(S["kc"], 1)
                        act.wait_ge(S["pqT"], n + 1)
                        nc.scalar.copy(qT[s][:, :], p_T[:, 0:P]).then_inc(S["qT"], 1)
                    act.wait_ge(S["poT"], g + 1)
                    nc.scalar.copy(oT[:, :], p_T[:, :]).then_inc(S["oT"], 1)
                    root_and_turn(2 * g + 1)
                    nc.scalar.copy(XN[:, bass.ds(g * GT, GT)].rearrange("p (t d) -> p t d", t=G), xn[:, :, :]).then_inc(S["kept"], 1)
                    act.wait_ge(S["shift"], g + 1)
                    nc.scalar.activation(prob[:, :, :], prob[:, :, :], ACT.Exp).then_inc(S["exp"], 1)

        @block.vector
        def _(dve):
            dve.sem_inc(S["moe"], 1)
            dve.wait_ge(S["mask"], 6)
            with dve.Fori(0, B) as b:
                for i in range(2):
                    g = b * 2 + i
                    n_own = [0]
                    n_chain = [0]

                    def step(ins):
                        n_own[0] += 1
                        ins.then_inc(S["own"], 1)
                        dve.wait_ge(S["own"], g * OWN + n_own[0])

                    def link(ins):
                        n_chain[0] += 1
                        ins.then_inc(S["chain"], 1)
                        dve.wait_ge(S["chain"], g * CHAIN * G + n_chain[0])

                    Xg = X[:, bass.ds(g * GT, GT)].rearrange("p (t d) -> p t d", t=G)
                    XNg = XN[:, bass.ds(g * GT, GT)].rearrange("p (t d) -> p t d", t=G)
                    dve.wait_ge(rows_in[i], (b + 1) * G * 2 * 16)
                    step(nc.vector.tensor_tensor(rows[i][:, :, :], rows[i][:, :, :],
                                                 GATE[:, bass.ds(g * G * 2, G * 2)].unsqueeze(2).broadcast_to([P, G * 2, D]), ALU.mult))
                    two = rows[i][:, :, :].rearrange("p (t k) d -> p t k d", k=2)
                    nc.vector.tensor_tensor(moe[:, :, :], two[:, :, 0, :], two[:, :, 1, :], ALU.add).then_inc(S["moe"], 1)
                    dve.wait_ge(S["moe"], 1 + g + 1)
                    step(nc.vector.tensor_tensor(moe[:, :, :], moe[:, :, :], XNg, ALU.add))
                    step(nc.vector.tensor_scalar(moe[:, :, :], moe[:, :, :], 100.0, -100.0, ALU.min, ALU.max))
                    nc.vector.tensor_tensor(Xg, Xg, moe[:, :, :], ALU.add).then_inc(S["x"], 1)
                    apart(dve, S["x"], 2 * g + 1, S["passed"])
                    apart(dve, S["kept"], g, S["passed"])
                    layer_norm(nc, dve, S["passed"], S["root"], Xg, xn[:, :, :], stats, mv, rstd, S["stats"], S["var"],
                               S["rstd"], S["xn"], 2 * g)

                    def features(t):
                        n, s = g * G + t, t % 2
                        dve.wait_ge(S["qkv"], n + 1)
                        dve.wait_ge(S["cum"], 2 + n - 1)
                        nc.vector.tensor_scalar(qk[s][:, :], p_qkv[:, 0:2 * D], 0.0, FEAT_EPS, ALU.max, ALU.add).then_inc(S["qk"], 1)
                        nc.vector.tensor_copy(v1[s][:, 0:D], p_qkv[:, 2 * D:3 * D]).then_inc(S["v"], 1)

                    features(0)
                    for t in range(G):
                        n, tb, s = g * G + t, i * G + t, t % 2
                        if t + 1 < G:
                            features(t + 1)
                        dve.wait_ge(S["st"], n + 1)
                        dve.wait_ge(S["prev"], b * (KT - 1) + tb)
                        nc.vector.tensor_tensor(state[:, 0:D], p_st[:, 0:D], own_head[:, 0:D], ALU.mult).then_inc(S["state"], 1)
                        nc.vector.tensor_scalar(state[:, D:D + H1], own_head[:, D:D + H1], p_st[:, D:D + 1], None, ALU.mult).then_inc(S["state"], 1)
                        q = qk[s][:, 0:D].rearrange("p (h d) -> p h d", h=H1)
                        dve.wait_ge(S["cum"], 2 + n + 1)
                        dve.wait_ge(S["o"], n)
                        for a in range(2):
                            hs = slice(a * H1 // 2, (a + 1) * H1 // 2)
                            last = nc.vector.tensor_tensor(prod[:, a * 512:(a + 1) * 512].rearrange("p (h d m) -> p h d m", d=DH1, m=DH1),
                                                           p_cum[:, a, :].rearrange("p (h d m) -> p h d m", d=DH1, m=DH1),
                                                           q[:, hs, :].unsqueeze(3).broadcast_to([P, H1 // 2, DH1, DH1]), ALU.mult)
                        last.then_inc(S["prod"], 1)
                        nc.vector.tensor_tensor(prod[:, KV1:KV1 + D], p_cum[:, 2, 0:D], qk[s][:, 0:D], ALU.mult).then_inc(S["prod"], 1)
                        dve.wait_ge(S["prod"], 2 * n + 2)
                        nc.vector.tensor_reduce(num[:, :].rearrange("p (h m) -> p h m", h=H1),
                                                prod[:, 0:KV1].rearrange("p (h d m) -> p h m d", h=H1, d=DH1), AX.X, ALU.add)
                        link(nc.vector.tensor_reduce(den[:, :], prod[:, KV1:KV1 + D].rearrange("p (h d) -> p h d", h=H1), AX.X, ALU.add))
                        if tb > 0:
                            dve.wait_ge(S["prev"], b * (KT - 1) + tb)
                            nc.vector.tensor_tensor(num[:, :], num[:, :], p_prev[:, 0:D], ALU.add)
                            link(nc.vector.tensor_tensor(den[:, :], den[:, :], p_prev[:, D:D + H1], ALU.add))
                        else:
                            dve.sem_inc(S["chain"], 1)
                            n_chain[0] += 1
                        link(nc.vector.tensor_scalar(den[:, :], den[:, :], FEAT_EPS, None, ALU.add))
                        link(nc.vector.reciprocal(den[:, :], den[:, :]))
                        if t == 0:
                            dve.wait_ge(S["poT"], g)
                        nc.vector.tensor_tensor(o[:, t, :].rearrange("p (h m) -> p h m", h=H1), num[:, :].rearrange("p (h m) -> p h m", h=H1),
                                                den[:, :].unsqueeze(2).broadcast_to([P, H1, DH1]), ALU.mult).then_inc(S["o"], 1)
                    dve.wait_ge(S["y"], g + 1)
                    nc.vector.tensor_tensor(Xg, Xg, p_y[:, :, :], ALU.add).then_inc(S["x"], 1)
                    apart(dve, S["x"], 2 * g + 2, S["passed"])
                    layer_norm(nc, dve, S["passed"], S["root"], Xg, xn[:, :, :], stats, mv, rstd, S["stats"], S["var"],
                               S["rstd"], S["xn"], 2 * g + 1)
                    logits = p_y[:, 0, 0:G * E1].rearrange("p (t e) -> p t e", e=E1)
                    wide = [P, G, E1]
                    dve.wait_ge(S["logits"], g + 1)
                    step(nc.vector.tensor_reduce(top[:, :], logits, AX.X, ALU.max))
                    nc.vector.tensor_tensor(prob[:, :, :], logits, top[:, :].unsqueeze(2).broadcast_to(wide), ALU.subtract).then_inc(S["shift"], 1)
                    dve.wait_ge(S["exp"], g + 1)
                    step(nc.vector.tensor_reduce(total[:, :], prob[:, :, :], AX.X, ALU.add))
                    step(nc.vector.reciprocal(total[:, :], total[:, :]))
                    nc.vector.tensor_tensor(prob[:, :, :], prob[:, :, :], total[:, :].unsqueeze(2).broadcast_to(wide), ALU.mult).then_inc(S["router"], 1)
                    apart(dve, S["router"], 4 * g + 1, S["passed"])
                    for t in range(G):
                        last = nc.vector.max(best[:, t, :], prob[:, t, :])
                    last.then_inc(S["router"], 1)
                    apart(dve, S["router"], 4 * g + 2, S["passed"])
                    for t in range(G):
                        last = nc.vector.max_index(at[:, t, :], best[:, t, :], prob[:, t, :])
                    last.then_inc(S["router"], 1)
                    dve.wait_ge(S["router"], 4 * g + 3)
                    step(nc.vector.tensor_copy(atf[:, :], at[:, :, 0]))
                    nc.vector.tensor_tensor(HOT[:, :, bass.ds(g * G, G)].rearrange("p e t -> p t e"),
                                            c["iota"][:, 0:E1].unsqueeze(1).broadcast_to(wide),
                                            atf[:, :].unsqueeze(2).broadcast_to(wide), ALU.is_equal).then_inc(S["router"], 1)
                    step(nc.vector.tensor_copy(BESTP[:, bass.ds(g * G, G)], best[:, :, 0]))
                    assert n_own[0] == OWN and n_chain[0] == CHAIN * G, (n_own, n_chain)


BITS = 27


def capacity(nc, c, XN, BESTP, HOT, SLOT, tabs, xs):
    with ExitStack() as ctx:
        def sb(name, shape, dt=F32):
            return ctx.enter_context(nc.sbuf_tensor(f"cp_{name}", shape, dt))

        def sem(name):
            return ctx.enter_context(nc.semaphore(f"cp_{name}"))

        ET = [P, E1, TILES]
        p_of, cmp, equal, keep, place, tiles_before = (sb(n, ET) for n in ("p_of", "cmp", "equal", "keep", "place", "before"))
        count, level, trial, bit, rise, room, start, zero = (sb(n, [P, E1]) for n in
                                                             ("count", "level", "trial", "bit", "rise", "room", "start", "zero"))
        none = sb("none", [P, TILES])
        slotf, scatter_slot = sb("slotf", [P, TILES]), sb("scatter_slot", [P, TILES], I32)
        xn = [sb(f"xn{i}", [P, G, D]) for i in range(2)]
        slot = [sb(f"slot{i}", [P, G], I32) for i in range(2)]
        zeros = sb("zeros", [P, BT // P, D])
        p_count = ctx.enter_context(nc.psum_tensor("cp_p_count", [P, 512], F32))
        p_rank = ctx.enter_context(nc.psum_tensor("cp_p_rank", [P, E1, TILES], F32))
        p_tiles = ctx.enter_context(nc.psum_tensor("cp_p_tiles", [P, E1, TILES], F32))
        step_d, counted, total_d, loop_d, ranks, slots_d, copied, tails_out, passed = (
            sem(n) for n in ("step", "counted", "total", "loop", "ranks", "slots", "copied", "tails_out", "passed"))
        rows_out = [sem(f"rows_out{i}") for i in range(2)]
        block = ctx.enter_context(nc.Block())
        wide = lambda a: a.unsqueeze(2).broadcast_to(ET)

        @block.tensor
        def _(pe):
            with pe.Fori(0, BITS) as k:
                pe.wait_ge(counted, k + 1)
                nc.tensor.matmul(p_count[:, 0:E1], c["ones"][:, :], count[:, :], start=True, stop=True).then_inc(total_d, 1)
            pe.wait_ge(counted, BITS + 1)
            nc.tensor.matmul(p_count[:, 0:E1], c["ones"][:, :], count[:, :], start=True, stop=True).then_inc(total_d, 1)
            for n, src in enumerate((equal, keep)):
                pe.wait_ge(counted, BITS + 2 + n)
                nc.tensor.matmul(p_rank[:, :, :], c["stri"][:, :], src[:, :, :], start=True, stop=True)
                nc.tensor.matmul(p_tiles[:, :, :], c["ones"][:, :], src[:, :, :], start=True, stop=True).then_inc(ranks, 1)

        @block.vector
        def _(dve):
            n = [0]

            def step(ins):
                n[0] += 1
                ins.then_inc(step_d, 1)
                dve.wait_ge(step_d, n[0])

            step(nc.vector.memset(zeros[:, :, :], 0.0))
            step(nc.vector.memset(zero[:, :], 0.0))
            step(nc.vector.memset(none[:, :], 0.0))
            step(nc.vector.tensor_scalar(start[:, :], c["iota"][:, 0:E1], float(REGION), None, ALU.mult))
            step(nc.vector.tensor_tensor(p_of[:, :, :], HOT[:, :, :], BESTP[:, :].unsqueeze(1).broadcast_to(ET), ALU.mult))
            step(nc.vector.tensor_tensor(p_of[:, :, :], p_of[:, :, :], HOT[:, :, :], ALU.add))
            step(nc.vector.tensor_scalar(p_of[:, :, :], p_of[:, :, :], -1.0, None, ALU.add))
            step(nc.vector.memset(level[:, :], 0.0))
            step(nc.vector.memset(trial[:, :], 0.5))
            step(nc.vector.memset(bit[:, :], 0.5))
            with dve.Fori(0, BITS) as k:
                nc.vector.tensor_tensor(cmp[:, :, :], p_of[:, :, :], wide(trial[:, :]), ALU.is_ge).then_inc(loop_d, 1)
                dve.wait_ge(loop_d, k * 5 + 1)
                nc.vector.tensor_reduce(count[:, :], cmp[:, :, :], AX.X, ALU.add).then_inc(counted, 1)
                dve.wait_ge(total_d, k + 1)
                nc.vector.tensor_scalar(rise[:, :], p_count[:, 0:E1], float(CAP1), None, ALU.is_ge).then_inc(loop_d, 1)
                dve.wait_ge(loop_d, k * 5 + 2)
                nc.vector.tensor_tensor(rise[:, :], rise[:, :], bit[:, :], ALU.mult).then_inc(loop_d, 1)
                dve.wait_ge(loop_d, k * 5 + 3)
                nc.vector.tensor_tensor(level[:, :], level[:, :], rise[:, :], ALU.add)
                nc.vector.tensor_scalar(bit[:, :], bit[:, :], 0.5, None, ALU.mult).then_inc(loop_d, 1)
                dve.wait_ge(loop_d, k * 5 + 4)
                nc.vector.tensor_tensor(trial[:, :], level[:, :], bit[:, :], ALU.add).then_inc(loop_d, 1)
                dve.wait_ge(loop_d, k * 5 + 5)
            step(nc.vector.tensor_tensor(keep[:, :, :], p_of[:, :, :], wide(level[:, :]), ALU.is_gt))
            nc.vector.tensor_reduce(count[:, :], keep[:, :, :], AX.X, ALU.add).then_inc(counted, 1)
            dve.wait_ge(total_d, BITS + 1)
            step(nc.vector.tensor_scalar(room[:, :], p_count[:, 0:E1], -1.0, float(CAP1), ALU.mult, ALU.add))
            nc.vector.tensor_tensor(equal[:, :, :], p_of[:, :, :], wide(level[:, :]), ALU.is_equal).then_inc(counted, 1)

            def rank(k):
                dve.wait_ge(ranks, k)
                for e in range(E1):
                    last = nc.vector.tensor_tensor_scan(tiles_before[:, e, :], p_tiles[:, e, :], none[:, :], 0.0, ALU.add, ALU.add)
                step(last)
                step(nc.vector.tensor_copy(count[:, :], tiles_before[:, :, TILES - 1]))
                step(nc.vector.tensor_tensor(tiles_before[:, :, :], tiles_before[:, :, :], p_tiles[:, :, :], ALU.subtract))
                step(nc.vector.tensor_tensor(place[:, :, :], tiles_before[:, :, :], p_rank[:, :, :], ALU.add))

            rank(1)
            step(nc.vector.tensor_tensor(cmp[:, :, :], place[:, :, :], wide(room[:, :]), ALU.is_lt))
            step(nc.vector.tensor_tensor(cmp[:, :, :], cmp[:, :, :], equal[:, :, :], ALU.mult))
            step(nc.vector.tensor_tensor(keep[:, :, :], keep[:, :, :], cmp[:, :, :], ALU.add))
            step(nc.vector.tensor_reduce(slotf[:, :], keep[:, 1:E1, :].rearrange("p e t -> p t e"), AX.X, ALU.add))
            nc.vector.tensor_scalar(keep[:, 0, :], slotf[:, :], -1.0, 1.0, ALU.mult, ALU.add).then_inc(counted, 1)
            rank(2)
            step(nc.vector.tensor_tensor(place[:, :, :], place[:, :, :], wide(start[:, :]), ALU.add))
            step(nc.vector.tensor_tensor(place[:, :, :], place[:, :, :], keep[:, :, :], ALU.mult))
            step(nc.vector.tensor_reduce(slotf[:, :], place[:, :, :].rearrange("p e t -> p t e"), AX.X, ALU.add))
            step(nc.vector.tensor_copy(SLOT[:, 0:TILES], slotf[:, :]))
            nc.vector.tensor_copy(scatter_slot[:, :], slotf[:, :]).then_inc(slots_d, 1)
            block_table(nc, dve, c, count[:, :], E1, blocks_of(1, E1), tabs, SLOT[:, 0:TILES], slots_d, 1)

        @block.sync
        def _(sp):
            sp.wait_ge(slots_d, 1 + TABLE_STEPS)
            zero_tails(nc, sp, xs, zeros, tabs, E1, surplus_of(1, E1), tails_out)

        @block.gpsimd
        def _(pool):
            pool.wait_ge(slots_d, 1)
            with pool.Fori(0, GROUPS // 2) as r:
                for i in range(2):
                    g = r * 2 + i
                    apart(pool, rows_out[i], r * G * 16, passed)
                    nc.gpsimd.tensor_copy(slot[i][:, :], scatter_slot[:, bass.ds(g * G, G)]).then_inc(copied, 1)
                    nc.gpsimd.tensor_copy(xn[i][:, :, :], XN[:, bass.ds(g * GT, GT)].rearrange("p (t d) -> p t d", t=G)).then_inc(copied, 1)
                    apart(pool, copied, g * 2 + 2, passed)
                    for t in range(G):
                        pool.indirect_dma_start(xs[:, :], bass.IndirectOffsetOnAxis(ap=slot[i][:, t:t + 1], axis=0),
                                                xn[i][:, t, :], None).then_inc(rows_out[i], 16)
            for i in range(2):
                pool.wait_ge(rows_out[i], GROUPS // 2 * G * 16)


def finish(nc, X, SLOT, ys, out):
    with ExitStack() as ctx:
        slot = [ctx.enter_context(nc.sbuf_tensor(f"fi_slot{i}", [P, G], I32)) for i in range(2)]
        rows = [ctx.enter_context(nc.sbuf_tensor(f"fi_rows{i}", [P, G, D], F32)) for i in range(2)]
        rows_in = [ctx.enter_context(nc.semaphore(f"fi_rows_in{i}")) for i in range(2)]
        slots_d, sum_d, out_d, passed = (ctx.enter_context(nc.semaphore(f"fi_{n}")) for n in ("slots", "sum", "out", "passed"))
        block = ctx.enter_context(nc.Block())
        out_v = out.rearrange("b t d -> (b t) d").rearrange("(g t p) d -> p g t d", p=P, t=G)

        @block.gpsimd
        def _(pool):
            with pool.Fori(0, GROUPS // 2) as r:
                for i in range(2):
                    g = r * 2 + i
                    apart(pool, sum_d, 1 + g - 1, passed)
                    nc.gpsimd.tensor_copy(slot[i][:, :], SLOT[:, bass.ds(g * G, G)]).then_inc(slots_d, 1)
                    apart(pool, slots_d, g + 1, passed)
                    for t in range(G):
                        pool.indirect_dma_start(rows[i][:, t, :], None, ys[:, :],
                                                bass.IndirectOffsetOnAxis(ap=slot[i][:, t:t + 1], axis=0)).then_inc(rows_in[i], 16)

        @block.vector
        def _(dve):
            dve.sem_inc(sum_d, 1)
            with dve.Fori(0, GROUPS // 2) as r:
                for i in range(2):
                    g = r * 2 + i
                    Xg = X[:, bass.ds(g * GT, GT)].rearrange("p (t d) -> p t d", t=G)
                    dve.wait_ge(rows_in[i], (r + 1) * G * 16)
                    nc.vector.tensor_tensor(Xg, Xg, rows[i][:, :, :], ALU.add).then_inc(sum_d, 1)

        @block.sync
        def _(sp):
            with sp.Fori(0, GROUPS) as g:
                apart(sp, sum_d, 1 + g + 1, passed)
                sp.dma_start(out_v[:, bass.ds(g, 1)].rearrange("p o t d -> p (o t) d"),
                             X[:, bass.ds(g * GT, GT)].rearrange("p (t d) -> p t d", t=G)).then_inc(out_d, 16)
            sp.wait_ge(out_d, GROUPS * 16)


def program(nc, a, out, upto=99):
    with ExitStack() as ctx:
        def sb(n, shape, dt=F32):
            return ctx.enter_context(nc.sbuf_tensor(n, shape, dt))

        def dram(n, shape, dt=F32):
            return nc.dram_tensor(n, shape, dt, kind="Internal").ap()

        c = {n: sb(f"c_{n}", [P, P]) for n in ("ident", "tri", "stri", "ones", "iota")}
        X, XN = sb("X", [P, TILES * D]), sb("XN", [P, TILES * D])
        GATE, SLOT = sb("GATE", [P, TILES * 2]), sb("SLOT", [P, TILES * 2], I32)
        q3, k3 = dram("q3", [3, UNITS, DH0, T], BF16), dram("k3", [3, UNITS, DH0, T], BF16)
        v0, o0 = dram("v0", [UNITS, P, KT * DH0]), dram("o0", [UNITS, DH0, T])
        xs0, ys0 = dram("xs0", [E0 * REGION + surplus_of(2, E0) * BT, D]), dram("ys0", [blocks_of(2, E0) * BT, D])
        NB0 = blocks_of(2, E0)
        xs1, ys1 = dram("xs1", [E1 * REGION + surplus_of(1, E1) * BT, D]), dram("ys1", [blocks_of(1, E1) * BT, D])
        NB1 = blocks_of(1, E1)
        BESTP, HOT = sb("BESTP", [P, TILES]), sb("HOT", [P, E1, TILES])
        tabs1 = tables(ctx, nc, "t1", 1, E1)
        tabs0 = tables(ctx, nc, "t0", 2, E0)
        constants(nc, c)
        project(nc, c, X, a["x"], a, q3, k3, v0)
        if upto >= 2:
            attend(nc, c, q3, k3, v0, o0)
        if upto >= 3:
            route2(nc, c, X, XN, GATE, SLOT, tabs0, a, o0, xs0)
        if upto >= 4:
            experts(nc, c, "e0", E0, F0, ACT.Gelu, tabs0, NB0, surplus_of(2, E0), {"W1": a["w1"], "b1": a["b1"], "W2": a["w2"], "b2": a["b2"]}, xs0, ys0)
        if upto >= 5:
            linear(nc, c, X, XN, GATE, SLOT, BESTP, HOT, a, ys0)
        if upto >= 6:
            capacity(nc, c, XN, BESTP, HOT, SLOT, tabs1, xs1)
        if upto >= 7:
            experts(nc, c, "e1", E1, F1, ACT.Relu, tabs1, NB1, surplus_of(1, E1), {"W1": a["W1"], "b1": a["B1"], "W2": a["W2"], "b2": a["B2"]}, xs1, ys1)
        if upto >= 8:
            finish(nc, X, SLOT, ys1, out)


def layout(d):
    import numpy as np
    t = lambda a: np.ascontiguousarray(np.swapaxes(a, -1, -2))
    col = lambda b: np.ascontiguousarray(b.reshape(b.shape[0], -1, P).transpose(0, 2, 1))
    return {"x": d["L0_attn_x"], "WqT": t(d["L0_attn_Wq"]), "WdT": t(d["L0_attn_Wkv_down"]),
            "WkuT": t(d["L0_attn_Wk_up"]), "WvuT": t(d["L0_attn_Wv_up"]), "WoT": t(d["L0_attn_Wo"]),
            "gateT": t(d["L0_ffn_gate_w"]), "w1": d["L0_ffn_w1"], "b1": col(d["L0_ffn_b1"]),
            "w2": d["L0_ffn_w2"], "b2": d["L0_ffn_b2"],
            "WqkvT": np.concatenate([t(d["L1_attn_Wq"]), t(d["L1_attn_Wk"]), t(d["L1_attn_Wv"])], axis=1),
            "Wo1T": t(d["L1_attn_Wo"]), "routerT": t(d["L1_ffn_router_w"]), "W1": d["L1_ffn_W1"],
            "B1": col(d["L1_ffn_b1"]), "W2": d["L1_ffn_W2"], "B2": d["L1_ffn_b2"]}


def kernel(**inputs):
    import numpy as np
    import concourse.bacc as bacc
    from concourse.bass_utils import run_bass_kernel_spmd

    arrays = {k: np.ascontiguousarray(v) for k, v in layout({k: np.asarray(v) for k, v in inputs.items()}).items()}
    nc = bacc.Bacc("TRN2", target_bir_lowering=False, num_devices=1)
    a = {k: nc.dram_tensor(f"in_{k}", v.shape, mybir.dt.from_np(v.dtype), kind="ExternalInput").ap()
         for k, v in arrays.items()}
    out = nc.dram_tensor("out_0", (B, T, D), F32, kind="ExternalOutput").ap()
    program(nc, a, out)
    r = run_bass_kernel_spmd(nc, [{f"in_{k}": v for k, v in arrays.items()}], core_ids=[0])
    return r.results[0]["out_0"]
```

```python
from contextlib import ExitStack

import concourse.bass as bass
from concourse import mybir

F32 = mybir.dt.float32
BF16 = mybir.dt.bfloat16
I32 = mybir.dt.int32
U32 = mybir.dt.uint32
ALU = mybir.AluOpType
ACT = mybir.ActivationFunctionType
AX = mybir.AxisListType

P = 128
B, T, D = 8, 1024, 128
NTOK = B * T
TILES = NTOK // P
G = 4
GT = G * P
GROUPS = TILES // G
H0, DH0, LR = 8, 32, 64
HW0 = H0 * DH0
UNITS = B * H0
KT = T // P
HALF = 512
SCALE = float(DH0) ** -0.5
H1, DH1 = 16, 8
KV1 = H1 * DH1 * DH1
E0, F0 = 14, 256
E1, F1 = 8, 512
BT = 256
REGION = NTOK + BT
LN_EPS = 1e-5
FEAT_EPS = 1e-6
CAP1 = -(-NTOK // E1 * 5 // 4)
assert CAP1 == 1280


def surplus_of(choices, experts):
    return blocks_of(choices, experts) - choices * NTOK // BT


def blocks_of(choices, experts):
    n = choices * NTOK // BT + experts - 1
    return n + n % 2


def apart(eng, sem, value, passed):
    eng.wait_ge(sem, value)
    eng.sem_inc(passed, 1)


def semaphores(ctx, nc, prefix, odd):
    free = sorted(nc.free_semaphores)
    ids = iter(free[len(free) // 2:] if odd else free[:len(free) // 2])
    held = []

    def sem(name):
        held.append(nc.alloc_semaphore(f"{prefix}_{name}", num=next(ids)))
        return held[-1]

    ctx.callback(lambda: nc.clear_and_free_semaphores(held))
    return sem


def layer_norm(nc, dve, passed, act_done, x, xn, stats, mv, rstd, stats_done, var_done, rstd_done, xn_done, n):
    for t in range(G):
        last = nc.vector.bn_stats(stats[:, t, :], x[:, t, :])
    last.then_inc(stats_done, 1)
    apart(dve, stats_done, 2 * n + 1, passed)
    for t in range(G):
        last = nc.vector.bn_aggr(mv[:, t, :], stats[:, t, :])
    last.then_inc(stats_done, 1)
    dve.wait_ge(stats_done, 2 * n + 2)
    nc.vector.tensor_scalar(rstd[:, :], mv[:, :, 1], LN_EPS, None, ALU.add).then_inc(var_done, 1)
    dve.wait_ge(act_done, n + 1)
    nc.vector.reciprocal(rstd[:, :], rstd[:, :]).then_inc(rstd_done, 1)
    dve.wait_ge(rstd_done, n + 1)
    for t in range(G):
        last = nc.vector.tensor_scalar(xn[:, t, :], x[:, t, :], mv[:, t, 0:1], rstd[:, t:t + 1],
                                       ALU.subtract, ALU.mult)
    last.then_inc(xn_done, 1)


def constants(nc, c):
    with ExitStack() as ctx:
        sem = semaphores(ctx, nc, "c", True)
        fill, done = sem("fill"), sem("done")
        block = ctx.enter_context(nc.Block())

        @block.gpsimd
        def _(pool):
            nc.gpsimd.memset(c["ident"][:, :], 0.0).then_inc(fill, 1)
            nc.gpsimd.memset(c["tri"][:, :], 1.0).then_inc(fill, 1)
            nc.gpsimd.memset(c["stri"][:, :], 1.0).then_inc(fill, 1)
            nc.gpsimd.memset(c["ones"][:, :], 1.0).then_inc(fill, 1)
            pool.wait_ge(fill, 4)
            nc.gpsimd.affine_select(out=c["ident"][:, :], in_=c["ident"][:, :], compare_op=ALU.not_equal,
                                    fill=1.0, base=0, pattern=[[-1, P]], channel_multiplier=1).then_inc(done, 1)
            nc.gpsimd.affine_select(out=c["tri"][:, :], in_=c["tri"][:, :], compare_op=ALU.is_ge,
                                    fill=0.0, base=0, pattern=[[1, P]], channel_multiplier=-1).then_inc(done, 1)
            nc.gpsimd.affine_select(out=c["stri"][:, :], in_=c["stri"][:, :], compare_op=ALU.is_gt,
                                    fill=0.0, base=0, pattern=[[1, P]], channel_multiplier=-1).then_inc(done, 1)
            nc.gpsimd.iota(c["iota"][:, :], pattern=[[1, 128]], base=0, channel_multiplier=0,
                           allow_small_or_imprecise_dtypes=True).then_inc(done, 1)
            pool.wait_ge(done, 4)


def project(nc, c, X, x_in, w, q3, k3, v0):
    with ExitStack() as ctx:
        def sb(name, shape, dt=F32):
            return ctx.enter_context(nc.sbuf_tensor(name, shape, dt))

        sem = semaphores(ctx, nc, "pj", False)

        wq, wd = sb("wq", [P, HW0]), sb("wd", [P, LR])
        wku, wvu = sb("wku", [LR, HW0]), sb("wvu", [LR, HW0])
        stats, mv, rstd = sb("pj_stats", [P, G, 6]), sb("pj_mv", [P, G, 2]), sb("pj_rstd", [P, G])
        xn = sb("pj_xn", [P, G, D])
        xT = sb("pj_xT", [P, GT])
        lat = sb("pj_lat", [LR, GT])
        hi, mid, lo = (sb(f"pj_{n}", [P, 4, GT], BF16) for n in ("hi", "mid", "lo"))
        rest = sb("pj_rest", [P, 4, GT])
        vs = sb("pj_v", [P, H0, KT, DH0])
        p_xT = ctx.enter_context(nc.psum_tensor("pj_pxT", [P, GT], F32))
        p_lat = ctx.enter_context(nc.psum_tensor("pj_plat", [P, GT], F32))
        p_qk = ctx.enter_context(nc.psum_tensor("pj_pqk", [P, 4, GT], F32))
        p_v = ctx.enter_context(nc.psum_tensor("pj_pv", [P, G, HW0], F32))
        (w_in, stats_d, var_d, root_d, rstd_d, xn_d, pxT_d, xT_d, plat_d, lat_d, pqk_d, hi_d,
         rest_d, mid_d, lo_d, pv_d, v_d, hi_out, mid_out, lo_out, v_out, passed) = (
            sem(n) for n in ("w_in", "stats", "var", "root", "rstd", "xn", "pxT", "xT",
                             "plat", "lat", "pqk", "hi_d", "rest_d", "mid_d", "lo_d", "pv",
                             "v_d", "hi_out", "mid_out", "lo_out", "v_out", "passed"))
        x_arrived = [sem(f"x_in{i}") for i in range(2)]
        block = ctx.enter_context(nc.Block())
        x_v = x_in.rearrange("b t d -> (b t) d").rearrange("(g t p) d -> p g t d", p=P, t=G)

        def after(g, n=1):
            return g[0] + (g[1] + n) // 2, (g[1] + n) % 2

        def number(g):
            return g[0] * 2 + g[1]

        def exists(g):
            return not isinstance(number(g), int) or 0 <= number(g) < GROUPS

        def from_first(eng, sem, value):
            if not (isinstance(value, int) and value <= 0):
                eng.wait_ge(sem, value)

        def groups(eng, iteration):
            for g in range(-2, 2):
                iteration((g // 2, g % 2))
            with eng.Fori(0, B - 3) as r:
                for i in range(2):
                    iteration((r + 1, i))
            for g in range(GROUPS - 4, GROUPS):
                iteration((g // 2, g % 2))

        def x_of(g):
            return X[:, bass.ds(number(g) * GT, GT)].rearrange("p (t d) -> p t d", t=G)

        @block.sync
        def _(sp):
            def load(g):
                sp.dma_start(x_of(g), x_v[:, bass.ds(number(g), 1)].rearrange("p o t d -> p (o t) d")).then_inc(x_arrived[g[1]], 16)

            def store(g, part, plane, ready, sent, s, dram):
                b, i = g
                apart(sp, ready, 2 * number(g) + s + 1, passed)
                for cc in range(2):
                    dst = dram[part, bass.ds(b * H0 + cc * 4, 4), :, i * GT:(i + 1) * GT]
                    sp.dma_start(dst.rearrange("h d t -> (h d) t"), plane[:, 2 * s + cc, :]).then_inc(sent, 16)

            def iteration(g):
                if exists(after(g, 4)):
                    apart(sp, var_d, number(g) + 3, passed)
                    load(after(g, 4))
                if exists(g):
                    for part, plane, ready, sent in ((0, hi, hi_d, hi_out), (1, mid, mid_d, mid_out), (2, lo, lo_d, lo_out)):
                        for s, dram in ((0, q3), (1, k3)):
                            store(g, part, plane, ready, sent, s, dram)
                    if g[1] == 1:
                        apart(sp, v_d, number(g) + 1, passed)
                        sp.dma_start(v0[bass.ds(g[0] * H0, H0)].rearrange("h p x -> p h x"),
                                     vs[:, :, :, :].rearrange("p h k d -> p h (k d)")).then_inc(v_out, 16)

            load((0, 0))
            for dst, src in ((wq, w["WqT"]), (wd, w["WdT"]), (wku, w["WkuT"]), (wvu, w["WvuT"])):
                sp.dma_start(dst[:, :], src).then_inc(w_in, 16)
            load((0, 1))
            groups(sp, iteration)
            sp.wait_ge(hi_out, GROUPS * 64)
            sp.wait_ge(mid_out, GROUPS * 64)
            sp.wait_ge(lo_out, GROUPS * 64)
            sp.wait_ge(v_out, B * 16)

        @block.tensor
        def _(pe):
            def turn(g):
                n = number(g)
                pe.wait_ge(xn_d, n + 1)
                from_first(pe, xT_d, n)
                for t in range(G):
                    mm = nc.tensor.transpose(p_xT[:, t * P:(t + 1) * P], xn[:, t, :], c["ident"][:, :])
                mm.then_inc(pxT_d, 1)

            def iteration(g):
                n = number(g)
                if exists(g):
                    pe.wait_ge(xT_d, n + 1)
                    from_first(pe, lat_d, n)
                    nc.tensor.matmul(p_lat[0:LR, :], wd[:, :], xT[:, :], start=True, stop=True).then_inc(plat_d, 1)
                    from_first(pe, rest_d, 2 * n - 1)
                    for cc in range(2):
                        mm = nc.tensor.matmul(p_qk[:, cc, :], wq[:, cc * P:(cc + 1) * P], xT[:, :], start=True, stop=True)
                    mm.then_inc(pqk_d, 1)
                    pe.wait_ge(lat_d, n + 1)
                    from_first(pe, rest_d, 2 * n)
                    for cc in range(2):
                        mm = nc.tensor.matmul(p_qk[:, 2 + cc, :], wku[:, cc * P:(cc + 1) * P], lat[:, :], start=True, stop=True)
                    mm.then_inc(pqk_d, 1)
                if exists(after(g)):
                    turn(after(g))
                if exists(g):
                    from_first(pe, v_d, n)
                    for t in range(G):
                        mm = nc.tensor.matmul(p_v[:, t, :], lat[:, t * P:(t + 1) * P], wvu[:, :], start=True, stop=True)
                    mm.then_inc(pv_d, 1)

            pe.wait_ge(w_in, 64)
            groups(pe, iteration)

        @block.scalar
        def _(act):
            def high(g, s):
                n = number(g)
                act.wait_ge(pqk_d, 2 * n + s + 1)
                from_first(act, hi_out, n * 64)
                nc.scalar.copy(hi[:, 2 * s:2 * s + 2, :], p_qk[:, 2 * s:2 * s + 2, :]).then_inc(hi_d, 1)

            def middle(g, s):
                n = number(g)
                act.wait_ge(rest_d, 2 * n + s + 1)
                from_first(act, mid_out, n * 64)
                nc.scalar.copy(mid[:, 2 * s:2 * s + 2, :], rest[:, 2 * s:2 * s + 2, :]).then_inc(mid_d, 1)

            def iteration(g):
                n = number(g)
                if exists(g):
                    act.wait_ge(plat_d, n + 1)
                    from_first(act, pv_d, n)
                    nc.scalar.copy(lat[:, :], p_lat[0:LR, :]).then_inc(lat_d, 1)
                    high(g, 0)
                if exists(after(g, 2)):
                    act.wait_ge(var_d, n + 3)
                    nc.scalar.activation(rstd[:, :], rstd[:, :], ACT.Sqrt).then_inc(root_d, 1)
                if exists(g):
                    high(g, 1)
                if exists(after(g)):
                    act.wait_ge(pxT_d, n + 2)
                    nc.scalar.copy(xT[:, :], p_xT[:, :]).then_inc(xT_d, 1)
                if exists(g):
                    middle(g, 0)
                    middle(g, 1)

            groups(act, iteration)

        @block.vector
        def _(dve):
            def moments(g):
                n = number(g)
                apart(dve, x_arrived[g[1]], (g[0] + 1) * 16, passed)
                for t in range(G):
                    last = nc.vector.bn_stats(stats[:, t, :], x_of(g)[:, t, :])
                last.then_inc(stats_d, 1)
                apart(dve, stats_d, 2 * n + 1, passed)
                for t in range(G):
                    last = nc.vector.bn_aggr(mv[:, t, :], stats[:, t, :])
                last.then_inc(stats_d, 1)
                dve.wait_ge(stats_d, 2 * n + 2)
                nc.vector.tensor_scalar(rstd[:, :], mv[:, :, 1], LN_EPS, None, ALU.add).then_inc(var_d, 1)

            def normalise(g):
                n = number(g)
                dve.wait_ge(root_d, n + 1)
                nc.vector.reciprocal(rstd[:, :], rstd[:, :]).then_inc(rstd_d, 1)
                from_first(dve, pxT_d, n)
                dve.wait_ge(rstd_d, n + 1)
                for t in range(G):
                    last = nc.vector.tensor_scalar(xn[:, t, :], x_of(g)[:, t, :], mv[:, t, 0:1], rstd[:, t:t + 1],
                                                   ALU.subtract, ALU.mult)
                last.then_inc(xn_d, 1)

            def remainder(g, s):
                n = number(g)
                dve.wait_ge(hi_d, 2 * n + s + 1)
                from_first(dve, lo_d, 2 * n + s - 1)
                cols = slice(2 * s, 2 * s + 2)
                nc.vector.tensor_tensor(rest[:, cols, :], p_qk[:, cols, :], hi[:, cols, :], ALU.subtract).then_inc(rest_d, 1)

            def iteration(g):
                n, (b, half) = number(g), g
                if exists(after(g)):
                    normalise(after(g))
                if exists(after(g, 2)):
                    moments(after(g, 2))
                if exists(g):
                    remainder(g, 0)
                    remainder(g, 1)
                    dve.wait_ge(pv_d, n + 1)
                    if half == 0:
                        from_first(dve, v_out, b * 16)
                    nc.vector.tensor_copy(vs[:, :, half * G:(half + 1) * G, :].rearrange("p h k d -> p k h d"),
                                          p_v[:, :, :].rearrange("p k (h d) -> p k h d", h=H0)).then_inc(v_d, 1)

            groups(dve, iteration)

        @block.gpsimd
        def _(pool):
            def iteration(g):
                n = number(g)
                if exists(g):
                    for s in range(2):
                        cols = slice(2 * s, 2 * s + 2)
                        pool.wait_ge(mid_d, 2 * n + s + 1)
                        from_first(pool, lo_out, n * 64)
                        nc.gpsimd.tensor_tensor(lo[:, cols, :], rest[:, cols, :], mid[:, cols, :], ALU.subtract).then_inc(lo_d, 1)

            groups(pool, iteration)


SLOTS = 4
MAX_PLAN = (0, 2, 2, 2, 3, 3, 2, 2)
POOL_SUMS = (1, 2, 4, 5, 6)


def attend(nc, c, q3, k3, v0, o0):
    with ExitStack() as ctx:
        def sb(name, shape, dt=F32):
            return ctx.enter_context(nc.sbuf_tensor(name, shape, dt))

        sem = semaphores(ctx, nc, "at", True)

        KB = 2 * DH0 + 2
        Q = T // 4
        qa = [sb(f"qa{s}", [P, T], BF16) for s in range(SLOTS)]
        ka = [sb(f"ka{s}", [P, T], BF16) for s in range(SLOTS)]
        qb = [sb(f"qb{s}", [KB, T], BF16) for s in range(SLOTS)]
        kb = [sb(f"kb{s}", [KB, T], BF16) for s in range(SLOTS)]
        v = [sb(f"vh{s}", [P, KT, DH0]) for s in range(SLOTS)]
        probs = [sb(f"probs{k}", [P, T]) for k in range(KT)]
        sum_p = [sb(f"sum_p{i}", [P, T]) for i in range(2)]
        sum_v = [sb(f"sum_v{i}", [P, T]) for i in range(2)]
        halfmax, rowmax = sb("halfmax", [P, 2, KT]), sb("rowmax", [P, KT])
        max_hi, max_lo = (sb(n, [KT, P], BF16) for n in ("max_hi", "max_lo"))
        inv = sb("inv", [P, Q])
        ot = [sb(f"ot{i}", [P, Q]) for i in range(2)]
        p_s = [ctx.enter_context(nc.psum_tensor(f"p_s{i}", [P, T], F32)) for i in range(2)]
        p_m = [ctx.enter_context(nc.psum_tensor(f"p_m{i}", [P, HALF], F32)) for i in range(2)]
        p_o = [ctx.enter_context(nc.psum_tensor(f"p_o{i}", [P, 2, Q], F32)) for i in range(2)]
        operands_in = [sem(f"operands_in{s}") for s in range(SLOTS)]
        o_out = [sem(f"o_out{i}") for i in range(2)]
        (ones_d, max_scores, max_read, max_row, max_T, max_parts, max_hi_d, max_in, scores,
         probs_d, pv_d, sum_p_d, sum_v_d, den_d, inv_d, o_d, passed) = (
            sem(f"{n}") for n in ("ones", "max_scores", "max_read", "max_row", "max_T",
                                     "max_parts", "max_hi_d", "max_in", "scores", "probs", "pv",
                                     "sum_p", "sum_v", "den", "inv", "o", "passed"))
        PV0, O0, DEN0, SP0, SV0, ONE = SLOTS * KT, 3, 3, len(POOL_SUMS) + 1, 2, 1
        LOADS, LAST = 9, UNITS // SLOTS - 1
        block = ctx.enter_context(nc.Block())

        def after(r, s, n=1):
            return (r, s + n) if s + n < SLOTS else (r + 1, s + n - SLOTS)

        def exists(r, s, n=0):
            r, s = after(r, s, n)
            return not isinstance(r, int) or r <= LAST

        def load(sp, r, s):
            u = r * SLOTS + s
            if not (isinstance(r, int) and r == 0):
                apart(sp, pv_d, PV0 + (u - SLOTS + 1) * KT, passed)

            def rows(dram, part):
                return dram[part, bass.ds(u, 1)].rearrange("o d t -> (o d) t")

            def parts(dram):
                return dram[0:2, bass.ds(u, 1)].rearrange("a o d t -> a (o d) t")

            for i in range(2):
                sp.dma_start(qa[s][i * 64:(i + 1) * 64, :], rows(q3, i).unsqueeze(0).broadcast_to([2, DH0, T])).then_inc(operands_in[s], 16)
                sp.dma_start(ka[s][i * 64:(i + 1) * 64, :], parts(k3)).then_inc(operands_in[s], 16)
            for i, (qp, kp) in enumerate(((0, 2), (2, 0))):
                sp.dma_start(qb[s][i * DH0:(i + 1) * DH0, :], rows(q3, qp)).then_inc(operands_in[s], 16)
                sp.dma_start(kb[s][i * DH0:(i + 1) * DH0, :], rows(k3, kp)).then_inc(operands_in[s], 16)
            sp.dma_start(v[s][:, :, :].rearrange("p k d -> p (k d)"),
                         v0[bass.ds(u, 1)].rearrange("o p x -> (o p) x")).then_inc(operands_in[s], 16)

        def rows_of_maxima(sp, r, s):
            apart(sp, max_parts, ONE + r * SLOTS + s + 1, passed)
            sp.dma_start(qb[s][2 * DH0:2 * DH0 + 1, :], max_hi[:, :]).then_inc(max_in, 16)
            sp.dma_start(qb[s][2 * DH0 + 1:KB, :], max_lo[:, :]).then_inc(max_in, 16)

        def store(sp, r, s):
            u = r * SLOTS + s
            apart(sp, o_d, O0 + u + 1, passed)
            for j in range(4):
                sp.dma_start(o0[bass.ds(u, 1), :, j * Q:(j + 1) * Q].rearrange("o d t -> (o d) t"),
                             ot[s % 2][j * DH0:(j + 1) * DH0, :]).then_inc(o_out[s % 2], 16)

        @block.sync
        def _(sp):
            for s in range(SLOTS):
                load(sp, 0, s)
            for sm in (max_parts, max_in, *o_out):
                sp.sem_inc(sm, ONE)
            rows_of_maxima(sp, 0, 0)
            with sp.Fori(0, LAST) as r:
                for s in range(SLOTS):
                    rows_of_maxima(sp, *after(r, s))
                    load(sp, r + 1, s)
                    store(sp, r, s)
            for s in range(SLOTS):
                if exists(LAST, s, 1):
                    rows_of_maxima(sp, *after(LAST, s))
                store(sp, LAST, s)
            for out_s in o_out:
                sp.wait_ge(out_s, ONE + UNITS // 2 * 64)

        @block.gpsimd
        def _(pool):
            for s in range(SLOTS):
                nc.gpsimd.memset(kb[s][2 * DH0:KB, :], 1.0).then_inc(ones_d, 1)
            pool.sem_inc(sum_p_d, SP0)
            with pool.Fori(0, UNITS // SLOTS) as r:
                for s in range(SLOTS):
                    u = r * SLOTS + s
                    pool.wait_ge(den_d, DEN0 + u - 1)
                    for n, k in enumerate(POOL_SUMS):
                        pool.wait_ge(probs_d, u * KT + k + 1)
                        if n:
                            pool.wait_ge(sum_p_d, SP0 + u * len(POOL_SUMS) + n)
                        nc.gpsimd.tensor_tensor(sum_p[s % 2][:, :], (sum_p[s % 2] if n else probs[0])[:, :],
                                                probs[k][:, :], ALU.add).then_inc(sum_p_d, 1)

        def max_half(pe, r, s, n):
            u = r * SLOTS + s
            if n == 0:
                pe.wait_ge(operands_in[s], (r + 1) * LOADS * 16)
                pe.wait_ge(max_parts, ONE + u)
            if n >= 2:
                pe.wait_ge(max_read, u * 2 * KT + n - 1)
            nc.tensor.matmul(p_m[n % 2][:, :], qa[s][:, (n // 2) * P:(n // 2 + 1) * P],
                             ka[s][:, (n % 2) * HALF:(n % 2 + 1) * HALF], start=True, stop=True).then_inc(max_scores, 1)

        def max_turn(pe, r, s):
            pe.wait_ge(max_row, ONE + r * SLOTS + s + 1)
            nc.tensor.transpose(p_m[0][0:KT, 0:P], rowmax[:, :], c["ident"][:, :]).then_inc(max_T, 1)

        def score(pe, r, s, k, h):
            u = r * SLOTS + s
            if k == 0 and h == 0:
                pe.wait_ge(max_in, ONE + (u + 1) * 32)
            g = u * KT + k
            if h == 0 and not (isinstance(g, int) and g < 2):
                pe.wait_ge(probs_d, g - 1)
            cols, q = slice(k * P, (k + 1) * P), slice(h * HALF, (h + 1) * HALF)
            nc.tensor.matmul(p_s[k % 2][:, q], ka[s][:, cols], qa[s][:, q], start=True, stop=False)
            mm = nc.tensor.matmul(p_s[k % 2][:, q], kb[s][:, cols], qb[s][:, q], start=False, stop=True)
            if h == 1:
                mm.then_inc(scores, 1)

        def spread(pe, s, col, lhs, rhs, start, stop):
            for j in range(4):
                mm = nc.tensor.matmul(p_o[s % 2][j * DH0:(j + 1) * DH0, col, :], lhs, rhs[:, j * Q:(j + 1) * Q],
                                      start=start, stop=stop, skip_group_check=True, tile_position=(0, j * DH0))
            return mm

        def values(pe, r, s, k):
            u = r * SLOTS + s
            pe.wait_ge(probs_d, u * KT + k + 1)
            if k == 0:
                pe.wait_ge(o_d, O0 + u - 1)
            spread(pe, s, 0, v[s][:, k, :], probs[k], k == 0, k == KT - 1).then_inc(pv_d, 1)

        def denominators(pe, r, s):
            u = r * SLOTS + s
            pe.wait_ge(sum_p_d, SP0 + (u + 1) * len(POOL_SUMS))
            pe.wait_ge(sum_v_d, SV0 + u + 1)
            spread(pe, s, 1, c["ones"][:, 0:DH0], sum_p[s % 2], False, False)
            spread(pe, s, 1, c["ones"][:, 0:DH0], sum_v[s % 2], False, True).then_inc(den_d, 1)

        def key_tile(pe, r, s, k):
            halves = list(range(sum(MAX_PLAN[:k]), sum(MAX_PLAN[:k + 1]))) if exists(r, s, 2) else []
            nxt = (r, s, k + 1) if k + 1 < KT else (*after(r, s), 0)
            for h in range(2):
                if exists(*nxt[:2]):
                    score(pe, *nxt, h)
                if halves:
                    max_half(pe, *after(r, s, 2), halves.pop(0))
            if k == 0 and exists(r, s, 1):
                max_turn(pe, *after(r, s))
            values(pe, r, s, k)
            for n in halves:
                max_half(pe, *after(r, s, 2), n)

        def rest_of_head(pe, r, s):
            for k in range(2, KT):
                key_tile(pe, r, s, k)
            if exists(r, s, 1):
                for k in range(2):
                    key_tile(pe, *after(r, s), k)
            denominators(pe, r, s)

        @block.tensor
        def _(pe):
            pe.sem_inc(pv_d, PV0)
            pe.sem_inc(den_d, DEN0)
            pe.wait_ge(ones_d, SLOTS)
            for n in range(2 * KT):
                max_half(pe, 0, 0, n)
            max_turn(pe, 0, 0)
            for n in range(2 * KT):
                max_half(pe, 0, 1, n)
            for h in range(2):
                score(pe, 0, 0, 0, h)
            for k in range(2):
                key_tile(pe, 0, 0, k)
            with pe.Fori(0, LAST) as r:
                for s in range(SLOTS):
                    rest_of_head(pe, r, s)
            for s in range(SLOTS):
                rest_of_head(pe, LAST, s)

        @block.scalar
        def _(act):
            with act.Fori(0, UNITS // SLOTS) as r:
                for s in range(SLOTS):
                    u = r * SLOTS + s
                    for k in range(KT):
                        act.wait_ge(scores, u * KT + k + 1)
                        act.wait_ge(pv_d, PV0 + (u - 1) * KT + k + 1)
                        if k in (3, 7):
                            act.wait_ge(sum_v_d, SV0 + u)
                        else:
                            act.wait_ge(sum_p_d, SP0 + (u - 1) * len(POOL_SUMS) + 1 + (POOL_SUMS.index(k) if k else 0))
                        nc.scalar.activation(probs[k][:, :], p_s[k % 2][:, :], ACT.Exp, scale=SCALE).then_inc(probs_d, 1)

        def half_maxima(dve, r, s, which):
            u = r * SLOTS + s
            for n in which:
                dve.wait_ge(max_scores, u * 2 * KT + n + 1)
                if n == 0:
                    dve.wait_ge(max_row, ONE + u)
                nc.vector.reduce_max(halfmax[:, n % 2, n // 2:n // 2 + 1], p_m[n % 2][:, :], AX.X).then_inc(max_read, 1)

        def row_maxima(dve, r, s):
            u = r * SLOTS + s
            dve.wait_ge(max_read, (u + 1) * 2 * KT)
            nc.vector.tensor_tensor(rowmax[:, :], halfmax[:, 0, :], halfmax[:, 1, :], ALU.max).then_inc(max_row, 1)

        def split_maxima(dve, r, s):
            u = r * SLOTS + s
            dve.wait_ge(max_T, u + 1)
            dve.wait_ge(max_in, ONE + u * 32)
            nc.vector.tensor_scalar(max_hi[:, :], p_m[0][0:KT, 0:P], -1.0, None, ALU.mult).then_inc(max_hi_d, 1)
            dve.wait_ge(max_hi_d, u + 1)
            nc.vector.scalar_tensor_tensor(out=max_lo[:, :], in0=p_m[0][0:KT, 0:P], scalar=-1.0,
                                           in1=max_hi[:, :], op0=ALU.mult, op1=ALU.subtract).then_inc(max_parts, 1)

        def add_last_tiles(dve, r, s):
            u = r * SLOTS + s
            dve.wait_ge(probs_d, (u + 1) * KT)
            dve.wait_ge(den_d, DEN0 + u - 1)
            nc.vector.tensor_tensor(sum_v[s % 2][:, :], probs[3][:, :], probs[7][:, :], ALU.add).then_inc(sum_v_d, 1)

        def normalise(dve, r, s):
            u = r * SLOTS + s
            dve.wait_ge(den_d, DEN0 + u + 1)
            dve.wait_ge(o_d, O0 + u)
            nc.vector.reciprocal(inv[:, :], p_o[s % 2][:, 1, :]).then_inc(inv_d, 1)
            dve.wait_ge(inv_d, u + 1)
            dve.wait_ge(o_out[s % 2], ONE + (r * (SLOTS // 2) + s // 2) * 64)
            nc.vector.tensor_tensor(ot[s % 2][:, :], p_o[s % 2][:, 0, :], inv[:, :], ALU.mult).then_inc(o_d, 1)

        EARLY = range(4)
        LATE = range(4, 2 * KT)

        @block.vector
        def _(dve):
            dve.sem_inc(o_d, O0)
            dve.sem_inc(sum_v_d, SV0)
            dve.sem_inc(max_row, ONE)
            half_maxima(dve, 0, 0, range(2 * KT))
            row_maxima(dve, 0, 0)
            split_maxima(dve, 0, 0)
            half_maxima(dve, 0, 1, range(2 * KT))
            row_maxima(dve, 0, 1)
            split_maxima(dve, 0, 1)
            half_maxima(dve, 0, 2, EARLY)

            def segment(r, s):
                if exists(r, s, 2):
                    half_maxima(dve, *after(r, s, 2), LATE)
                    row_maxima(dve, *after(r, s, 2))
                add_last_tiles(dve, r, s)
                if exists(r, s, 2):
                    split_maxima(dve, *after(r, s, 2))
                if exists(r, s, 3):
                    half_maxima(dve, *after(r, s, 3), EARLY)
                normalise(dve, r, s)

            with dve.Fori(0, LAST) as r:
                for s in range(SLOTS):
                    segment(r, s)
            for s in range(SLOTS):
                segment(LAST, s)


def block_table(nc, dve, c, count, experts, blocks, tabs, SLOT, done, n0):
    n = [n0]

    def step(ins):
        ins.then_inc(done, 1)
        n[0] += 1
        dve.wait_ge(done, n[0])

    R = NTOK // BT
    cmp, used, upto, zero = tabs["cmp"], tabs["used"], tabs["upto"], tabs["zero"]
    ge, past, first, live = tabs["ge"], tabs["past"], tabs["first"], tabs["live"]
    step(nc.vector.memset(zero[:, :], 0.0))
    step(nc.vector.tensor_scalar(cmp[:, 0:R], c["iota"][:, 0:R], float(BT), None, ALU.mult))
    step(nc.vector.tensor_tensor(ge[:, 0:experts * R].rearrange("p (e r) -> p e r", r=R),
                                 count.unsqueeze(2).broadcast_to([P, experts, R]),
                                 cmp[:, 0:R].unsqueeze(1).broadcast_to([P, experts, R]), ALU.is_gt))
    step(nc.vector.tensor_reduce(used[:, :], ge[:, 0:experts * R].rearrange("p (e r) -> p e r", r=R), AX.X, ALU.add))
    step(nc.vector.tensor_tensor_scan(upto[:, :], used[:, :], zero[:, :], 0.0, ALU.add, ALU.add))
    je = ge[:, 0:blocks * experts].rearrange("p (j e) -> p j e", e=experts)
    shape = [P, blocks, experts]
    step(nc.vector.tensor_tensor(je, c["iota"][:, 0:blocks].unsqueeze(2).broadcast_to(shape),
                                 upto[:, :].unsqueeze(1).broadcast_to(shape), ALU.is_ge))
    step(nc.vector.tensor_reduce(past[:, :], je, AX.X, ALU.add))
    step(nc.vector.tensor_tensor(je, je, used[:, :].unsqueeze(1).broadcast_to(shape), ALU.mult))
    step(nc.vector.tensor_reduce(first[:, :], je, AX.X, ALU.add))
    step(nc.vector.tensor_tensor(first[:, :], c["iota"][:, 0:blocks], first[:, :], ALU.subtract))
    step(nc.vector.tensor_scalar(first[:, :], first[:, :], float(BT), None, ALU.mult))
    step(nc.vector.tensor_scalar(live[:, :], past[:, :], float(REGION), None, ALU.mult))
    step(nc.vector.tensor_tensor(tabs["row"][:, :], first[:, :], live[:, :], ALU.add))
    step(nc.vector.tensor_scalar(tabs["expert"][:, :], past[:, :], float(experts - 1), None, ALU.min))
    step(nc.vector.tensor_scalar(cmp[:, 0:experts], c["iota"][:, 0:experts], float(REGION), None, ALU.mult))
    step(nc.vector.tensor_tensor(tabs["tail"][:, :], cmp[:, 0:experts], count, ALU.add))
    slotf, over, jump = tabs["slotf"], tabs["over"], tabs["jump"]
    step(nc.vector.tensor_tensor(upto[:, :], upto[:, :], used[:, :], ALU.subtract))
    step(nc.vector.scalar_tensor_tensor(out=upto[:, :], in0=upto[:, :], scalar=float(BT), in1=cmp[:, 0:experts],
                                        op0=ALU.mult, op1=ALU.subtract))
    step(nc.vector.tensor_tensor(jump[:, :], upto[:, 1:experts], upto[:, 0:experts - 1], ALU.subtract))
    step(nc.vector.tensor_copy(slotf[:, :], SLOT))
    shape = [P, slotf.shape[1], experts - 1]
    step(nc.vector.tensor_tensor(over[:, :, :], slotf[:, :].unsqueeze(2).broadcast_to(shape),
                                 cmp[:, 1:experts].unsqueeze(1).broadcast_to(shape), ALU.is_ge))
    step(nc.vector.tensor_tensor(over[:, :, :], over[:, :, :], jump[:, :].unsqueeze(1).broadcast_to(shape), ALU.mult))
    step(nc.vector.tensor_reduce(tabs["moved"][:, :], over[:, :, :], AX.X, ALU.add))
    step(nc.vector.tensor_tensor(slotf[:, :], slotf[:, :], tabs["moved"][:, :], ALU.add))
    step(nc.vector.tensor_copy(SLOT, slotf[:, :]))


TABLE_STEPS = 17


def tables(ctx, nc, name, choices, experts):
    blocks, slots = blocks_of(choices, experts), choices * TILES
    wide = {"cmp": 128, "used": experts, "upto": experts, "zero": experts, "past": blocks, "first": blocks,
            "ge": max(blocks, NTOK // BT) * experts, "live": blocks, "jump": experts - 1, "slotf": slots,
            "moved": slots}
    tabs = {n: ctx.enter_context(nc.sbuf_tensor(f"{name}_{n}", [P, w], F32)) for n, w in wide.items()}
    tabs["over"] = ctx.enter_context(nc.sbuf_tensor(f"{name}_over", [P, slots, experts - 1], F32))
    for n, w in (("row", blocks), ("expert", blocks), ("tail", experts)):
        tabs[n] = ctx.enter_context(nc.sbuf_tensor(f"{name}_{n}", [P, w], I32))
    return tabs


def zero_tails(nc, sp, xs, zeros, tabs, experts, surplus, out):
    for e in range(experts):
        row = sp.value_load(tabs["tail"][0:1, e:e + 1], min_val=0, max_val=experts * REGION - BT)
        sp.dma_start(xs[bass.ds(row, BT), :].rearrange("(t p) d -> p t d", p=P), zeros[:, :, :]).then_inc(out, 16)
    for n in range(surplus):
        rows = slice(experts * REGION + n * BT, experts * REGION + (n + 1) * BT)
        sp.dma_start(xs[rows, :].rearrange("(t p) d -> p t d", p=P), zeros[:, :, :]).then_inc(out, 16)
    sp.wait_ge(out, (experts + surplus) * 16)


def route2(nc, c, X, XN, GATE, SLOT, tabs, w, o0, xs):
    with ExitStack() as ctx:
        def sb(name, shape, dt=F32):
            return ctx.enter_context(nc.sbuf_tensor(f"r2_{name}", shape, dt))

        sem = semaphores(ctx, nc, "r2", False)

        def ps(name, shape):
            return ctx.enter_context(nc.psum_tensor(f"r2_{name}", shape, F32))

        R = 4
        wo, wg = sb("wo", [P, 2, D]), sb("wg", [P, E0])
        oT = [sb(f"oT{i}", [P, 2, GT]) for i in range(2)]
        xn = [sb(f"xn{s}", [P, G, D]) for s in range(R)]
        slot = [sb(f"slot{s}", [P, G * 2], I32) for s in range(R)]
        stats, mv, rstd = sb("stats", [P, G, 6]), sb("mv", [P, G, 2]), sb("rstd", [P, G])
        xT = sb("xT", [P, GT])
        top, total = sb("top", [P, G]), sb("total", [P, G])
        prob = sb("prob", [P, G, E0])
        best, at = sb("best", [P, G, 8]), sb("at", [P, G, 8], U32)
        atf, slotf = sb("atf", [P, G, 2]), sb("slotf", [P, G, 2])
        hot, both = sb("hot", [P, G, 2, E0]), sb("both", [P, G, E0])
        seen, now = sb("seen", [P, E0]), sb("now", [P, E0])
        start = sb("start", [P, E0])
        place, placed = sb("place", [P, G, E0]), sb("placed", [P, G, 2, E0])
        zeros = sb("zeros", [P, BT // P, D])
        p_y, p_xT = ps("p_y", [P, G, D]), ps("p_xT", [P, GT])
        p_g, p_pos = ps("p_g", [P, 512]), ps("p_pos", [P, 512])
        gate_ps = p_g[:, 0:G * E0].rearrange("p (t e) -> p t e", e=E0)
        pos_ps = p_pos[:, 0:G * E0].rearrange("p (t e) -> p t e", e=E0)
        (w_in, y_d, x_d, stats_d, var_d, root_d, rstd_d, xn_d, pxT_d, xT_d, kept_d, gate_d, top_d, shift_d, exp_d,
         choice, hot_d, now_d, pos_d, places, slot_d, seen_d, sent, count_d, tabs_d, zeros_d, tails_out, passed) = (
            sem(n) for n in ("w_in", "y", "x", "stats", "var", "root", "rstd", "xn", "pxT", "xT", "kept", "gate",
                             "top", "shift", "exp", "choice", "hot", "now", "pos", "places", "slot", "seen", "sent", "count",
                             "tabs", "zeros", "tails_out", "passed"))
        oT_in = [sem(f"oT_in{i}") for i in range(2)]
        rows_out = [sem(f"rows_out{s}") for s in range(R)]
        SENT0 = KEPT0 = R
        block = ctx.enter_context(nc.Block())

        def after(g, n=1):
            return g[0] + (g[1] + n) // R, (g[1] + n) % R

        def number(g):
            return g[0] * R + g[1]

        def exists(g):
            return not isinstance(number(g), int) or 0 <= number(g) < GROUPS

        def from_first(eng, sem, value):
            if not (isinstance(value, int) and value <= 0):
                eng.wait_ge(sem, value)

        def groups(eng, iteration):
            for g in range(3):
                iteration((0, g))
            with eng.Fori(0, GROUPS // R - 1) as r:
                for m in range(3, 3 + R):
                    iteration((r + m // R, m % R))
            for g in range(GROUPS - R + 3, GROUPS + 3):
                iteration((g // R, g % R))

        def group_of(T_, g):
            return T_[:, bass.ds(number(g) * GT, GT)].rearrange("p (t d) -> p t d", t=G)

        @block.sync
        def _(sp):
            def load(g):
                n, i = number(g), g[1] % 2
                if not (isinstance(n, int) and n < 2):
                    apart(sp, y_d, n - 1, passed)
                for cc in range(2):
                    b = g[0] * (R // 2) + g[1] // 2
                    sp.dma_start(oT[i][:, cc, :], o0[bass.ds(b * H0 + cc * 4, 4), :, i * GT:(i + 1) * GT]
                                 .rearrange("h d t -> (h d) t")).then_inc(oT_in[i], 16)

            for cc in range(2):
                sp.dma_start(wo[:, cc, :], w["WoT"][cc * P:(cc + 1) * P, :]).then_inc(w_in, 16)
            sp.dma_start(wg[:, :], w["gateT"]).then_inc(w_in, 16)
            groups(sp, lambda g: load(g) if exists(g) else None)
            sp.wait_ge(zeros_d, 3)
            sp.wait_ge(tabs_d, 1 + TABLE_STEPS)
            zero_tails(nc, sp, xs, zeros, tabs, E0, surplus_of(2, E0), tails_out)

        @block.tensor
        def _(pe):
            def attention(g):
                n, i = number(g), g[1] % 2
                pe.wait_ge(oT_in[i], (g[0] * (R // 2) + g[1] // 2 + 1) * 32)
                from_first(pe, x_d, n)
                for t in range(G):
                    for cc in range(2):
                        mm = nc.tensor.matmul(p_y[:, t, :], oT[i][:, cc, t * P:(t + 1) * P], wo[:, cc, :],
                                              start=(cc == 0), stop=(cc == 1))
                mm.then_inc(y_d, 1)

            def turn(g):
                n = number(g)
                pe.wait_ge(xn_d, n + 1)
                from_first(pe, xT_d, n)
                for t in range(G):
                    mm = nc.tensor.transpose(p_xT[:, t * P:(t + 1) * P], xn[g[1]][:, t, :], c["ident"][:, :])
                mm.then_inc(pxT_d, 1)

            def logits(g):
                n = number(g)
                pe.wait_ge(xT_d, n + 1)
                from_first(pe, shift_d, n)
                for t in range(G):
                    mm = nc.tensor.matmul(gate_ps[:, t, :], xT[:, t * P:(t + 1) * P], wg[:, :], start=True, stop=True)
                mm.then_inc(gate_d, 1)

            def ranks(g):
                n = number(g)
                pe.wait_ge(hot_d, n + 1)
                from_first(pe, seen_d, n)
                for t in range(G):
                    nc.tensor.matmul(pos_ps[:, t, :], c["stri"][:, :], both[:, t, :], start=True, stop=False)
                    for t2 in range(t):
                        nc.tensor.matmul(pos_ps[:, t, :], c["ones"][:, :], both[:, t2, :], start=False, stop=False)
                    mm = nc.tensor.matmul(pos_ps[:, t, :], c["ones"][:, :], seen[:, :], start=False, stop=True)
                mm.then_inc(pos_d, 1)

            def iteration(g):
                if exists(after(g, -1)):
                    turn(after(g, -1))
                    logits(after(g, -1))
                if exists(after(g)):
                    attention(after(g))
                if exists(after(g, -2)):
                    ranks(after(g, -2))

            pe.wait_ge(w_in, 48)
            pe.wait_ge(zeros_d, 3)
            attention((0, 0))
            groups(pe, iteration)
            pe.wait_ge(seen_d, GROUPS)
            nc.tensor.matmul(p_pos[:, 0:E0], c["ones"][:, :], seen[:, :], start=True, stop=True).then_inc(count_d, 1)

        @block.scalar
        def _(act):
            def iteration(g):
                n, before = number(g), after(g, -1)
                if exists(before):
                    act.wait_ge(pxT_d, n)
                    from_first(act, gate_d, n - 1)
                    nc.scalar.copy(xT[:, :], p_xT[:, :]).then_inc(xT_d, 1)
                    nc.scalar.copy(group_of(XN, before), xn[before[1]][:, :, :]).then_inc(kept_d, 1)
                if exists(g):
                    act.wait_ge(var_d, n + 1)
                    nc.scalar.activation(rstd[:, :], rstd[:, :], ACT.Sqrt).then_inc(root_d, 1)
                if exists(before):
                    act.wait_ge(shift_d, n)
                    nc.scalar.activation(prob[:, :, :], prob[:, :, :], ACT.Exp).then_inc(exp_d, 1)

            act.sem_inc(kept_d, KEPT0)
            groups(act, iteration)

        @block.vector
        def _(dve):
            def chain(sem, base):
                n = [0]

                def step(ins):
                    n[0] += 1
                    ins.then_inc(sem, 1)
                    dve.wait_ge(sem, base + n[0])
                return step

            def add_attention(g):
                n = number(g)
                dve.wait_ge(y_d, n + 1)
                nc.vector.tensor_tensor(group_of(X, g), group_of(X, g), p_y[:, :, :], ALU.add).then_inc(x_d, 1)
                apart(dve, x_d, n + 1, passed)
                for t in range(G):
                    last = nc.vector.bn_stats(stats[:, t, :], group_of(X, g)[:, t, :])
                last.then_inc(stats_d, 1)
                apart(dve, stats_d, 2 * n + 1, passed)
                for t in range(G):
                    last = nc.vector.bn_aggr(mv[:, t, :], stats[:, t, :])
                last.then_inc(stats_d, 1)
                dve.wait_ge(stats_d, 2 * n + 2)
                nc.vector.tensor_scalar(rstd[:, :], mv[:, :, 1], LN_EPS, None, ALU.add).then_inc(var_d, 1)

            def normalise(g):
                n, s = number(g), g[1]
                dve.wait_ge(root_d, n + 1)
                nc.vector.reciprocal(rstd[:, :], rstd[:, :]).then_inc(rstd_d, 1)
                apart(dve, sent, SENT0 + n - R + 1, passed)
                apart(dve, kept_d, KEPT0 + n - R + 1, passed)
                dve.wait_ge(rstd_d, n + 1)
                for t in range(G):
                    last = nc.vector.tensor_scalar(xn[s][:, t, :], group_of(X, g)[:, t, :], mv[:, t, 0:1], rstd[:, t:t + 1],
                                                   ALU.subtract, ALU.mult)
                last.then_inc(xn_d, 1)

            def shift_logits(g):
                n = number(g)
                dve.wait_ge(gate_d, n + 1)
                nc.vector.tensor_reduce(top[:, :], gate_ps, AX.X, ALU.max).then_inc(top_d, 1)
                dve.wait_ge(top_d, n + 1)
                nc.vector.tensor_tensor(prob[:, :, :], gate_ps, top[:, :].unsqueeze(2).broadcast_to([P, G, E0]),
                                        ALU.subtract).then_inc(shift_d, 1)

            def choose(g):
                n = number(g)
                step = chain(choice, n * 10)
                dve.wait_ge(exp_d, n + 1)
                step(nc.vector.tensor_reduce(total[:, :], prob[:, :, :], AX.X, ALU.add))
                step(nc.vector.reciprocal(total[:, :], total[:, :]))
                step(nc.vector.tensor_tensor(prob[:, :, :], prob[:, :, :], total[:, :].unsqueeze(2).broadcast_to([P, G, E0]), ALU.mult))
                dve.sem_inc(passed, 1)
                for t in range(G):
                    last = nc.vector.max(best[:, t, :], prob[:, t, :])
                step(last)
                dve.sem_inc(passed, 1)
                for t in range(G):
                    last = nc.vector.max_index(at[:, t, :], best[:, t, :], prob[:, t, :])
                step(last)
                step(nc.vector.tensor_copy(atf[:, :, :], at[:, :, 0:2]))
                step(nc.vector.tensor_tensor(hot[:, :, :, :], c["iota"][:, 0:E0].unsqueeze(1).unsqueeze(1).broadcast_to([P, G, 2, E0]),
                                             atf[:, :, :].unsqueeze(3).broadcast_to([P, G, 2, E0]), ALU.is_equal))
                nc.vector.tensor_tensor(both[:, :, :], hot[:, :, 0, :], hot[:, :, 1, :], ALU.add).then_inc(hot_d, 1)
                step(nc.vector.tensor_tensor(total[:, :], best[:, :, 0], best[:, :, 1], ALU.add))
                step(nc.vector.tensor_scalar(total[:, :], total[:, :], 1e-10, None, ALU.max))
                step(nc.vector.reciprocal(total[:, :], total[:, :]))
                nc.vector.tensor_tensor(GATE[:, bass.ds(n * G * 2, G * 2)].rearrange("p (t k) -> p t k", k=2), best[:, :, 0:2],
                                        total[:, :].unsqueeze(2).broadcast_to([P, G, 2]), ALU.mult)
                dve.wait_ge(hot_d, n + 1)
                nc.vector.tensor_reduce(now[:, :], both[:, :, :].rearrange("p t e -> p e t"), AX.X, ALU.add).then_inc(now_d, 1)

            def find_slots(g):
                n, s = number(g), g[1]
                step = chain(places, n * 3)
                dve.wait_ge(pos_d, n + 1)
                step(nc.vector.tensor_tensor(place[:, :, :], pos_ps, start[:, :].unsqueeze(1).broadcast_to([P, G, E0]), ALU.add))
                step(nc.vector.tensor_tensor(placed[:, :, :, :], hot[:, :, :, :], place[:, :, :].unsqueeze(2).broadcast_to([P, G, 2, E0]), ALU.mult))
                step(nc.vector.tensor_reduce(slotf[:, :, :], placed[:, :, :, :], AX.X, ALU.add))
                nc.vector.tensor_copy(slot[s][:, :], slotf[:, :, :].rearrange("p t k -> p (t k)")).then_inc(slot_d, 1)
                nc.vector.tensor_copy(SLOT[:, bass.ds(n * G * 2, G * 2)], slotf[:, :, :].rearrange("p t k -> p (t k)"))
                dve.wait_ge(now_d, n + 1)
                nc.vector.tensor_tensor(seen[:, :], seen[:, :], now[:, :], ALU.add).then_inc(seen_d, 1)

            def iteration(g):
                before, choosing = after(g, -1), after(g, -2)
                if exists(before):
                    normalise(before)
                if exists(choosing):
                    choose(choosing)
                if exists(g):
                    add_attention(g)
                if exists(before):
                    shift_logits(before)
                if exists(choosing):
                    find_slots(choosing)

            nc.vector.tensor_scalar(start[:, :], c["iota"][:, 0:E0], float(REGION), None, ALU.mult).then_inc(zeros_d, 1)
            nc.vector.memset(zeros[:, :, :], 0.0).then_inc(zeros_d, 1)
            nc.vector.memset(seen[:, :], 0.0).then_inc(zeros_d, 1)
            dve.wait_ge(zeros_d, 3)
            groups(dve, iteration)
            dve.wait_ge(count_d, 1)
            nc.vector.tensor_copy(now[:, :], p_pos[:, 0:E0]).then_inc(tabs_d, 1)
            dve.wait_ge(tabs_d, 1)
            block_table(nc, dve, c, now[:, :], E0, blocks_of(2, E0), tabs, SLOT[:, :], tabs_d, 1)

        @block.gpsimd
        def _(pool):
            def scatter(g):
                s = g[1]
                apart(pool, slot_d, number(g) + 1, passed)
                for t in range(G):
                    for k in range(2):
                        pool.indirect_dma_start(xs[:, :], bass.IndirectOffsetOnAxis(ap=slot[s][:, t * 2 + k:t * 2 + k + 1], axis=0),
                                                xn[s][:, t, :], None).then_inc(rows_out[s], 16)

            def iteration(g):
                if exists(after(g, -2)):
                    scatter(after(g, -2))
                q, s = after(g, -3)
                if exists((q, s)):
                    apart(pool, rows_out[s], (q + 1) * G * 2 * 16, sent)

            pool.sem_inc(sent, SENT0)
            groups(pool, iteration)
            pool.wait_ge(rows_out[R - 1], GROUPS // R * G * 2 * 16)


def experts(nc, c, name, odd, E, F, act_fn, tabs, blocks, surplus, weights, b2_rows, xs, ys):
    with ExitStack() as ctx:
        def sb(n, shape, dt=F32):
            return ctx.enter_context(nc.sbuf_tensor(f"{name}_{n}", shape, dt))

        sem = semaphores(ctx, nc, name, odd)

        def ps(n, shape):
            return ctx.enter_context(nc.psum_tensor(f"{name}_{n}", shape, F32))

        AHEAD = 4
        NF, NT = F // P, BT // P
        W = F + NF + NF * D
        wb = [sb(f"w{i}", [P, W]) for i in range(AHEAD)]
        w1, b1 = [t[:, 0:F] for t in wb], [t[:, F:F + NF] for t in wb]
        w2 = [t[:, F + NF:W].rearrange("p (f d) -> p f d", f=NF) for t in wb]
        b2 = [sb(f"b2_{i}", [P, D]) for i in range(AHEAD)]
        xb = [sb(f"xb{i}", [P, NT, D]) for i in range(AHEAD)]
        y = [sb(f"y{i}", [P, NT, D]) for i in range(AHEAD)]
        xT = [sb(f"xT{i}", [P, BT]) for i in range(2)]
        h = [sb(f"h{i}", [P, NF, BT]) for i in range(2)]
        p_xT = [ps(f"p_xT{i}", [P, 512]) for i in range(2)]
        p_h = [ps(f"p_h{i}", [P, max(NF, 2), BT]) for i in range(2)]
        p_y = [ps(f"p_y{i}", [P, 512]) for i in range(2)]
        rows_in = [sem(f"rows_in{i}") for i in range(AHEAD)]
        weights_in = [sem(f"weights_in{i}") for i in range(AHEAD)]
        y_out = [sem(f"y_out{i}") for i in range(AHEAD)]
        pxT_d, xT_d, ph_d, h_d, py_d, y_d, passed = (sem(n) for n in ("pxT", "xT", "ph", "h", "py", "y", "passed"))
        PH0 = PY0 = 2
        Y0, OUT0 = AHEAD, 1
        block = ctx.enter_context(nc.Block())

        def turn(pe, j, s, q):
            pe.wait_ge(rows_in[s], (q + 1) * 16)
            for t in range(NT):
                mm = nc.tensor.transpose(p_xT[s % 2][:, t * P:(t + 1) * P], xb[s][:, t, :], c["ident"][:, :])
            mm.then_inc(pxT_d, 1)

        def hidden(pe, j, s, q):
            pe.wait_ge(weights_in[s], (q + 1) * 32)
            pe.wait_ge(xT_d, j + 1)
            for f in range(NF):
                mm = nc.tensor.matmul(p_h[s % 2][:, f, :], w1[s][:, f * P:(f + 1) * P], xT[s % 2][:, :], start=True, stop=True)
            mm.then_inc(ph_d, 1)

        def outputs(pe, j, s, q):
            pe.wait_ge(h_d, j + 1)
            pe.wait_ge(y_d, Y0 + j - 1)
            for t in range(NT):
                for f in range(NF):
                    mm = nc.tensor.matmul(p_y[s % 2][:, t * P:(t + 1) * P], h[s % 2][:, f, t * P:(t + 1) * P], w2[s][:, f, :],
                                          start=(f == 0), stop=(f == NF - 1))
            mm.then_inc(py_d, 1)

        def copy_turned(dve, j, s, q):
            dve.wait_ge(pxT_d, j + 1)
            dve.wait_ge(ph_d, PH0 + j - 1)
            nc.vector.tensor_copy(xT[s % 2][:, :], p_xT[s % 2][:, 0:BT]).then_inc(xT_d, 1)

        def activate(act, j, s, q):
            act.wait_ge(ph_d, PH0 + j + 1)
            act.wait_ge(py_d, PY0 + j - 1)
            for f in range(NF):
                last = nc.scalar.activation(h[s % 2][:, f, :], p_h[s % 2][:, f, :], act_fn, bias=b1[s][:, f:f + 1])
            last.then_inc(h_d, 1)

        def add_bias(dve, j, s, q):
            dve.wait_ge(py_d, PY0 + j + 1)
            dve.wait_ge(y_out[s], OUT0 + q * 16)
            nc.vector.tensor_tensor(y[s][:, :, :], p_y[s % 2][:, 0:BT].rearrange("p (t d) -> p t d", t=NT),
                                    b2[s][:, :].unsqueeze(1).broadcast_to([P, NT, D]), ALU.add).then_inc(y_d, 1)

        def load(sp, j, s, q):
            row = sp.value_load(tabs["row"][0:1, bass.ds(j, 1)], min_val=0, max_val=E * REGION + surplus * BT - BT)
            e = sp.value_load(tabs["expert"][0:1, bass.ds(j, 1)], min_val=0, max_val=E - 1)
            sp.dma_start(xb[s][:, :, :], xs[bass.ds(row, BT), :].rearrange("(p t) d -> p t d", p=P)).then_inc(rows_in[s], 16)
            sp.dma_start(wb[s][:, :], weights[bass.ds(e, 1)].rearrange("o p w -> (o p) w")).then_inc(weights_in[s], 16)
            sp.dma_start(b2[s][:, :], b2_rows[bass.ds(e, 1), :].broadcast_to([P, D])).then_inc(weights_in[s], 16)

        def store(sp, j, s, q):
            apart(sp, y_d, Y0 + j + 1, passed)
            sp.dma_start(ys[bass.ds(j * BT, BT), :].rearrange("(p t) d -> p t d", p=P), y[s][:, :, :]).then_inc(y_out[s], 16)

        def steps(eng, first, end, *parts):
            def step(r, k):
                for offset, part in parts:
                    m = k + offset
                    part(eng, r * AHEAD + m, m % AHEAD, r + m // AHEAD)

            rounds = (end - first) // AHEAD
            with eng.Fori(0, rounds) as r:
                for k in range(first, first + AHEAD):
                    step(r, k)
            for k in range(first + rounds * AHEAD, end):
                step(0, k)

        @block.sync
        def _(sp):
            for s in range(AHEAD):
                load(sp, s, s, 0)
            for s in range(AHEAD):
                sp.sem_inc(y_out[s], OUT0)
            steps(sp, 0, blocks - AHEAD, (0, store), (AHEAD, load))
            for j in range(blocks - AHEAD, blocks):
                store(sp, j, j % AHEAD, j // AHEAD)
            for s in range(AHEAD):
                sp.wait_ge(y_out[s], OUT0 + len(range(s, blocks, AHEAD)) * 16)

        @block.tensor
        def _(pe):
            pe.sem_inc(py_d, PY0)
            pe.sem_inc(ph_d, PH0)
            turn(pe, 0, 0, 0)
            hidden(pe, 0, 0, 0)
            turn(pe, 1, 1, 0)
            steps(pe, 1, blocks - 1, (0, hidden), (1, turn), (-1, outputs))
            hidden(pe, blocks - 1, (blocks - 1) % AHEAD, (blocks - 1) // AHEAD)
            for j in (blocks - 2, blocks - 1):
                outputs(pe, j, j % AHEAD, j // AHEAD)

        @block.scalar
        def _(act):
            steps(act, 0, blocks, (0, activate))

        @block.vector
        def _(dve):
            dve.sem_inc(y_d, Y0)
            copy_turned(dve, 0, 0, 0)
            copy_turned(dve, 1, 1, 0)
            steps(dve, 1, blocks - 1, (1, copy_turned), (-1, add_bias))
            for j in (blocks - 2, blocks - 1):
                add_bias(dve, j, j % AHEAD, j // AHEAD)


def linear(nc, c, X, XN, GATE, SLOT, BESTP, HOT, w, ys):
    with ExitStack() as ctx:
        def sb(name, shape, dt=F32):
            return ctx.enter_context(nc.sbuf_tensor(f"ln_{name}", shape, dt))

        sem = semaphores(ctx, nc, "ln", False)

        def ps(name, shape):
            return ctx.enter_context(nc.psum_tensor(f"ln_{name}", shape, F32))

        wqkv, wo, wr = sb("wqkv", [P, 3 * D]), sb("wo", [P, D]), sb("wr", [P, E1])
        slot = [sb(f"slot{i}", [P, G * 2], I32) for i in range(2)]
        rows = [sb(f"rows{i}", [P, G * 2, D]) for i in range(2)]
        moe = sb("moe", [P, G, D])
        stats, mv, rstd, xn, xT = ({k: sb(f"{n}_{k}", shape) for k in "ac"} for n, shape in (
            ("stats", [P, G, 6]), ("mv", [P, G, 2]), ("rstd", [P, G]), ("xn", [P, G, D]), ("xT", [P, GT])))
        qk = [sb(f"qk{i}", [P, 2 * D]) for i in range(2)]
        v1 = [sb(f"v1_{i}", [P, D + 1]) for i in range(2)]
        qT = [sb(f"qT{i}", [P, P]) for i in range(2)]
        kv = [sb(f"kv{i}", [P, KV1 + D]) for i in range(2)]
        state = sb("state", [P, D + H1])
        own_head = sb("own_head", [P, D + H1])
        prod = sb("prod", [P, KV1 + D])
        num, den = sb("num", [P, D]), sb("den", [P, H1])
        o, oT = sb("o", [P, G, D]), sb("oT", [P, GT])
        top, total = sb("top", [P, G]), sb("total", [P, G])
        prob, best, at = sb("prob", [P, G, E1]), sb("best", [P, G, 8]), sb("at", [P, G, 8], U32)
        atf = sb("atf", [P, G])
        p_T, p_qkv = ps("p_T", [P, 512]), ps("p_qkv", [P, 512])
        p_cum = ps("p_cum", [P, 3, 512])
        p_prev, p_st, p_y = ps("p_prev", [P, 512]), ps("p_st", [P, 512]), ps("p_y", [P, G, D])
        S = {n: sem(n) for n in (
            "w_in", "ones", "mask", "x_a", "x_c", "stats_a", "stats_c", "var_a", "var_c", "root_a", "root_c",
            "rstd_a", "rstd_c", "xn_a", "xn_c", "pxT_a", "pxT_c", "xT_a", "xT_c", "qkv", "qk", "v", "pqT", "qT",
            "kc", "kv", "st", "state", "cum", "prev", "prod", "o", "poT", "oT", "y", "kept", "logits", "shift",
            "exp", "passed", "moe", "chain", "slots", "gated", "combine", "top", "router", "kept_best")}
        rows_in = [sem(f"rows_in{i}") for i in range(2)]
        passed = S["passed"]
        block = ctx.enter_context(nc.Block())

        def after(g, n=1):
            return g[0] + (g[1] + n) // 2, (g[1] + n) % 2

        def number(g):
            return g[0] * 2 + g[1]

        def exists(g):
            return not isinstance(number(g), int) or 0 <= number(g) < GROUPS

        def from_first(eng, name, value):
            if not (isinstance(value, int) and value <= 0):
                eng.wait_ge(S[name], value)

        def next_tile(g, t, n=1):
            return after(g, (t + n) // G), (t + n) % G

        def tile_number(g, t):
            return number(g) * G + t

        def prevs(b, tb):
            return b * (KT - 1) + (tb if tb >= 0 else tb + 1)

        def groups(eng, iteration):
            for g in range(-2, 2):
                iteration((g // 2, g % 2))
            with eng.Fori(0, B - 2) as r:
                for i in range(2):
                    iteration((r + 1, i))
            for g in range(GROUPS - 2, GROUPS + 2):
                iteration((g // 2, g % 2))

        def group_of(T_, g, width=D):
            return T_[:, bass.ds(number(g) * G * width, G * width)].rearrange("p (t d) -> p t d", t=G)

        @block.sync
        def _(sp):
            for dst, src in ((wqkv, w["WqkvT"]), (wo, w["Wo1T"]), (wr, w["routerT"])):
                sp.dma_start(dst[:, :], src).then_inc(S["w_in"], 16)
            sp.wait_ge(S["w_in"], 48)

        @block.gpsimd
        def _(pool):
            def masked(out, keys, reps):
                nc.gpsimd.memset(out, 1.0).then_inc(S["mask"], 1)
                pool.wait_ge(S["mask"], keys + 1)
                nc.gpsimd.affine_select(out=out, in_=out, compare_op=ALU.is_ge, fill=0.0, base=0,
                                        pattern=[[-DH1, H1], [0, reps]], channel_multiplier=1).then_inc(S["mask"], 1)
                pool.wait_ge(S["mask"], keys + 2)
                nc.gpsimd.affine_select(out=out, in_=out, compare_op=ALU.is_ge, fill=0.0, base=DH1 - 1,
                                        pattern=[[DH1, H1], [0, reps]], channel_multiplier=-1).then_inc(S["mask"], 1)

            masked(own_head[:, 0:D].rearrange("p (h m) -> p h m", h=H1), 0, DH1)
            masked(own_head[:, D:D + H1].rearrange("p (h m) -> p h m", h=H1), 3, 1)
            for i in range(2):
                nc.gpsimd.memset(v1[i][:, D:D + 1], 1.0).then_inc(S["ones"], 1)

            def take_slots(g):
                n, i = number(g), g[1]
                nc.gpsimd.tensor_copy(slot[i][:, :], SLOT[:, bass.ds(n * G * 2, G * 2)]).then_inc(S["slots"], 1)
                apart(pool, S["slots"], n + 1, passed)
                if not (isinstance(n, int) and n < 2):
                    apart(pool, S["moe"], n - 1, passed)

            def gather(g, t):
                i = g[1]
                for n in ((0, 1, 2), (3, 4, 5), (6, 7), ())[t]:
                    pool.indirect_dma_start(rows[i][:, n, :], None, ys[:, :],
                                            bass.IndirectOffsetOnAxis(ap=slot[i][:, n:n + 1], axis=0)).then_inc(rows_in[i], 16)

            def gate(g):
                b, i = g
                n = number(g)
                two = rows[i][:, :, :].rearrange("p (t k) d -> p t k d", k=2)
                apart(pool, rows_in[i], (b + 1) * G * 2 * 16, passed)
                nc.gpsimd.tensor_tensor(rows[i][:, :, :], rows[i][:, :, :],
                                        GATE[:, bass.ds(number(g) * G * 2, G * 2)].unsqueeze(2).broadcast_to([P, G * 2, D]),
                                        ALU.mult).then_inc(S["gated"], 1)
                pool.wait_ge(S["gated"], 2 * n + 1)
                nc.gpsimd.tensor_tensor(two[:, :, 0, :], two[:, :, 0, :], two[:, :, 1, :], ALU.add).then_inc(S["gated"], 1)
                if not (isinstance(n, int) and n == 0):
                    apart(pool, S["x_a"], n, passed)
                apart(pool, S["gated"], 2 * n + 2, passed)
                nc.gpsimd.tensor_tensor(moe[:, :, :], two[:, :, 0, :], group_of(XN, g), ALU.add).then_inc(S["moe"], 1)

            def outer(g, t):
                n = tile_number(g, t)
                pool.wait_ge(S["v"], n + 1)
                from_first(pool, "cum", n - 1)
                shape = [P, H1, DH1, DH1]
                k = qk[t % 2][:, D:2 * D].rearrange("p (h d) -> p h d", h=H1)
                v = v1[t % 2][:, 0:D].rearrange("p (h m) -> p h m", h=H1)
                nc.gpsimd.tensor_tensor(kv[t % 2][:, 0:KV1].rearrange("p (h d m) -> p h d m", h=H1, d=DH1),
                                        k.unsqueeze(3).broadcast_to(shape), v.unsqueeze(2).broadcast_to(shape),
                                        ALU.mult).then_inc(S["kv"], 1)

            def iteration(g):
                for t in range(G):
                    nxt = next_tile(g, t)
                    if exists(nxt[0]):
                        outer(*nxt)
                    if exists(after(g, 2)):
                        if t == 0:
                            take_slots(after(g, 2))
                        gather(after(g, 2), t)
                        if t == 3:
                            gate(after(g, 2))

            groups(pool, iteration)

        @block.tensor
        def _(pe):
            def turned(src, done):
                for t in range(G):
                    mm = nc.tensor.transpose(p_T[:, t * P:(t + 1) * P], src[:, t, :], c["ident"][:, :])
                mm.then_inc(done, 1)

            def project_tile(g, t):
                n = tile_number(g, t)
                if t == 0:
                    pe.wait_ge(S["xT_a"], number(g) + 1)
                from_first(pe, "v", n)
                nc.tensor.matmul(p_qkv[:, 0:3 * D], xT["a"][:, t * P:(t + 1) * P], wqkv[:, :], start=True,
                                 stop=True).then_inc(S["qkv"], 1)

            def add_state(g, t):
                n, tb = tile_number(g, t), g[1] * G + t
                pe.wait_ge(S["v"], n + 1)
                from_first(pe, "state", 2 * n)
                nc.tensor.matmul(p_st[:, 0:D + 1], qk[t % 2][:, D:2 * D], v1[t % 2][:, :], start=(tb == 0),
                                 stop=(tb == KT - 1), skip_group_check=True).then_inc(S["st"], 1)

            def turn_q(g, t):
                n = tile_number(g, t)
                from_first(pe, "qT", n)
                nc.tensor.transpose(p_T[:, 0:P], qk[t % 2][:, 0:D], c["ident"][:, :]).then_inc(S["pqT"], 1)

            def sums(g, t):
                n = tile_number(g, t)
                pe.wait_ge(S["kv"], n + 1)
                pe.wait_ge(S["kc"], n + 1)
                from_first(pe, "prod", 2 * n)
                for a in range(3):
                    z = min(512, KV1 + D - a * 512)
                    mm = nc.tensor.matmul(p_cum[:, a, 0:z], c["tri"][:, :], kv[t % 2][:, a * 512:a * 512 + z],
                                          start=True, stop=True)
                mm.then_inc(S["cum"], 1)

            def earlier(g, t):
                n = tile_number(g, t)
                if g[1] * G + t == 0:
                    return
                pe.wait_ge(S["qT"], n + 1)
                pe.wait_ge(S["state"], 2 * n)
                pe.wait_ge(S["o"], n)
                nc.tensor.matmul(p_prev[:, 0:D + H1], qT[t % 2][:, :], state[:, :], start=True,
                                 stop=True).then_inc(S["prev"], 1)

            def turn_output(g):
                n = number(g)
                pe.wait_ge(S["o"], n * G + G)
                pe.wait_ge(S["qT"], min(n * G + G + 1, NTOK // P) if isinstance(n, int) else n * G + G + 1)
                turned(o, S["poT"])

            def output_rows(g):
                n = number(g)
                pe.wait_ge(S["oT"], n + 1)
                from_first(pe, "shift", n)
                for t in range(G):
                    mm = nc.tensor.matmul(p_y[:, t, :], oT[:, t * P:(t + 1) * P], wo[:, :], start=True, stop=True)
                mm.then_inc(S["y"], 1)

            def turn_first(g):
                n = number(g)
                from_first(pe, "qT", n * G - 1)
                pe.wait_ge(S["xn_a"], n + 1)
                turned(xn["a"], S["pxT_a"])

            def turn_second(g):
                n = number(g)
                tiles = (n + 2) * G
                pe.wait_ge(S["qT"], min(tiles, NTOK // P) if isinstance(n, int) else tiles)
                pe.wait_ge(S["xn_c"], n + 1)
                turned(xn["c"], S["pxT_c"])

            def router(g):
                n = number(g)
                pe.wait_ge(S["xT_c"], n + 1)
                for t in range(G):
                    mm = nc.tensor.matmul(p_y[:, 0, t * E1:(t + 1) * E1], xT["c"][:, t * P:(t + 1) * P], wr[:, :], start=True, stop=True)
                mm.then_inc(S["logits"], 1)

            def iteration(g):
                before = after(g, -1)
                for t in range(G):
                    nxt, second = next_tile(g, t), next_tile(g, t, 2)
                    if t == 0 and exists(before):
                        turn_output(before)
                    if t == 3 and exists(before):
                        turn_second(before)
                    if exists(nxt[0]):
                        add_state(*nxt)
                    if t != 2 and exists(second[0]):
                        project_tile(*second)
                    if t == 2 and exists(after(g)):
                        turn_first(after(g))
                        project_tile(*second)
                    if t == 0 and exists(before):
                        output_rows(before)
                    if t == 3 and exists(before):
                        router(before)
                    if exists(nxt[0]):
                        turn_q(*nxt)
                        sums(*nxt)
                        earlier(*nxt)

            pe.wait_ge(S["w_in"], 48)
            pe.wait_ge(S["ones"], 2)
            groups(pe, iteration)

        @block.scalar
        def _(act):
            def root(g, k):
                act.wait_ge(S[f"var_{k}"], number(g) + 1)
                nc.scalar.activation(rstd[k][:, :], rstd[k][:, :], ACT.Sqrt).then_inc(S[f"root_{k}"], 1)

            def keep_turned(g, k):
                n = number(g)
                act.wait_ge(S[f"pxT_{k}"], n + 1)
                from_first(act, *(("qkv", n * G) if k == "a" else ("logits", n)))
                nc.scalar.copy(xT[k][:, :], p_T[:, :]).then_inc(S[f"xT_{k}"], 1)

            def keep_rows(g):
                nc.scalar.copy(group_of(XN, g), xn["c"][:, :, :]).then_inc(S["kept"], 1)

            def keep_output(g):
                n = number(g)
                act.wait_ge(S["poT"], n + 1)
                from_first(act, "y", n)
                nc.scalar.copy(oT[:, :], p_T[:, :]).then_inc(S["oT"], 1)

            def keep_tile(g, t):
                n, tb = tile_number(g, t), g[1] * G + t
                act.wait_ge(S["v"], n + 1)
                from_first(act, "cum", n - 1)
                nc.scalar.copy(kv[t % 2][:, KV1:KV1 + D], qk[t % 2][:, D:2 * D]).then_inc(S["kc"], 1)
                act.wait_ge(S["pqT"], n + 1)
                from_first(act, "prev", prevs(g[0], tb - 2))
                nc.scalar.copy(qT[t % 2][:, :], p_T[:, 0:P]).then_inc(S["qT"], 1)

            def exps(g):
                act.wait_ge(S["shift"], number(g) + 1)
                nc.scalar.activation(prob[:, :, :], prob[:, :, :], ACT.Exp).then_inc(S["exp"], 1)

            def iteration(g):
                before = after(g, -1)
                for t in range(G):
                    if t == 0 and exists(after(g, -2)):
                        exps(after(g, -2))
                    if t == 0 and exists(before):
                        keep_output(before)
                    if t == 1 and exists(after(g)):
                        root(after(g), "a")
                    if t == 2 and exists(before):
                        root(before, "c")
                    if t == 3 and exists(before):
                        keep_turned(before, "c")
                        keep_rows(before)
                    if t == 2 and exists(after(g)):
                        keep_turned(after(g), "a")
                    if exists(next_tile(g, t)[0]):
                        keep_tile(*next_tile(g, t))

            groups(act, iteration)

        @block.vector
        def _(dve):
            def chain(name, base):
                n = [0]

                def step(ins):
                    n[0] += 1
                    ins.then_inc(S[name], 1)
                    dve.wait_ge(S[name], base + n[0])
                return step

            def combine(g):
                n = number(g)
                step = chain("combine", n)
                dve.wait_ge(S["moe"], n + 1)
                step(nc.vector.tensor_scalar(moe[:, :, :], moe[:, :, :], 100.0, -100.0, ALU.min, ALU.max))
                nc.vector.tensor_tensor(group_of(X, g), group_of(X, g), moe[:, :, :], ALU.add).then_inc(S["x_a"], 1)

            def moments(g, k):
                n = number(g)
                apart(dve, S[f"x_{k}"], n + 1, passed)
                for t in range(G):
                    last = nc.vector.bn_stats(stats[k][:, t, :], group_of(X, g)[:, t, :])
                last.then_inc(S[f"stats_{k}"], 1)
                apart(dve, S[f"stats_{k}"], 2 * n + 1, passed)
                for t in range(G):
                    last = nc.vector.bn_aggr(mv[k][:, t, :], stats[k][:, t, :])
                last.then_inc(S[f"stats_{k}"], 1)
                dve.wait_ge(S[f"stats_{k}"], 2 * n + 2)
                nc.vector.tensor_scalar(rstd[k][:, :], mv[k][:, :, 1], LN_EPS, None, ALU.add).then_inc(S[f"var_{k}"], 1)

            def normalise(g, k):
                n = number(g)
                dve.wait_ge(S[f"root_{k}"], n + 1)
                nc.vector.reciprocal(rstd[k][:, :], rstd[k][:, :]).then_inc(S[f"rstd_{k}"], 1)
                dve.wait_ge(S[f"rstd_{k}"], n + 1)
                from_first(dve, f"pxT_{k}", n)
                if k == "c" and not (isinstance(n, int) and n == 0):
                    apart(dve, S["kept"], n, passed)
                for t in range(G):
                    last = nc.vector.tensor_scalar(xn[k][:, t, :], group_of(X, g)[:, t, :], mv[k][:, t, 0:1],
                                                   rstd[k][:, t:t + 1], ALU.subtract, ALU.mult)
                last.then_inc(S[f"xn_{k}"], 1)

            def features(g, t):
                n, s = tile_number(g, t), t % 2
                dve.wait_ge(S["qkv"], n + 1)
                from_first(dve, "cum", n - 1)
                nc.vector.tensor_scalar(qk[s][:, :], p_qkv[:, 0:2 * D], 0.0, FEAT_EPS, ALU.max, ALU.add).then_inc(S["qk"], 1)
                nc.vector.tensor_copy(v1[s][:, 0:D], p_qkv[:, 2 * D:3 * D]).then_inc(S["v"], 1)

            def attend_tile(g, t):
                n, tb, s = tile_number(g, t), g[1] * G + t, t % 2
                link = chain("chain", n * 3)
                dve.wait_ge(S["st"], n + 1)
                from_first(dve, "prev", prevs(g[0], tb))
                nc.vector.tensor_tensor(state[:, 0:D], p_st[:, 0:D], own_head[:, 0:D], ALU.mult).then_inc(S["state"], 1)
                nc.vector.tensor_scalar(state[:, D:D + H1], own_head[:, D:D + H1], p_st[:, D:D + 1], None, ALU.mult).then_inc(S["state"], 1)
                q = qk[s][:, 0:D].rearrange("p (h d) -> p h d", h=H1)
                dve.wait_ge(S["cum"], n + 1)
                from_first(dve, "o", n)
                for a in range(2):
                    hs = slice(a * H1 // 2, (a + 1) * H1 // 2)
                    last = nc.vector.tensor_tensor(prod[:, a * 512:(a + 1) * 512].rearrange("p (h d m) -> p h d m", d=DH1, m=DH1),
                                                   p_cum[:, a, :].rearrange("p (h d m) -> p h d m", d=DH1, m=DH1),
                                                   q[:, hs, :].unsqueeze(3).broadcast_to([P, H1 // 2, DH1, DH1]), ALU.mult)
                last.then_inc(S["prod"], 1)
                nc.vector.tensor_tensor(prod[:, KV1:KV1 + D], p_cum[:, 2, 0:D], qk[s][:, 0:D], ALU.mult).then_inc(S["prod"], 1)
                dve.wait_ge(S["prod"], 2 * n + 2)
                nc.vector.tensor_reduce(num[:, :].rearrange("p (h m) -> p h m", h=H1),
                                        prod[:, 0:KV1].rearrange("p (h d m) -> p h m d", h=H1, d=DH1), AX.X, ALU.add)
                link(nc.vector.tensor_reduce(den[:, :], prod[:, KV1:KV1 + D].rearrange("p (h d) -> p h d", h=H1), AX.X, ALU.add))
                if tb > 0:
                    dve.wait_ge(S["prev"], prevs(g[0], tb))
                    nc.vector.tensor_tensor(num[:, :], num[:, :], p_prev[:, 0:D], ALU.add)
                    link(nc.vector.scalar_tensor_tensor(out=den[:, :], in0=den[:, :], scalar=FEAT_EPS,
                                                        in1=p_prev[:, D:D + H1], op0=ALU.add, op1=ALU.add))
                else:
                    link(nc.vector.tensor_scalar(den[:, :], den[:, :], FEAT_EPS, None, ALU.add))
                link(nc.vector.reciprocal(den[:, :], den[:, :]))
                if t == 0:
                    from_first(dve, "poT", number(g))
                nc.vector.tensor_tensor(o[:, t, :].rearrange("p (h m) -> p h m", h=H1), num[:, :].rearrange("p (h m) -> p h m", h=H1),
                                        den[:, :].unsqueeze(2).broadcast_to([P, H1, DH1]), ALU.mult).then_inc(S["o"], 1)

            def add_output(g):
                dve.wait_ge(S["y"], number(g) + 1)
                nc.vector.tensor_tensor(group_of(X, g), group_of(X, g), p_y[:, :, :], ALU.add).then_inc(S["x_c"], 1)

            wide = [P, G, E1]

            def shift_logits(g):
                n = number(g)
                logits = p_y[:, 0, 0:G * E1].rearrange("p (t e) -> p t e", e=E1)
                dve.wait_ge(S["logits"], n + 1)
                nc.vector.tensor_reduce(top[:, :], logits, AX.X, ALU.max).then_inc(S["top"], 1)
                dve.wait_ge(S["top"], n + 1)
                nc.vector.tensor_tensor(prob[:, :, :], logits, top[:, :].unsqueeze(2).broadcast_to(wide), ALU.subtract).then_inc(S["shift"], 1)

            def choose(g):
                n = number(g)
                step = chain("router", n * 7)
                dve.wait_ge(S["exp"], n + 1)
                step(nc.vector.tensor_reduce(total[:, :], prob[:, :, :], AX.X, ALU.add))
                step(nc.vector.reciprocal(total[:, :], total[:, :]))
                step(nc.vector.tensor_tensor(prob[:, :, :], prob[:, :, :], total[:, :].unsqueeze(2).broadcast_to(wide), ALU.mult))
                dve.sem_inc(passed, 1)
                for t in range(G):
                    last = nc.vector.max(best[:, t, :], prob[:, t, :])
                step(last)
                dve.sem_inc(passed, 1)
                for t in range(G):
                    last = nc.vector.max_index(at[:, t, :], best[:, t, :], prob[:, t, :])
                step(last)
                step(nc.vector.tensor_copy(atf[:, :], at[:, :, 0]))
                nc.vector.tensor_copy(BESTP[:, bass.ds(n * G, G)], best[:, :, 0])
                step(nc.vector.tensor_tensor(HOT[:, :, bass.ds(n * G, G)].rearrange("p e t -> p t e"),
                                             c["iota"][:, 0:E1].unsqueeze(1).broadcast_to(wide),
                                             atf[:, :].unsqueeze(2).broadcast_to(wide), ALU.is_equal))

            def iteration(g):
                before = after(g, -1)
                for t in range(G):
                    if exists(next_tile(g, t)[0]):
                        features(*next_tile(g, t))
                    if exists(g):
                        attend_tile(g, t)
                    if t == 0 and exists(after(g)):
                        combine(after(g))
                        moments(after(g), "a")
                    if t == 0 and exists(after(g, -2)):
                        choose(after(g, -2))
                    if t == 1 and exists(after(g)):
                        normalise(after(g), "a")
                    if t == 1 and exists(before):
                        add_output(before)
                        moments(before, "c")
                    if t == 2 and exists(before):
                        normalise(before, "c")
                    if t == 3 and exists(before):
                        shift_logits(before)

            dve.wait_ge(S["mask"], 6)
            groups(dve, iteration)


BITS = 27


def capacity(nc, c, XN, BESTP, HOT, SLOT, tabs, xs):
    with ExitStack() as ctx:
        def sb(name, shape, dt=F32):
            return ctx.enter_context(nc.sbuf_tensor(f"cp_{name}", shape, dt))

        sem = semaphores(ctx, nc, "cp", True)

        ET = [P, E1, TILES]
        p_of, cmp, equal, keep, place, tiles_before = (sb(n, ET) for n in ("p_of", "cmp", "equal", "keep", "place", "before"))
        count, level, trial, bit, rise, room, start, zero = (sb(n, [P, E1]) for n in
                                                             ("count", "level", "trial", "bit", "rise", "room", "start", "zero"))
        none = sb("none", [P, TILES])
        slotf, scatter_slot = sb("slotf", [P, TILES]), sb("scatter_slot", [P, TILES], I32)
        xn = [sb(f"xn{i}", [P, G, D]) for i in range(2)]
        slot = [sb(f"slot{i}", [P, G], I32) for i in range(2)]
        zeros = sb("zeros", [P, BT // P, D])
        p_count = ctx.enter_context(nc.psum_tensor("cp_p_count", [P, 512], F32))
        p_rank = ctx.enter_context(nc.psum_tensor("cp_p_rank", [P, E1, TILES], F32))
        p_tiles = ctx.enter_context(nc.psum_tensor("cp_p_tiles", [P, E1, TILES], F32))
        step_d, counted, total_d, loop_d, ranks, slots_d, copied, tails_out, passed = (
            sem(n) for n in ("step", "counted", "total", "loop", "ranks", "slots", "copied", "tails_out", "passed"))
        rows_out = [sem(f"rows_out{i}") for i in range(2)]
        block = ctx.enter_context(nc.Block())
        wide = lambda a: a.unsqueeze(2).broadcast_to(ET)

        @block.tensor
        def _(pe):
            with pe.Fori(0, BITS) as k:
                pe.wait_ge(counted, k + 1)
                nc.tensor.matmul(p_count[:, 0:E1], c["ones"][:, :], count[:, :], start=True, stop=True).then_inc(total_d, 1)
            pe.wait_ge(counted, BITS + 1)
            nc.tensor.matmul(p_count[:, 0:E1], c["ones"][:, :], count[:, :], start=True, stop=True).then_inc(total_d, 1)
            for n, src in enumerate((equal, keep)):
                pe.wait_ge(counted, BITS + 2 + n)
                nc.tensor.matmul(p_rank[:, :, :], c["stri"][:, :], src[:, :, :], start=True, stop=True)
                nc.tensor.matmul(p_tiles[:, :, :], c["ones"][:, :], src[:, :, :], start=True, stop=True).then_inc(ranks, 1)

        @block.vector
        def _(dve):
            n = [0]

            def step(ins):
                n[0] += 1
                ins.then_inc(step_d, 1)
                dve.wait_ge(step_d, n[0])

            step(nc.vector.memset(zeros[:, :, :], 0.0))
            step(nc.vector.memset(zero[:, :], 0.0))
            step(nc.vector.memset(none[:, :], 0.0))
            step(nc.vector.tensor_scalar(start[:, :], c["iota"][:, 0:E1], float(REGION), None, ALU.mult))
            step(nc.vector.tensor_tensor(p_of[:, :, :], HOT[:, :, :], BESTP[:, :].unsqueeze(1).broadcast_to(ET), ALU.mult))
            step(nc.vector.tensor_tensor(p_of[:, :, :], p_of[:, :, :], HOT[:, :, :], ALU.add))
            step(nc.vector.tensor_scalar(p_of[:, :, :], p_of[:, :, :], -1.0, None, ALU.add))
            step(nc.vector.memset(level[:, :], 0.0))
            step(nc.vector.memset(trial[:, :], 0.5))
            step(nc.vector.memset(bit[:, :], 0.5))
            with dve.Fori(0, BITS) as k:
                nc.vector.tensor_tensor(cmp[:, :, :], p_of[:, :, :], wide(trial[:, :]), ALU.is_ge).then_inc(loop_d, 1)
                dve.wait_ge(loop_d, k * 5 + 1)
                nc.vector.tensor_reduce(count[:, :], cmp[:, :, :], AX.X, ALU.add).then_inc(counted, 1)
                dve.wait_ge(total_d, k + 1)
                nc.vector.tensor_scalar(rise[:, :], p_count[:, 0:E1], float(CAP1), None, ALU.is_ge).then_inc(loop_d, 1)
                dve.wait_ge(loop_d, k * 5 + 2)
                nc.vector.tensor_tensor(rise[:, :], rise[:, :], bit[:, :], ALU.mult).then_inc(loop_d, 1)
                dve.wait_ge(loop_d, k * 5 + 3)
                nc.vector.tensor_tensor(level[:, :], level[:, :], rise[:, :], ALU.add)
                nc.vector.tensor_scalar(bit[:, :], bit[:, :], 0.5, None, ALU.mult).then_inc(loop_d, 1)
                dve.wait_ge(loop_d, k * 5 + 4)
                nc.vector.tensor_tensor(trial[:, :], level[:, :], bit[:, :], ALU.add).then_inc(loop_d, 1)
                dve.wait_ge(loop_d, k * 5 + 5)
            step(nc.vector.tensor_tensor(keep[:, :, :], p_of[:, :, :], wide(level[:, :]), ALU.is_gt))
            nc.vector.tensor_reduce(count[:, :], keep[:, :, :], AX.X, ALU.add).then_inc(counted, 1)
            dve.wait_ge(total_d, BITS + 1)
            step(nc.vector.tensor_scalar(room[:, :], p_count[:, 0:E1], -1.0, float(CAP1), ALU.mult, ALU.add))
            nc.vector.tensor_tensor(equal[:, :, :], p_of[:, :, :], wide(level[:, :]), ALU.is_equal).then_inc(counted, 1)

            def rank(k):
                dve.wait_ge(ranks, k)
                for e in range(E1):
                    last = nc.vector.tensor_tensor_scan(tiles_before[:, e, :], p_tiles[:, e, :], none[:, :], 0.0, ALU.add, ALU.add)
                step(last)
                step(nc.vector.tensor_copy(count[:, :], tiles_before[:, :, TILES - 1]))
                step(nc.vector.tensor_tensor(tiles_before[:, :, :], tiles_before[:, :, :], p_tiles[:, :, :], ALU.subtract))
                step(nc.vector.tensor_tensor(place[:, :, :], tiles_before[:, :, :], p_rank[:, :, :], ALU.add))

            rank(1)
            step(nc.vector.tensor_tensor(cmp[:, :, :], place[:, :, :], wide(room[:, :]), ALU.is_lt))
            step(nc.vector.tensor_tensor(cmp[:, :, :], cmp[:, :, :], equal[:, :, :], ALU.mult))
            step(nc.vector.tensor_tensor(keep[:, :, :], keep[:, :, :], cmp[:, :, :], ALU.add))
            step(nc.vector.tensor_reduce(slotf[:, :], keep[:, 1:E1, :].rearrange("p e t -> p t e"), AX.X, ALU.add))
            nc.vector.tensor_scalar(keep[:, 0, :], slotf[:, :], -1.0, 1.0, ALU.mult, ALU.add).then_inc(counted, 1)
            rank(2)
            step(nc.vector.tensor_tensor(place[:, :, :], place[:, :, :], wide(start[:, :]), ALU.add))
            step(nc.vector.tensor_tensor(place[:, :, :], place[:, :, :], keep[:, :, :], ALU.mult))
            step(nc.vector.tensor_reduce(slotf[:, :], place[:, :, :].rearrange("p e t -> p t e"), AX.X, ALU.add))
            step(nc.vector.tensor_copy(SLOT[:, 0:TILES], slotf[:, :]))
            nc.vector.tensor_copy(scatter_slot[:, :], slotf[:, :]).then_inc(slots_d, 1)
            block_table(nc, dve, c, count[:, :], E1, blocks_of(1, E1), tabs, SLOT[:, 0:TILES], slots_d, 1)

        @block.sync
        def _(sp):
            sp.wait_ge(slots_d, 1 + TABLE_STEPS)
            zero_tails(nc, sp, xs, zeros, tabs, E1, surplus_of(1, E1), tails_out)

        @block.gpsimd
        def _(pool):
            pool.wait_ge(slots_d, 1)
            with pool.Fori(0, GROUPS // 2) as r:
                for i in range(2):
                    g = r * 2 + i
                    apart(pool, rows_out[i], r * G * 16, passed)
                    nc.gpsimd.tensor_copy(slot[i][:, :], scatter_slot[:, bass.ds(g * G, G)]).then_inc(copied, 1)
                    nc.gpsimd.tensor_copy(xn[i][:, :, :], XN[:, bass.ds(g * GT, GT)].rearrange("p (t d) -> p t d", t=G)).then_inc(copied, 1)
                    apart(pool, copied, g * 2 + 2, passed)
                    for t in range(G):
                        pool.indirect_dma_start(xs[:, :], bass.IndirectOffsetOnAxis(ap=slot[i][:, t:t + 1], axis=0),
                                                xn[i][:, t, :], None).then_inc(rows_out[i], 16)
            for i in range(2):
                pool.wait_ge(rows_out[i], GROUPS // 2 * G * 16)


def finish(nc, X, SLOT, ys, out):
    with ExitStack() as ctx:
        slot = [ctx.enter_context(nc.sbuf_tensor(f"fi_slot{i}", [P, G], I32)) for i in range(2)]
        rows = [ctx.enter_context(nc.sbuf_tensor(f"fi_rows{i}", [P, G, D], F32)) for i in range(2)]
        sem = semaphores(ctx, nc, "fi", True)
        rows_in = [sem(f"rows_in{i}") for i in range(2)]
        slots_d, sum_d, out_d, passed = (sem(n) for n in ("slots", "sum", "out", "passed"))
        block = ctx.enter_context(nc.Block())
        out_v = out.rearrange("b t d -> (b t) d").rearrange("(g t p) d -> p g t d", p=P, t=G)

        @block.gpsimd
        def _(pool):
            with pool.Fori(0, GROUPS // 2) as r:
                for i in range(2):
                    g = r * 2 + i
                    apart(pool, sum_d, 1 + g - 1, passed)
                    nc.gpsimd.tensor_copy(slot[i][:, :], SLOT[:, bass.ds(g * G, G)]).then_inc(slots_d, 1)
                    apart(pool, slots_d, g + 1, passed)
                    for t in range(G):
                        pool.indirect_dma_start(rows[i][:, t, :], None, ys[:, :],
                                                bass.IndirectOffsetOnAxis(ap=slot[i][:, t:t + 1], axis=0)).then_inc(rows_in[i], 16)

        @block.vector
        def _(dve):
            dve.sem_inc(sum_d, 1)
            with dve.Fori(0, GROUPS // 2) as r:
                for i in range(2):
                    g = r * 2 + i
                    Xg = X[:, bass.ds(g * GT, GT)].rearrange("p (t d) -> p t d", t=G)
                    dve.wait_ge(rows_in[i], (r + 1) * G * 16)
                    nc.vector.tensor_tensor(Xg, Xg, rows[i][:, :, :], ALU.add).then_inc(sum_d, 1)

        @block.sync
        def _(sp):
            with sp.Fori(0, GROUPS) as g:
                apart(sp, sum_d, 1 + g + 1, passed)
                sp.dma_start(out_v[:, bass.ds(g, 1)].rearrange("p o t d -> p (o t) d"),
                             X[:, bass.ds(g * GT, GT)].rearrange("p (t d) -> p t d", t=G)).then_inc(out_d, 16)
            sp.wait_ge(out_d, GROUPS * 16)


def program(nc, a, out, upto=99):
    with ExitStack() as ctx:
        def sb(n, shape, dt=F32):
            return ctx.enter_context(nc.sbuf_tensor(n, shape, dt))

        def dram(n, shape, dt=F32):
            return nc.dram_tensor(n, shape, dt, kind="Internal").ap()

        c = {n: sb(f"c_{n}", [P, P]) for n in ("ident", "tri", "stri", "ones", "iota")}
        X, XN = sb("X", [P, TILES * D]), sb("XN", [P, TILES * D])
        GATE, SLOT = sb("GATE", [P, TILES * 2]), sb("SLOT", [P, TILES * 2], I32)
        q3, k3 = dram("q3", [3, UNITS, DH0, T], BF16), dram("k3", [3, UNITS, DH0, T], BF16)
        v0, o0 = dram("v0", [UNITS, P, KT * DH0]), dram("o0", [UNITS, DH0, T])
        xs0, ys0 = dram("xs0", [E0 * REGION + surplus_of(2, E0) * BT, D]), dram("ys0", [blocks_of(2, E0) * BT, D])
        NB0 = blocks_of(2, E0)
        xs1, ys1 = dram("xs1", [E1 * REGION + surplus_of(1, E1) * BT, D]), dram("ys1", [blocks_of(1, E1) * BT, D])
        NB1 = blocks_of(1, E1)
        BESTP, HOT = sb("BESTP", [P, TILES]), sb("HOT", [P, E1, TILES])
        tabs1 = tables(ctx, nc, "t1", 1, E1)
        tabs0 = tables(ctx, nc, "t0", 2, E0)
        constants(nc, c)
        project(nc, c, X, a["x"], a, q3, k3, v0)
        if upto >= 2:
            attend(nc, c, q3, k3, v0, o0)
        if upto >= 3:
            route2(nc, c, X, XN, GATE, SLOT, tabs0, a, o0, xs0)
        if upto >= 4:
            experts(nc, c, "e0", True, E0, F0, ACT.Gelu, tabs0, NB0, surplus_of(2, E0), a["weights0"], a["b2"], xs0, ys0)
        if upto >= 5:
            linear(nc, c, X, XN, GATE, SLOT, BESTP, HOT, a, ys0)
        if upto >= 6:
            capacity(nc, c, XN, BESTP, HOT, SLOT, tabs1, xs1)
        if upto >= 7:
            experts(nc, c, "e1", False, E1, F1, ACT.Relu, tabs1, NB1, surplus_of(1, E1), a["weights1"], a["B2"], xs1, ys1)
        if upto >= 8:
            finish(nc, X, SLOT, ys1, out)


def layout(d):
    import numpy as np
    t = lambda a: np.ascontiguousarray(np.swapaxes(a, -1, -2))

    def expert_rows(w1, b1, w2):
        E = w1.shape[0]
        return np.concatenate([w1, b1.reshape(E, -1, P).transpose(0, 2, 1),
                               w2.reshape(E, -1, P, D).transpose(0, 2, 1, 3).reshape(E, P, -1)], axis=2)

    return {"x": d["L0_attn_x"], "WqT": t(d["L0_attn_Wq"]), "WdT": t(d["L0_attn_Wkv_down"]),
            "WkuT": t(d["L0_attn_Wk_up"]), "WvuT": t(d["L0_attn_Wv_up"]), "WoT": t(d["L0_attn_Wo"]),
            "gateT": t(d["L0_ffn_gate_w"]), "b2": d["L0_ffn_b2"],
            "weights0": expert_rows(d["L0_ffn_w1"], d["L0_ffn_b1"], d["L0_ffn_w2"]),
            "WqkvT": np.concatenate([t(d["L1_attn_Wq"]), t(d["L1_attn_Wk"]), t(d["L1_attn_Wv"])], axis=1),
            "Wo1T": t(d["L1_attn_Wo"]), "routerT": t(d["L1_ffn_router_w"]), "B2": d["L1_ffn_b2"],
            "weights1": expert_rows(d["L1_ffn_W1"], d["L1_ffn_b1"], d["L1_ffn_W2"])}


def kernel(**inputs):
    import numpy as np
    import concourse.bacc as bacc
    from concourse.bass_utils import run_bass_kernel_spmd

    arrays = {k: np.ascontiguousarray(v) for k, v in layout({k: np.asarray(v) for k, v in inputs.items()}).items()}
    nc = bacc.Bacc("TRN2", target_bir_lowering=False, num_devices=1)
    a = {k: nc.dram_tensor(f"in_{k}", v.shape, mybir.dt.from_np(v.dtype), kind="ExternalInput").ap()
         for k, v in arrays.items()}
    out = nc.dram_tensor("out_0", (B, T, D), F32, kind="ExternalOutput").ap()
    program(nc, a, out)
    r = run_bass_kernel_spmd(nc, [{f"in_{k}": v for k, v in arrays.items()}], core_ids=[0])
    return r.results[0]["out_0"]
```

```python
from contextlib import ExitStack

import concourse.bass as bass
from concourse import mybir

F32 = mybir.dt.float32
BF16 = mybir.dt.bfloat16
I32 = mybir.dt.int32
U32 = mybir.dt.uint32
ALU = mybir.AluOpType
ACT = mybir.ActivationFunctionType
AX = mybir.AxisListType

P = 128
B, T, D = 8, 1024, 128
NTOK = B * T
TILES = NTOK // P
G = 4
GT = G * P
GROUPS = TILES // G
H0, DH0, LR = 8, 32, 64
HW0 = H0 * DH0
UNITS = B * H0
KT = T // P
HALF = 512
SCALE = float(DH0) ** -0.5
H1, DH1 = 16, 8
KV1 = H1 * DH1 * DH1
E0, F0 = 14, 256
E1, F1 = 8, 512
BT = 256
REGION = NTOK + BT
LN_EPS = 1e-5
FEAT_EPS = 1e-6
CAP1 = -(-NTOK // E1 * 5 // 4)
assert CAP1 == 1280


def surplus_of(choices, experts):
    return blocks_of(choices, experts) - choices * NTOK // BT


def blocks_of(choices, experts):
    n = choices * NTOK // BT + experts - 1
    return n + n % 2


def apart(eng, sem, value, passed):
    eng.wait_ge(sem, value)
    eng.sem_inc(passed, 1)


def semaphores(ctx, nc, prefix, odd):
    free = sorted(nc.free_semaphores)
    ids = iter(free[len(free) // 2:] if odd else free[:len(free) // 2])
    held = []

    def sem(name):
        held.append(nc.alloc_semaphore(f"{prefix}_{name}", num=next(ids)))
        return held[-1]

    ctx.callback(lambda: nc.clear_and_free_semaphores(held))
    return sem


def constants(nc, c):
    with ExitStack() as ctx:
        sem = semaphores(ctx, nc, "c", True)
        fill, done = sem("fill"), sem("done")
        block = ctx.enter_context(nc.Block())

        @block.gpsimd
        def _(pool):
            nc.gpsimd.memset(c["ident"][:, :], 0.0).then_inc(fill, 1)
            nc.gpsimd.memset(c["tri"][:, :], 1.0).then_inc(fill, 1)
            nc.gpsimd.memset(c["stri"][:, :], 1.0).then_inc(fill, 1)
            nc.gpsimd.memset(c["ones"][:, :], 1.0).then_inc(fill, 1)
            pool.wait_ge(fill, 4)
            nc.gpsimd.affine_select(out=c["ident"][:, :], in_=c["ident"][:, :], compare_op=ALU.not_equal,
                                    fill=1.0, base=0, pattern=[[-1, P]], channel_multiplier=1).then_inc(done, 1)
            nc.gpsimd.affine_select(out=c["tri"][:, :], in_=c["tri"][:, :], compare_op=ALU.is_ge,
                                    fill=0.0, base=0, pattern=[[1, P]], channel_multiplier=-1).then_inc(done, 1)
            nc.gpsimd.affine_select(out=c["stri"][:, :], in_=c["stri"][:, :], compare_op=ALU.is_gt,
                                    fill=0.0, base=0, pattern=[[1, P]], channel_multiplier=-1).then_inc(done, 1)
            nc.gpsimd.iota(c["iota"][:, :], pattern=[[1, 128]], base=0, channel_multiplier=0,
                           allow_small_or_imprecise_dtypes=True).then_inc(done, 1)
            pool.wait_ge(done, 4)


def project(nc, c, X, x_in, w, q3, k3, v0):
    with ExitStack() as ctx:
        def sb(name, shape, dt=F32):
            return ctx.enter_context(nc.sbuf_tensor(name, shape, dt))

        sem = semaphores(ctx, nc, "pj", False)

        wq, wd = sb("wq", [P, HW0]), sb("wd", [P, LR])
        wku, wvu = sb("wku", [LR, HW0]), sb("wvu", [LR, HW0])
        stats, mv, rstd = sb("pj_stats", [P, G, 6]), sb("pj_mv", [P, G, 2]), sb("pj_rstd", [P, G])
        xn = sb("pj_xn", [P, G, D])
        xT = sb("pj_xT", [P, GT])
        lat = sb("pj_lat", [LR, GT])
        hi, mid, lo = (sb(f"pj_{n}", [P, 4, GT], BF16) for n in ("hi", "mid", "lo"))
        rest = sb("pj_rest", [P, 4, GT])
        vs = sb("pj_v", [P, H0, KT, DH0])
        p_xT = ctx.enter_context(nc.psum_tensor("pj_pxT", [P, GT], F32))
        p_lat = ctx.enter_context(nc.psum_tensor("pj_plat", [P, GT], F32))
        p_qk = ctx.enter_context(nc.psum_tensor("pj_pqk", [P, 4, GT], F32))
        p_v = ctx.enter_context(nc.psum_tensor("pj_pv", [P, G, HW0], F32))
        (w_in, stats_d, var_d, root_d, rstd_d, xn_d, pxT_d, xT_d, plat_d, lat_d, pqk_d, hi_d,
         rest_d, mid_d, lo_d, pv_d, v_d, hi_out, mid_out, lo_out, v_out, passed) = (
            sem(n) for n in ("w_in", "stats", "var", "root", "rstd", "xn", "pxT", "xT",
                             "plat", "lat", "pqk", "hi_d", "rest_d", "mid_d", "lo_d", "pv",
                             "v_d", "hi_out", "mid_out", "lo_out", "v_out", "passed"))
        x_arrived = [sem(f"x_in{i}") for i in range(2)]
        block = ctx.enter_context(nc.Block())
        x_v = x_in.rearrange("b t d -> (b t) d").rearrange("(g t p) d -> p g t d", p=P, t=G)

        def after(g, n=1):
            return g[0] + (g[1] + n) // 2, (g[1] + n) % 2

        def number(g):
            return g[0] * 2 + g[1]

        def exists(g):
            return not isinstance(number(g), int) or 0 <= number(g) < GROUPS

        def from_first(eng, sem, value):
            if not (isinstance(value, int) and value <= 0):
                eng.wait_ge(sem, value)

        def groups(eng, iteration):
            for g in range(-2, 2):
                iteration((g // 2, g % 2))
            with eng.Fori(0, B - 3) as r:
                for i in range(2):
                    iteration((r + 1, i))
            for g in range(GROUPS - 4, GROUPS):
                iteration((g // 2, g % 2))

        def x_of(g):
            return X[:, bass.ds(number(g) * GT, GT)].rearrange("p (t d) -> p t d", t=G)

        @block.sync
        def _(sp):
            def load(g):
                sp.dma_start(x_of(g), x_v[:, bass.ds(number(g), 1)].rearrange("p o t d -> p (o t) d")).then_inc(x_arrived[g[1]], 16)

            def store(g, part, plane, ready, sent, s, dram):
                b, i = g
                apart(sp, ready, 2 * number(g) + s + 1, passed)
                for cc in range(2):
                    dst = dram[part, bass.ds(b * H0 + cc * 4, 4), :, i * GT:(i + 1) * GT]
                    sp.dma_start(dst.rearrange("h d t -> (h d) t"), plane[:, 2 * s + cc, :]).then_inc(sent, 16)

            def iteration(g):
                if exists(after(g, 4)):
                    apart(sp, var_d, number(g) + 3, passed)
                    load(after(g, 4))
                if exists(g):
                    for part, plane, ready, sent in ((0, hi, hi_d, hi_out), (1, mid, mid_d, mid_out), (2, lo, lo_d, lo_out)):
                        for s, dram in ((0, q3), (1, k3)):
                            store(g, part, plane, ready, sent, s, dram)
                    if g[1] == 1:
                        apart(sp, v_d, number(g) + 1, passed)
                        sp.dma_start(v0[bass.ds(g[0] * H0, H0)].rearrange("h p x -> p h x"),
                                     vs[:, :, :, :].rearrange("p h k d -> p h (k d)")).then_inc(v_out, 16)

            load((0, 0))
            for dst, src in ((wq, w["WqT"]), (wd, w["WdT"]), (wku, w["WkuT"]), (wvu, w["WvuT"])):
                sp.dma_start(dst[:, :], src).then_inc(w_in, 16)
            load((0, 1))
            groups(sp, iteration)
            sp.wait_ge(hi_out, GROUPS * 64)
            sp.wait_ge(mid_out, GROUPS * 64)
            sp.wait_ge(lo_out, GROUPS * 64)
            sp.wait_ge(v_out, B * 16)

        @block.tensor
        def _(pe):
            def turn(g):
                n = number(g)
                pe.wait_ge(xn_d, n + 1)
                from_first(pe, xT_d, n)
                for t in range(G):
                    mm = nc.tensor.transpose(p_xT[:, t * P:(t + 1) * P], xn[:, t, :], c["ident"][:, :])
                mm.then_inc(pxT_d, 1)

            def iteration(g):
                n = number(g)
                if exists(g):
                    pe.wait_ge(xT_d, n + 1)
                    from_first(pe, lat_d, n)
                    nc.tensor.matmul(p_lat[0:LR, :], wd[:, :], xT[:, :], start=True, stop=True).then_inc(plat_d, 1)
                    from_first(pe, rest_d, 2 * n - 1)
                    for cc in range(2):
                        mm = nc.tensor.matmul(p_qk[:, cc, :], wq[:, cc * P:(cc + 1) * P], xT[:, :], start=True, stop=True)
                    mm.then_inc(pqk_d, 1)
                    pe.wait_ge(lat_d, n + 1)
                    from_first(pe, rest_d, 2 * n)
                    for cc in range(2):
                        mm = nc.tensor.matmul(p_qk[:, 2 + cc, :], wku[:, cc * P:(cc + 1) * P], lat[:, :], start=True, stop=True)
                    mm.then_inc(pqk_d, 1)
                if exists(after(g)):
                    turn(after(g))
                if exists(g):
                    from_first(pe, v_d, n)
                    for t in range(G):
                        mm = nc.tensor.matmul(p_v[:, t, :], lat[:, t * P:(t + 1) * P], wvu[:, :], start=True, stop=True)
                    mm.then_inc(pv_d, 1)

            pe.wait_ge(w_in, 64)
            groups(pe, iteration)

        @block.scalar
        def _(act):
            def high(g, s):
                n = number(g)
                act.wait_ge(pqk_d, 2 * n + s + 1)
                from_first(act, hi_out, n * 64)
                nc.scalar.copy(hi[:, 2 * s:2 * s + 2, :], p_qk[:, 2 * s:2 * s + 2, :]).then_inc(hi_d, 1)

            def middle(g, s):
                n = number(g)
                act.wait_ge(rest_d, 2 * n + s + 1)
                from_first(act, mid_out, n * 64)
                nc.scalar.copy(mid[:, 2 * s:2 * s + 2, :], rest[:, 2 * s:2 * s + 2, :]).then_inc(mid_d, 1)

            def iteration(g):
                n = number(g)
                if exists(g):
                    act.wait_ge(plat_d, n + 1)
                    from_first(act, pv_d, n)
                    nc.scalar.copy(lat[:, :], p_lat[0:LR, :]).then_inc(lat_d, 1)
                    high(g, 0)
                if exists(after(g, 2)):
                    act.wait_ge(var_d, n + 3)
                    nc.scalar.activation(rstd[:, :], rstd[:, :], ACT.Sqrt).then_inc(root_d, 1)
                if exists(g):
                    high(g, 1)
                if exists(after(g)):
                    act.wait_ge(pxT_d, n + 2)
                    nc.scalar.copy(xT[:, :], p_xT[:, :]).then_inc(xT_d, 1)
                if exists(g):
                    middle(g, 0)
                    middle(g, 1)

            groups(act, iteration)

        @block.vector
        def _(dve):
            def moments(g):
                n = number(g)
                apart(dve, x_arrived[g[1]], (g[0] + 1) * 16, passed)
                for t in range(G):
                    last = nc.vector.bn_stats(stats[:, t, :], x_of(g)[:, t, :])
                last.then_inc(stats_d, 1)
                apart(dve, stats_d, 2 * n + 1, passed)
                for t in range(G):
                    last = nc.vector.bn_aggr(mv[:, t, :], stats[:, t, :])
                last.then_inc(stats_d, 1)
                dve.wait_ge(stats_d, 2 * n + 2)
                nc.vector.tensor_scalar(rstd[:, :], mv[:, :, 1], LN_EPS, None, ALU.add).then_inc(var_d, 1)

            def normalise(g):
                n = number(g)
                dve.wait_ge(root_d, n + 1)
                nc.vector.reciprocal(rstd[:, :], rstd[:, :]).then_inc(rstd_d, 1)
                from_first(dve, pxT_d, n)
                dve.wait_ge(rstd_d, n + 1)
                for t in range(G):
                    last = nc.vector.tensor_scalar(xn[:, t, :], x_of(g)[:, t, :], mv[:, t, 0:1], rstd[:, t:t + 1],
                                                   ALU.subtract, ALU.mult)
                last.then_inc(xn_d, 1)

            def remainder(g, s):
                n = number(g)
                dve.wait_ge(hi_d, 2 * n + s + 1)
                from_first(dve, lo_d, 2 * n + s - 1)
                cols = slice(2 * s, 2 * s + 2)
                nc.vector.tensor_tensor(rest[:, cols, :], p_qk[:, cols, :], hi[:, cols, :], ALU.subtract).then_inc(rest_d, 1)

            def iteration(g):
                n, (b, half) = number(g), g
                if exists(after(g)):
                    normalise(after(g))
                if exists(after(g, 2)):
                    moments(after(g, 2))
                if exists(g):
                    remainder(g, 0)
                    remainder(g, 1)
                    dve.wait_ge(pv_d, n + 1)
                    if half == 0:
                        from_first(dve, v_out, b * 16)
                    nc.vector.tensor_copy(vs[:, :, half * G:(half + 1) * G, :].rearrange("p h k d -> p k h d"),
                                          p_v[:, :, :].rearrange("p k (h d) -> p k h d", h=H0)).then_inc(v_d, 1)

            groups(dve, iteration)

        @block.gpsimd
        def _(pool):
            def iteration(g):
                n = number(g)
                if exists(g):
                    for s in range(2):
                        cols = slice(2 * s, 2 * s + 2)
                        pool.wait_ge(mid_d, 2 * n + s + 1)
                        from_first(pool, lo_out, n * 64)
                        nc.gpsimd.tensor_tensor(lo[:, cols, :], rest[:, cols, :], mid[:, cols, :], ALU.subtract).then_inc(lo_d, 1)

            groups(pool, iteration)


SLOTS = 4
MAX_PLAN = (0, 3, 0, 3, 3, 3, 3, 1)
POOL_SUMS = (1, 2, 4, 5, 6)


def attend(nc, c, q3, k3, v0, o0):
    with ExitStack() as ctx:
        def sb(name, shape, dt=F32):
            return ctx.enter_context(nc.sbuf_tensor(name, shape, dt))

        sem = semaphores(ctx, nc, "at", True)

        KB = 2 * DH0 + 2
        Q = T // 4
        qa = [sb(f"qa{s}", [P, T], BF16) for s in range(SLOTS)]
        ka = [sb(f"ka{s}", [P, T], BF16) for s in range(SLOTS)]
        qb = [sb(f"qb{s}", [KB, T], BF16) for s in range(SLOTS)]
        kb = [sb(f"kb{s}", [KB, T], BF16) for s in range(SLOTS)]
        v = [sb(f"vh{s}", [P, KT, DH0]) for s in range(SLOTS)]
        probs = [sb(f"probs{k}", [P, T]) for k in range(KT)]
        sum_p = [sb(f"sum_p{i}", [P, T]) for i in range(2)]
        sum_v = [sb(f"sum_v{i}", [P, T]) for i in range(2)]
        halfmax, rowmax = sb("halfmax", [P, 2, KT]), sb("rowmax", [P, KT])
        max_hi, max_lo = (sb(n, [KT, P], BF16) for n in ("max_hi", "max_lo"))
        inv = sb("inv", [P, Q])
        ot = [sb(f"ot{i}", [P, Q]) for i in range(2)]
        p_s = [ctx.enter_context(nc.psum_tensor(f"p_s{i}", [P, T], F32)) for i in range(2)]
        p_m = [ctx.enter_context(nc.psum_tensor(f"p_m{i}", [P, HALF], F32)) for i in range(2)]
        p_o = [ctx.enter_context(nc.psum_tensor(f"p_o{i}", [P, 2, Q], F32)) for i in range(2)]
        operands_in = [sem(f"operands_in{s}") for s in range(SLOTS)]
        o_out = [sem(f"o_out{i}") for i in range(2)]
        (ones_d, max_scores, max_read, max_row, max_T, max_parts, max_hi_d, max_in, scores,
         probs_d, pv_d, sum_p_d, sum_v_d, den_d, inv_d, o_d, passed) = (
            sem(f"{n}") for n in ("ones", "max_scores", "max_read", "max_row", "max_T",
                                     "max_parts", "max_hi_d", "max_in", "scores", "probs", "pv",
                                     "sum_p", "sum_v", "den", "inv", "o", "passed"))
        PV0, O0, DEN0, SP0, SV0, ONE = SLOTS * KT, 3, 3, len(POOL_SUMS) + 1, 2, 1
        LOADS, LAST = 9, UNITS // SLOTS - 1
        block = ctx.enter_context(nc.Block())

        def after(r, s, n=1):
            return (r, s + n) if s + n < SLOTS else (r + 1, s + n - SLOTS)

        def exists(r, s, n=0):
            r, s = after(r, s, n)
            return not isinstance(r, int) or r <= LAST

        def load(sp, r, s):
            u = r * SLOTS + s
            if not (isinstance(r, int) and r == 0):
                apart(sp, pv_d, PV0 + (u - SLOTS + 1) * KT, passed)

            def rows(dram, part):
                return dram[part, bass.ds(u, 1)].rearrange("o d t -> (o d) t")

            def parts(dram):
                return dram[0:2, bass.ds(u, 1)].rearrange("a o d t -> a (o d) t")

            for i in range(2):
                sp.dma_start(qa[s][i * 64:(i + 1) * 64, :], rows(q3, i).unsqueeze(0).broadcast_to([2, DH0, T])).then_inc(operands_in[s], 16)
                sp.dma_start(ka[s][i * 64:(i + 1) * 64, :], parts(k3)).then_inc(operands_in[s], 16)
            for i, (qp, kp) in enumerate(((0, 2), (2, 0))):
                sp.dma_start(qb[s][i * DH0:(i + 1) * DH0, :], rows(q3, qp)).then_inc(operands_in[s], 16)
                sp.dma_start(kb[s][i * DH0:(i + 1) * DH0, :], rows(k3, kp)).then_inc(operands_in[s], 16)
            sp.dma_start(v[s][:, :, :].rearrange("p k d -> p (k d)"),
                         v0[bass.ds(u, 1)].rearrange("o p x -> (o p) x")).then_inc(operands_in[s], 16)

        def rows_of_maxima(sp, r, s):
            apart(sp, max_parts, ONE + r * SLOTS + s + 1, passed)
            sp.dma_start(qb[s][2 * DH0:2 * DH0 + 1, :], max_hi[:, :]).then_inc(max_in, 16)
            sp.dma_start(qb[s][2 * DH0 + 1:KB, :], max_lo[:, :]).then_inc(max_in, 16)

        def store(sp, r, s):
            u = r * SLOTS + s
            apart(sp, o_d, O0 + u + 1, passed)
            for j in range(4):
                sp.dma_start(o0[bass.ds(u, 1), :, j * Q:(j + 1) * Q].rearrange("o d t -> (o d) t"),
                             ot[s % 2][j * DH0:(j + 1) * DH0, :]).then_inc(o_out[s % 2], 16)

        @block.sync
        def _(sp):
            for sm in (max_parts, max_in, *o_out):
                sp.sem_inc(sm, ONE)
            for s in range(SLOTS):
                load(sp, 0, s)
            rows_of_maxima(sp, 0, 0)
            with sp.Fori(0, LAST) as r:
                for s in range(SLOTS):
                    rows_of_maxima(sp, *after(r, s))
                    load(sp, r + 1, s)
                    store(sp, r, s)
            for s in range(SLOTS):
                if exists(LAST, s, 1):
                    rows_of_maxima(sp, *after(LAST, s))
                store(sp, LAST, s)
            for out_s in o_out:
                sp.wait_ge(out_s, ONE + UNITS // 2 * 64)

        @block.gpsimd
        def _(pool):
            for s in range(SLOTS):
                nc.gpsimd.memset(kb[s][2 * DH0:KB, :], 1.0).then_inc(ones_d, 1)
            pool.sem_inc(sum_p_d, SP0)
            with pool.Fori(0, UNITS // SLOTS) as r:
                for s in range(SLOTS):
                    u = r * SLOTS + s
                    pool.wait_ge(den_d, DEN0 + u - 1)
                    for n, k in enumerate(POOL_SUMS):
                        pool.wait_ge(probs_d, u * KT + k + 1)
                        if n:
                            pool.wait_ge(sum_p_d, SP0 + u * len(POOL_SUMS) + n)
                        nc.gpsimd.tensor_tensor(sum_p[s % 2][:, :], (sum_p[s % 2] if n else probs[0])[:, :],
                                                probs[k][:, :], ALU.add).then_inc(sum_p_d, 1)

        def max_half(pe, r, s, n):
            u = r * SLOTS + s
            if n == 0:
                pe.wait_ge(operands_in[s], (r + 1) * LOADS * 16)
                pe.wait_ge(max_parts, ONE + u)
            if n >= 2:
                pe.wait_ge(max_read, u * 2 * KT + n - 1)
            nc.tensor.matmul(p_m[n % 2][:, :], qa[s][:, (n // 2) * P:(n // 2 + 1) * P],
                             ka[s][:, (n % 2) * HALF:(n % 2 + 1) * HALF], start=True, stop=True).then_inc(max_scores, 1)

        def max_turn(pe, r, s):
            pe.wait_ge(max_row, ONE + r * SLOTS + s + 1)
            nc.tensor.transpose(p_m[0][0:KT, 0:P], rowmax[:, :], c["ident"][:, :]).then_inc(max_T, 1)

        def score(pe, r, s, k, h):
            u = r * SLOTS + s
            if k == 0 and h == 0:
                pe.wait_ge(max_in, ONE + (u + 1) * 32)
            g = u * KT + k
            if h == 0 and not (isinstance(g, int) and g < 2):
                pe.wait_ge(probs_d, g - 1)
            cols, q = slice(k * P, (k + 1) * P), slice(h * HALF, (h + 1) * HALF)
            nc.tensor.matmul(p_s[k % 2][:, q], ka[s][:, cols], qa[s][:, q], start=True, stop=False)
            mm = nc.tensor.matmul(p_s[k % 2][:, q], kb[s][:, cols], qb[s][:, q], start=False, stop=True)
            if h == 1:
                mm.then_inc(scores, 1)

        def spread(pe, s, col, lhs, rhs, start, stop):
            for j in range(4):
                mm = nc.tensor.matmul(p_o[s % 2][j * DH0:(j + 1) * DH0, col, :], lhs, rhs[:, j * Q:(j + 1) * Q],
                                      start=start, stop=stop, skip_group_check=True, tile_position=(0, j * DH0))
            return mm

        def values(pe, r, s, k):
            u = r * SLOTS + s
            pe.wait_ge(probs_d, u * KT + k + 1)
            if k == 0:
                pe.wait_ge(o_d, O0 + u - 1)
            spread(pe, s, 0, v[s][:, k, :], probs[k], k == 0, k == KT - 1).then_inc(pv_d, 1)

        def denominators(pe, r, s):
            u = r * SLOTS + s
            pe.wait_ge(sum_p_d, SP0 + (u + 1) * len(POOL_SUMS))
            pe.wait_ge(sum_v_d, SV0 + u + 1)
            spread(pe, s, 1, c["ones"][:, 0:DH0], sum_p[s % 2], False, False)
            spread(pe, s, 1, c["ones"][:, 0:DH0], sum_v[s % 2], False, True).then_inc(den_d, 1)

        def key_tile(pe, r, s, k):
            halves = list(range(sum(MAX_PLAN[:k]), sum(MAX_PLAN[:k + 1]))) if exists(r, s, 2) else []
            nxt = (r, s, k + 1) if k + 1 < KT else (*after(r, s), 0)
            for h in range(2):
                if exists(*nxt[:2]):
                    score(pe, *nxt, h)
                if halves:
                    max_half(pe, *after(r, s, 2), halves.pop(0))
            if k == 0 and exists(r, s, 1):
                max_turn(pe, *after(r, s))
            values(pe, r, s, k)
            for n in halves:
                max_half(pe, *after(r, s, 2), n)

        def rest_of_head(pe, r, s):
            for k in range(2, KT):
                key_tile(pe, r, s, k)
            if exists(r, s, 1):
                for k in range(2):
                    key_tile(pe, *after(r, s), k)
            denominators(pe, r, s)

        @block.tensor
        def _(pe):
            pe.sem_inc(pv_d, PV0)
            pe.sem_inc(den_d, DEN0)
            pe.wait_ge(ones_d, SLOTS)
            for n in range(2 * KT):
                max_half(pe, 0, 0, n)
            max_turn(pe, 0, 0)
            for n in range(2 * KT):
                max_half(pe, 0, 1, n)
            for h in range(2):
                score(pe, 0, 0, 0, h)
            for k in range(2):
                key_tile(pe, 0, 0, k)
            with pe.Fori(0, LAST) as r:
                for s in range(SLOTS):
                    rest_of_head(pe, r, s)
            for s in range(SLOTS):
                rest_of_head(pe, LAST, s)

        @block.scalar
        def _(act):
            with act.Fori(0, UNITS // SLOTS) as r:
                for s in range(SLOTS):
                    u = r * SLOTS + s
                    for k in range(KT):
                        act.wait_ge(scores, u * KT + k + 1)
                        act.wait_ge(pv_d, PV0 + (u - 1) * KT + k + 1)
                        if k in (3, 7):
                            act.wait_ge(sum_v_d, SV0 + u)
                        else:
                            act.wait_ge(sum_p_d, SP0 + (u - 1) * len(POOL_SUMS) + 1 + (POOL_SUMS.index(k) if k else 0))
                        nc.scalar.activation(probs[k][:, :], p_s[k % 2][:, :], ACT.Exp, scale=SCALE).then_inc(probs_d, 1)

        def half_maxima(dve, r, s, which):
            u = r * SLOTS + s
            for n in which:
                dve.wait_ge(max_scores, u * 2 * KT + n + 1)
                if n == 0:
                    dve.wait_ge(max_row, ONE + u)
                nc.vector.reduce_max(halfmax[:, n % 2, n // 2:n // 2 + 1], p_m[n % 2][:, :], AX.X).then_inc(max_read, 1)

        def row_maxima(dve, r, s):
            u = r * SLOTS + s
            dve.wait_ge(max_read, (u + 1) * 2 * KT)
            nc.vector.tensor_tensor(rowmax[:, :], halfmax[:, 0, :], halfmax[:, 1, :], ALU.max).then_inc(max_row, 1)

        def split_maxima(dve, r, s):
            u = r * SLOTS + s
            dve.wait_ge(max_T, u + 1)
            dve.wait_ge(max_in, ONE + u * 32)
            nc.vector.tensor_scalar(max_hi[:, :], p_m[0][0:KT, 0:P], -1.0, None, ALU.mult).then_inc(max_hi_d, 1)
            dve.wait_ge(max_hi_d, u + 1)
            nc.vector.scalar_tensor_tensor(out=max_lo[:, :], in0=p_m[0][0:KT, 0:P], scalar=-1.0,
                                           in1=max_hi[:, :], op0=ALU.mult, op1=ALU.subtract).then_inc(max_parts, 1)

        def add_last_tiles(dve, r, s):
            u = r * SLOTS + s
            dve.wait_ge(probs_d, (u + 1) * KT)
            dve.wait_ge(den_d, DEN0 + u - 1)
            nc.vector.tensor_tensor(sum_v[s % 2][:, :], probs[3][:, :], probs[7][:, :], ALU.add).then_inc(sum_v_d, 1)

        def normalise(dve, r, s):
            u = r * SLOTS + s
            dve.wait_ge(den_d, DEN0 + u + 1)
            dve.wait_ge(o_d, O0 + u)
            nc.vector.reciprocal(inv[:, :], p_o[s % 2][:, 1, :]).then_inc(inv_d, 1)
            dve.wait_ge(inv_d, u + 1)
            dve.wait_ge(o_out[s % 2], ONE + (r * (SLOTS // 2) + s // 2) * 64)
            nc.vector.tensor_tensor(ot[s % 2][:, :], p_o[s % 2][:, 0, :], inv[:, :], ALU.mult).then_inc(o_d, 1)

        EARLY, LATE = range(sum(MAX_PLAN[:2])), range(sum(MAX_PLAN[:2]), 2 * KT)

        @block.vector
        def _(dve):
            dve.sem_inc(o_d, O0)
            dve.sem_inc(sum_v_d, SV0)
            dve.sem_inc(max_row, ONE)
            half_maxima(dve, 0, 0, range(2 * KT))
            row_maxima(dve, 0, 0)
            split_maxima(dve, 0, 0)
            half_maxima(dve, 0, 1, range(2 * KT))
            row_maxima(dve, 0, 1)
            split_maxima(dve, 0, 1)
            half_maxima(dve, 0, 2, EARLY)

            def segment(r, s):
                if exists(r, s, 2):
                    half_maxima(dve, *after(r, s, 2), LATE)
                    row_maxima(dve, *after(r, s, 2))
                add_last_tiles(dve, r, s)
                if exists(r, s, 2):
                    split_maxima(dve, *after(r, s, 2))
                if exists(r, s, 3):
                    half_maxima(dve, *after(r, s, 3), EARLY)
                normalise(dve, r, s)

            with dve.Fori(0, LAST) as r:
                for s in range(SLOTS):
                    segment(r, s)
            for s in range(SLOTS):
                segment(LAST, s)


def block_table(nc, dve, c, count, experts, blocks, tabs, done, n0):
    n = [n0]

    def step(ins):
        ins.then_inc(done, 1)
        n[0] += 1
        dve.wait_ge(done, n[0])

    R = NTOK // BT
    region = tabs["region"]
    step(nc.vector.tensor_scalar(region[:, :], c["iota"][:, 0:experts], float(REGION), None, ALU.mult))
    step(nc.vector.tensor_tensor(tabs["tail"][:, :], region[:, :], count, ALU.add))
    cmp, used, upto, zero = tabs["cmp"], tabs["used"], tabs["upto"], tabs["zero"]
    ge, past, first, live = tabs["ge"], tabs["past"], tabs["first"], tabs["live"]
    step(nc.vector.memset(zero[:, :], 0.0))
    step(nc.vector.tensor_scalar(cmp[:, 0:R], c["iota"][:, 0:R], float(BT), None, ALU.mult))
    step(nc.vector.tensor_tensor(ge[:, 0:experts * R].rearrange("p (e r) -> p e r", r=R),
                                 count.unsqueeze(2).broadcast_to([P, experts, R]),
                                 cmp[:, 0:R].unsqueeze(1).broadcast_to([P, experts, R]), ALU.is_gt))
    step(nc.vector.tensor_reduce(used[:, :], ge[:, 0:experts * R].rearrange("p (e r) -> p e r", r=R), AX.X, ALU.add))
    step(nc.vector.tensor_tensor_scan(upto[:, :], used[:, :], zero[:, :], 0.0, ALU.add, ALU.add))
    je = ge[:, 0:blocks * experts].rearrange("p (j e) -> p j e", e=experts)
    shape = [P, blocks, experts]
    step(nc.vector.tensor_tensor(je, c["iota"][:, 0:blocks].unsqueeze(2).broadcast_to(shape),
                                 upto[:, :].unsqueeze(1).broadcast_to(shape), ALU.is_ge))
    step(nc.vector.tensor_reduce(past[:, :], je, AX.X, ALU.add))
    step(nc.vector.tensor_tensor(je, je, used[:, :].unsqueeze(1).broadcast_to(shape), ALU.mult))
    step(nc.vector.tensor_reduce(first[:, :], je, AX.X, ALU.add))
    step(nc.vector.tensor_tensor(first[:, :], c["iota"][:, 0:blocks], first[:, :], ALU.subtract))
    step(nc.vector.tensor_scalar(first[:, :], first[:, :], float(BT), None, ALU.mult))
    step(nc.vector.tensor_scalar(live[:, :], past[:, :], float(REGION), None, ALU.mult))
    step(nc.vector.tensor_tensor(tabs["row"][:, :], first[:, :], live[:, :], ALU.add))
    step(nc.vector.tensor_scalar(tabs["expert"][:, :], past[:, :], float(experts - 1), None, ALU.min))


def find_rows(nc, dve, tabs, experts, SLOT, done, part):
    def step(n, ins):
        ins.then_inc(done, 1)
        dve.wait_ge(done, n)

    region, used, upto = tabs["region"], tabs["used"], tabs["upto"]
    slotf, over, jump = tabs["slotf"], tabs["over"], tabs["jump"]
    shape = [P, slotf.shape[1], experts - 1]
    if part == 0:
        step(1, nc.vector.tensor_tensor(upto[:, :], upto[:, :], used[:, :], ALU.subtract))
        step(2, nc.vector.scalar_tensor_tensor(out=upto[:, :], in0=upto[:, :], scalar=float(BT), in1=region[:, :],
                                               op0=ALU.mult, op1=ALU.subtract))
        step(3, nc.vector.tensor_tensor(jump[:, :], upto[:, 1:experts], upto[:, 0:experts - 1], ALU.subtract))
        step(4, nc.vector.tensor_copy(slotf[:, :], SLOT))
        step(5, nc.vector.tensor_tensor(over[:, :, :], slotf[:, :].unsqueeze(2).broadcast_to(shape),
                                        region[:, 1:experts].unsqueeze(1).broadcast_to(shape), ALU.is_ge))
    else:
        step(6, nc.vector.tensor_tensor(over[:, :, :], over[:, :, :], jump[:, :].unsqueeze(1).broadcast_to(shape), ALU.mult))
        step(7, nc.vector.tensor_reduce(tabs["moved"][:, :], over[:, :, :], AX.X, ALU.add))
        step(8, nc.vector.tensor_tensor(slotf[:, :], slotf[:, :], tabs["moved"][:, :], ALU.add))
        step(9, nc.vector.tensor_copy(SLOT, slotf[:, :]))


TAIL_STEPS = 2


def tables(ctx, nc, name, choices, experts):
    blocks, slots = blocks_of(choices, experts), choices * TILES
    wide = {"cmp": 128, "region": experts, "used": experts, "upto": experts, "zero": experts, "past": blocks, "first": blocks,
            "ge": max(blocks, NTOK // BT) * experts, "live": blocks, "jump": experts - 1, "slotf": slots,
            "moved": slots}
    tabs = {n: ctx.enter_context(nc.sbuf_tensor(f"{name}_{n}", [P, w], F32)) for n, w in wide.items()}
    tabs["over"] = ctx.enter_context(nc.sbuf_tensor(f"{name}_over", [P, slots, experts - 1], F32))
    for n, w in (("row", blocks), ("expert", blocks), ("tail", experts)):
        tabs[n] = ctx.enter_context(nc.sbuf_tensor(f"{name}_{n}", [P, w], I32))
    return tabs


def zero_surplus(eng, xs, zeros, experts, surplus, out):
    for n in range(surplus):
        rows = slice(experts * REGION + n * BT, experts * REGION + (n + 1) * BT)
        eng.dma_start(xs[rows, :].rearrange("(p t) d -> p t d", p=P), zeros(n)).then_inc(out, 16)


def zero_tails(eng, xs, zeros, tabs, which, experts, out):
    for e in which:
        row = eng.value_load(tabs["tail"][0:1, e:e + 1], min_val=0, max_val=experts * REGION - BT)
        eng.dma_start(xs[bass.ds(row, BT), :].rearrange("(p t) d -> p t d", p=P), zeros(e)).then_inc(out, 16)


def route2(nc, c, X, XN, GATE, SLOT, tabs, w, o0, xs):
    with ExitStack() as ctx:
        def sb(name, shape, dt=F32):
            return ctx.enter_context(nc.sbuf_tensor(f"r2_{name}", shape, dt))

        sem = semaphores(ctx, nc, "r2", False)

        def ps(name, shape):
            return ctx.enter_context(nc.psum_tensor(f"r2_{name}", shape, F32))

        R = 4
        wo, wg = sb("wo", [P, 2, D]), sb("wg", [P, E0])
        oT = [sb(f"oT{i}", [P, 2, GT]) for i in range(2)]
        xn = [sb(f"xn{s}", [P, G, D]) for s in range(R)]
        slot = [sb(f"slot{s}", [P, G * 2], I32) for s in range(R)]
        stats, mv, rstd = sb("stats", [P, G, 6]), sb("mv", [P, G, 2]), sb("rstd", [P, G])
        xT = sb("xT", [P, GT])
        top, total = sb("top", [P, G]), sb("total", [P, G])
        prob = sb("prob", [P, G, E0])
        best, at = sb("best", [P, G, 8]), sb("at", [P, G, 8], U32)
        atf, slotf = sb("atf", [P, G, 2]), sb("slotf", [P, G, 2])
        hot, both = sb("hot", [P, G, 2, E0]), sb("both", [P, G, E0])
        seen = sb("seen", [P, G + 1, E0])
        now = sb("now", [P, E0])
        start = sb("start", [P, E0])
        place, placed = sb("place", [P, G, E0]), sb("placed", [P, G, 2, E0])
        zeros = sb("zeros", [P, BT // P, D])
        p_y, p_xT = ps("p_y", [P, G, D]), ps("p_xT", [P, GT])
        p_g, p_pos = ps("p_g", [P, 512]), ps("p_pos", [P, 512])
        gate_ps = p_g[:, 0:G * E0].rearrange("p (t e) -> p t e", e=E0)
        pos_ps = p_pos[:, 0:G * E0].rearrange("p (t e) -> p t e", e=E0)
        (w_in, y_d, x_d, stats_d, var_d, root_d, rstd_d, xn_d, pxT_d, xT_d, kept_d, gate_d, top_d, shift_d, exp_d,
         choice, hot_d, now_d, pos_d, places, slot_d, seen_d, sent, count_d, tabs_d, zeros_d, surplus_out, passed) = (
            sem(n) for n in ("w_in", "y", "x", "stats", "var", "root", "rstd", "xn", "pxT", "xT", "kept", "gate",
                             "top", "shift", "exp", "choice", "hot", "now", "pos", "places", "slot", "seen", "sent", "count",
                             "tabs", "zeros", "surplus_out", "passed"))
        tails_out = [sem(f"tails_out{i}") for i in range(2)]
        oT_in = [sem(f"oT_in{i}") for i in range(2)]
        rows_out = [sem(f"rows_out{s}") for s in range(R)]
        SENT0 = KEPT0 = R
        block = ctx.enter_context(nc.Block())

        def after(g, n=1):
            return g[0] + (g[1] + n) // R, (g[1] + n) % R

        def number(g):
            return g[0] * R + g[1]

        def exists(g):
            return not isinstance(number(g), int) or 0 <= number(g) < GROUPS

        def from_first(eng, sem, value):
            if not (isinstance(value, int) and value <= 0):
                eng.wait_ge(sem, value)

        def groups(eng, iteration):
            for g in range(3):
                iteration((0, g))
            with eng.Fori(0, GROUPS // R - 1) as r:
                for m in range(3, 3 + R):
                    iteration((r + m // R, m % R))
            for g in range(GROUPS - R + 3, GROUPS + 3):
                iteration((g // R, g % R))

        def group_of(T_, g):
            return T_[:, bass.ds(number(g) * GT, GT)].rearrange("p (t d) -> p t d", t=G)

        @block.sync
        def _(sp):
            def load(g):
                n, i = number(g), g[1] % 2
                if not (isinstance(n, int) and n < 2):
                    apart(sp, y_d, n - 1, passed)
                for cc in range(2):
                    b = g[0] * (R // 2) + g[1] // 2
                    sp.dma_start(oT[i][:, cc, :], o0[bass.ds(b * H0 + cc * 4, 4), :, i * GT:(i + 1) * GT]
                                 .rearrange("h d t -> (h d) t")).then_inc(oT_in[i], 16)

            for cc in range(2):
                sp.dma_start(wo[:, cc, :], w["WoT"][cc * P:(cc + 1) * P, :]).then_inc(w_in, 16)
            sp.dma_start(wg[:, :], w["gateT"]).then_inc(w_in, 16)
            groups(sp, lambda g: load(g) if exists(g) else None)
            sp.wait_ge(zeros_d, 3)
            zero_surplus(sp, xs, lambda n: zeros[:, :, :], E0, surplus_of(2, E0), surplus_out)
            sp.wait_ge(tabs_d, 1 + TAIL_STEPS)
            zero_tails(sp, xs, lambda e: zeros[:, :, :], tabs, range(0, E0 // 2), E0, tails_out[0])
            sp.wait_ge(surplus_out, surplus_of(2, E0) * 16)
            sp.wait_ge(tails_out[0], E0 // 2 * 16)

        @block.tensor
        def _(pe):
            def attention(g):
                n, i = number(g), g[1] % 2
                pe.wait_ge(oT_in[i], (g[0] * (R // 2) + g[1] // 2 + 1) * 32)
                from_first(pe, x_d, n)
                for t in range(G):
                    for cc in range(2):
                        mm = nc.tensor.matmul(p_y[:, t, :], oT[i][:, cc, t * P:(t + 1) * P], wo[:, cc, :],
                                              start=(cc == 0), stop=(cc == 1))
                mm.then_inc(y_d, 1)

            def turn(g):
                n = number(g)
                pe.wait_ge(xn_d, n + 1)
                from_first(pe, xT_d, n)
                for t in range(G):
                    mm = nc.tensor.transpose(p_xT[:, t * P:(t + 1) * P], xn[g[1]][:, t, :], c["ident"][:, :])
                mm.then_inc(pxT_d, 1)

            def logits(g):
                n = number(g)
                pe.wait_ge(xT_d, n + 1)
                from_first(pe, shift_d, n)
                for t in range(G):
                    mm = nc.tensor.matmul(gate_ps[:, t, :], xT[:, t * P:(t + 1) * P], wg[:, :], start=True, stop=True)
                mm.then_inc(gate_d, 1)

            def ranks(g):
                n = number(g)
                pe.wait_ge(hot_d, n + 1)
                pe.wait_ge(seen_d, (n + 1) * G)
                nc.tensor.matmul(pos_ps, c["stri"][:, :], both[:, :, :], start=True, stop=False)
                nc.tensor.matmul(pos_ps, c["ones"][:, :], seen[:, 0:G, :], start=False, stop=True).then_inc(pos_d, 1)

            def iteration(g):
                if exists(after(g, -1)):
                    turn(after(g, -1))
                    logits(after(g, -1))
                if exists(after(g, -2)):
                    ranks(after(g, -2))
                if exists(after(g)):
                    attention(after(g))

            pe.wait_ge(w_in, 48)
            pe.wait_ge(zeros_d, 3)
            attention((0, 0))
            groups(pe, iteration)
            pe.wait_ge(seen_d, GROUPS * G + 1)
            nc.tensor.matmul(p_pos[:, 0:E0], c["ones"][:, :], seen[:, 0, :], start=True, stop=True).then_inc(count_d, 1)

        @block.scalar
        def _(act):
            def iteration(g):
                n, before = number(g), after(g, -1)
                if exists(before):
                    act.wait_ge(pxT_d, n)
                    from_first(act, gate_d, n - 1)
                    nc.scalar.copy(xT[:, :], p_xT[:, :]).then_inc(xT_d, 1)
                    nc.scalar.copy(group_of(XN, before), xn[before[1]][:, :, :]).then_inc(kept_d, 1)
                if exists(g):
                    act.wait_ge(var_d, n + 1)
                    nc.scalar.activation(rstd[:, :], rstd[:, :], ACT.Sqrt).then_inc(root_d, 1)
                if exists(before):
                    act.wait_ge(shift_d, n)
                    nc.scalar.activation(prob[:, :, :], prob[:, :, :], ACT.Exp).then_inc(exp_d, 1)

            act.sem_inc(kept_d, KEPT0)
            groups(act, iteration)
            act.wait_ge(tabs_d, 1 + TAIL_STEPS)
            zero_tails(act, xs, lambda e: zeros[:, :, :], tabs, range(E0 // 2, E0), E0, tails_out[1])
            act.wait_ge(tails_out[1], (E0 - E0 // 2) * 16)

        @block.vector
        def _(dve):
            def chain(sem, base):
                n = [0]

                def step(ins):
                    n[0] += 1
                    ins.then_inc(sem, 1)
                    dve.wait_ge(sem, base + n[0])
                return step

            def add_attention(g):
                n = number(g)
                dve.wait_ge(y_d, n + 1)
                nc.vector.tensor_tensor(group_of(X, g), group_of(X, g), p_y[:, :, :], ALU.add).then_inc(x_d, 1)
                apart(dve, x_d, n + 1, passed)
                for t in range(G):
                    last = nc.vector.bn_stats(stats[:, t, :], group_of(X, g)[:, t, :])
                last.then_inc(stats_d, 1)
                apart(dve, stats_d, 2 * n + 1, passed)
                for t in range(G):
                    last = nc.vector.bn_aggr(mv[:, t, :], stats[:, t, :])
                last.then_inc(stats_d, 1)
                dve.wait_ge(stats_d, 2 * n + 2)
                nc.vector.tensor_scalar(rstd[:, :], mv[:, :, 1], LN_EPS, None, ALU.add).then_inc(var_d, 1)

            def normalise(g):
                n, s = number(g), g[1]
                dve.wait_ge(root_d, n + 1)
                nc.vector.reciprocal(rstd[:, :], rstd[:, :]).then_inc(rstd_d, 1)
                apart(dve, sent, SENT0 + n - R + 1, passed)
                apart(dve, kept_d, KEPT0 + n - R + 1, passed)
                dve.wait_ge(rstd_d, n + 1)
                for t in range(G):
                    last = nc.vector.tensor_scalar(xn[s][:, t, :], group_of(X, g)[:, t, :], mv[:, t, 0:1], rstd[:, t:t + 1],
                                                   ALU.subtract, ALU.mult)
                last.then_inc(xn_d, 1)

            def shift_logits(g):
                n = number(g)
                dve.wait_ge(gate_d, n + 1)
                nc.vector.tensor_reduce(top[:, :], gate_ps, AX.X, ALU.max).then_inc(top_d, 1)
                dve.wait_ge(top_d, n + 1)
                nc.vector.tensor_tensor(prob[:, :, :], gate_ps, top[:, :].unsqueeze(2).broadcast_to([P, G, E0]),
                                        ALU.subtract).then_inc(shift_d, 1)

            def choose(g):
                n = number(g)
                step = chain(choice, n * 10)
                dve.wait_ge(exp_d, n + 1)
                step(nc.vector.tensor_reduce(total[:, :], prob[:, :, :], AX.X, ALU.add))
                step(nc.vector.reciprocal(total[:, :], total[:, :]))
                step(nc.vector.tensor_tensor(prob[:, :, :], prob[:, :, :], total[:, :].unsqueeze(2).broadcast_to([P, G, E0]), ALU.mult))
                dve.sem_inc(passed, 1)
                for t in range(G):
                    last = nc.vector.max(best[:, t, :], prob[:, t, :])
                step(last)
                dve.sem_inc(passed, 1)
                for t in range(G):
                    last = nc.vector.max_index(at[:, t, :], best[:, t, :], prob[:, t, :])
                step(last)
                step(nc.vector.tensor_copy(atf[:, :, :], at[:, :, 0:2]))
                step(nc.vector.tensor_tensor(hot[:, :, :, :], c["iota"][:, 0:E0].unsqueeze(1).unsqueeze(1).broadcast_to([P, G, 2, E0]),
                                             atf[:, :, :].unsqueeze(3).broadcast_to([P, G, 2, E0]), ALU.is_equal))
                nc.vector.tensor_tensor(both[:, :, :], hot[:, :, 0, :], hot[:, :, 1, :], ALU.add).then_inc(hot_d, 1)
                dve.wait_ge(hot_d, n + 1)
                count = chain(seen_d, n * G)
                from_first(dve, pos_d, n)
                count(nc.vector.tensor_copy(seen[:, 0, :], seen[:, G, :]))
                for t in range(G - 1):
                    count(nc.vector.tensor_tensor(seen[:, t + 1, :], seen[:, t, :], both[:, t, :], ALU.add))
                nc.vector.tensor_tensor(seen[:, G, :], seen[:, G - 1, :], both[:, G - 1, :], ALU.add).then_inc(now_d, 1)
                step(nc.vector.tensor_tensor(total[:, :], best[:, :, 0], best[:, :, 1], ALU.add))
                step(nc.vector.tensor_scalar(total[:, :], total[:, :], 1e-10, None, ALU.max))
                step(nc.vector.reciprocal(total[:, :], total[:, :]))
                nc.vector.tensor_tensor(GATE[:, bass.ds(n * G * 2, G * 2)].rearrange("p (t k) -> p t k", k=2), best[:, :, 0:2],
                                        total[:, :].unsqueeze(2).broadcast_to([P, G, 2]), ALU.mult)

            def find_slots(g):
                n, s = number(g), g[1]
                step = chain(places, n * 3)
                dve.wait_ge(pos_d, n + 1)
                step(nc.vector.tensor_tensor(place[:, :, :], pos_ps, start[:, :].unsqueeze(1).broadcast_to([P, G, E0]), ALU.add))
                step(nc.vector.tensor_tensor(placed[:, :, :, :], hot[:, :, :, :], place[:, :, :].unsqueeze(2).broadcast_to([P, G, 2, E0]), ALU.mult))
                step(nc.vector.tensor_reduce(slotf[:, :, :], placed[:, :, :, :], AX.X, ALU.add))
                nc.vector.tensor_copy(slot[s][:, :], slotf[:, :, :].rearrange("p t k -> p (t k)")).then_inc(slot_d, 1)
                nc.vector.tensor_copy(SLOT[:, bass.ds(n * G * 2, G * 2)], slotf[:, :, :].rearrange("p t k -> p (t k)"))
                dve.wait_ge(now_d, n + 1)

            def iteration(g):
                before, choosing = after(g, -1), after(g, -2)
                if exists(before):
                    normalise(before)
                if exists(choosing):
                    choose(choosing)
                if exists(g):
                    add_attention(g)
                if exists(before):
                    shift_logits(before)
                if exists(choosing):
                    find_slots(choosing)

            nc.vector.tensor_scalar(start[:, :], c["iota"][:, 0:E0], float(REGION), None, ALU.mult).then_inc(zeros_d, 1)
            nc.vector.memset(zeros[:, :, :], 0.0).then_inc(zeros_d, 1)
            nc.vector.memset(seen[:, :, :], 0.0).then_inc(zeros_d, 1)
            dve.wait_ge(zeros_d, 3)
            groups(dve, iteration)
            nc.vector.tensor_copy(seen[:, 0, :], seen[:, G, :]).then_inc(seen_d, 1)
            dve.wait_ge(count_d, 1)
            nc.vector.tensor_copy(now[:, :], p_pos[:, 0:E0]).then_inc(tabs_d, 1)
            dve.wait_ge(tabs_d, 1)
            block_table(nc, dve, c, now[:, :], E0, blocks_of(2, E0), tabs, tabs_d, 1)

        @block.gpsimd
        def _(pool):
            def scatter(g):
                s = g[1]
                apart(pool, slot_d, number(g) + 1, passed)
                for t in range(G):
                    for k in range(2):
                        pool.indirect_dma_start(xs[:, :], bass.IndirectOffsetOnAxis(ap=slot[s][:, t * 2 + k:t * 2 + k + 1], axis=0),
                                                xn[s][:, t, :], None).then_inc(rows_out[s], 16)

            def iteration(g):
                if exists(after(g, -2)):
                    scatter(after(g, -2))
                q, s = after(g, -3)
                if exists((q, s)):
                    apart(pool, rows_out[s], (q + 1) * G * 2 * 16, sent)

            pool.sem_inc(sent, SENT0)
            groups(pool, iteration)
            pool.wait_ge(rows_out[R - 1], GROUPS // R * G * 2 * 16)


def experts(nc, c, name, odd, E, F, act_fn, tabs, blocks, surplus, weights, b2_rows, xs, ys, named, SLOT=None):
    with ExitStack() as ctx:
        def sb(n, shape, dt=F32):
            return ctx.enter_context(nc.sbuf_tensor(f"{name}_{n}", shape, dt))

        sem = semaphores(ctx, nc, name, odd)

        def ps(n, shape):
            return ctx.enter_context(nc.psum_tensor(f"{name}_{n}", shape, F32))

        AHEAD = 4
        NF, NT = F // P, BT // P
        W = F + NF + NF * D
        wb = [sb(f"w{i}", [P, W]) for i in range(AHEAD)]
        w1, b1 = [t[:, 0:F] for t in wb], [t[:, F:F + NF] for t in wb]
        w2 = [t[:, F + NF:W].rearrange("p (f d) -> p f d", f=NF) for t in wb]
        b2 = [sb(f"b2_{i}", [P, D]) for i in range(AHEAD)]
        xb = [sb(f"xb{i}", [P, NT, D + named]) for i in range(AHEAD)]
        row_of = [sb(f"row_of{i}", [P, NT], I32) for i in range(AHEAD)]
        y = [sb(f"y{i}", [P, NT, D]) for i in range(AHEAD)]
        xT = [sb(f"xT{i}", [P, BT]) for i in range(2)]
        h = [sb(f"h{i}", [P, NF, BT]) for i in range(2)]
        p_xT = [ps(f"p_xT{i}", [P, 512]) for i in range(2)]
        p_h = [ps(f"p_h{i}", [P, max(NF, 2), BT]) for i in range(2)]
        p_y = [ps(f"p_y{i}", [P, 512]) for i in range(2)]
        rows_in = [sem(f"rows_in{i}") for i in range(AHEAD)]
        weights_in = [sem(f"weights_in{i}") for i in range(AHEAD)]
        y_out = [sem(f"y_out{i}") for i in range(AHEAD)]
        pxT_d, xT_d, ph_d, h_d, py_d, y_d, sent, found, passed = (
            sem(n) for n in ("pxT", "xT", "ph", "h", "py", "y", "sent", "found", "passed"))
        PH0 = PY0 = 2
        Y0 = SENT0 = AHEAD
        block = ctx.enter_context(nc.Block())

        def turn(pe, j, s, q):
            pe.wait_ge(rows_in[s], (q + 1) * 16)
            for t in range(NT):
                mm = nc.tensor.transpose(p_xT[s % 2][:, t * P:(t + 1) * P], xb[s][:, t, 0:D], c["ident"][:, :])
            mm.then_inc(pxT_d, 1)

        def hidden(pe, j, s, q):
            pe.wait_ge(weights_in[s], (q + 1) * 32)
            pe.wait_ge(xT_d, j + 1)
            for f in range(NF):
                mm = nc.tensor.matmul(p_h[s % 2][:, f, :], w1[s][:, f * P:(f + 1) * P], xT[s % 2][:, :], start=True, stop=True)
            mm.then_inc(ph_d, 1)

        def outputs(pe, j, s, q):
            pe.wait_ge(h_d, j + 1)
            pe.wait_ge(y_d, Y0 + j - 1)
            for t in range(NT):
                for f in range(NF):
                    mm = nc.tensor.matmul(p_y[s % 2][:, t * P:(t + 1) * P], h[s % 2][:, f, t * P:(t + 1) * P], w2[s][:, f, :],
                                          start=(f == 0), stop=(f == NF - 1))
            mm.then_inc(py_d, 1)

        def copy_turned(dve, j, s, q):
            dve.wait_ge(pxT_d, j + 1)
            dve.wait_ge(ph_d, PH0 + j - 1)
            nc.vector.tensor_copy(xT[s % 2][:, :], p_xT[s % 2][:, 0:BT]).then_inc(xT_d, 1)

        def activate(act, j, s, q):
            act.wait_ge(ph_d, PH0 + j + 1)
            act.wait_ge(py_d, PY0 + j - 1)
            for f in range(NF):
                last = nc.scalar.activation(h[s % 2][:, f, :], p_h[s % 2][:, f, :], act_fn, bias=b1[s][:, f:f + 1])
            last.then_inc(h_d, 1)

        def add_bias(dve, j, s, q):
            apart(dve, sent, SENT0 + j - AHEAD + 1, passed)
            if named:
                apart(dve, py_d, PY0 + j + 1, passed)
                nc.vector.tensor_copy(row_of[s][:, :], xb[s][:, :, D])
            else:
                dve.wait_ge(py_d, PY0 + j + 1)
            nc.vector.tensor_tensor(y[s][:, :, :], p_y[s % 2][:, 0:BT].rearrange("p (t d) -> p t d", t=NT),
                                    b2[s][:, :].unsqueeze(1).broadcast_to([P, NT, D]), ALU.add).then_inc(y_d, 1)

        def load(sp, j, s, q):
            row = sp.value_load(tabs["row"][0:1, bass.ds(j, 1)], min_val=0, max_val=E * REGION + surplus * BT - BT)
            e = sp.value_load(tabs["expert"][0:1, bass.ds(j, 1)], min_val=0, max_val=E - 1)
            sp.dma_start(xb[s][:, :, :], xs[bass.ds(row, BT), :].rearrange("(p t) d -> p t d", p=P)).then_inc(rows_in[s], 16)
            sp.dma_start(wb[s][:, :], weights[bass.ds(e, 1)].rearrange("o p w -> (o p) w")).then_inc(weights_in[s], 16)
            sp.dma_start(b2[s][:, :], b2_rows[bass.ds(e, 1), :].broadcast_to([P, D])).then_inc(weights_in[s], 16)

        def used(sp, j, s, q):
            apart(sp, y_d, Y0 + j + 1, passed)

        def store(eng, j, s, q):
            if named:
                apart(eng, y_d, Y0 + j + 1, passed)
                for t in range(NT):
                    eng.indirect_dma_start(ys[:, :], bass.IndirectOffsetOnAxis(ap=row_of[s][:, t:t + 1], axis=0),
                                           y[s][:, t, :], None).then_inc(y_out[s], 16)
            else:
                eng.dma_start(ys[bass.ds(j * BT, BT), :].rearrange("(p t) d -> p t d", p=P), y[s][:, :, :]).then_inc(y_out[s], 16)

        def stored(eng, j, s, q):
            apart(eng, y_out[s], (q + 1) * (16 * NT if named else 16), sent)

        def steps(eng, first, end, *parts):
            def step(r, k):
                for offset, part in parts:
                    m = k + offset
                    part(eng, r * AHEAD + m, m % AHEAD, r + m // AHEAD)

            rounds = (end - first) // AHEAD
            with eng.Fori(0, rounds) as r:
                for k in range(first, first + AHEAD):
                    step(r, k)
            for k in range(first + rounds * AHEAD, end):
                step(0, k)

        @block.sync
        def _(sp):
            for s in range(AHEAD):
                load(sp, s, s, 0)
            if named:
                steps(sp, 0, blocks - AHEAD, (0, used), (AHEAD, load))
            else:
                used(sp, 0, 0, 0)
                store(sp, 0, 0, 0)
                load(sp, AHEAD, 0, 1)
                steps(sp, 1, blocks - AHEAD, (0, used), (0, store), (AHEAD, load))
                for j in range(blocks - AHEAD, blocks):
                    used(sp, j, j % AHEAD, j // AHEAD)
                    store(sp, j, j % AHEAD, j // AHEAD)

        @block.gpsimd
        def _(pool):
            pool.sem_inc(sent, SENT0)
            if named:
                store(pool, 0, 0, 0)
                store(pool, 1, 1, 0)
                steps(pool, 2, blocks, (0, store), (-2, stored))
                for j in (blocks - 2, blocks - 1):
                    stored(pool, j, j % AHEAD, j // AHEAD)
            else:
                steps(pool, 0, blocks, (0, stored))

        @block.tensor
        def _(pe):
            pe.sem_inc(py_d, PY0)
            pe.sem_inc(ph_d, PH0)
            turn(pe, 0, 0, 0)
            hidden(pe, 0, 0, 0)
            turn(pe, 1, 1, 0)
            steps(pe, 1, blocks - 1, (0, hidden), (1, turn), (-1, outputs))
            hidden(pe, blocks - 1, (blocks - 1) % AHEAD, (blocks - 1) // AHEAD)
            for j in (blocks - 2, blocks - 1):
                outputs(pe, j, j % AHEAD, j // AHEAD)

        @block.scalar
        def _(act):
            steps(act, 0, blocks, (0, activate))

        @block.vector
        def _(dve):
            dve.sem_inc(y_d, Y0)
            if SLOT is not None:
                find_rows(nc, dve, tabs, E, SLOT, found, 0)
            copy_turned(dve, 0, 0, 0)
            if SLOT is not None:
                find_rows(nc, dve, tabs, E, SLOT, found, 1)
            copy_turned(dve, 1, 1, 0)
            steps(dve, 1, blocks - 1, (1, copy_turned), (-1, add_bias))
            for j in (blocks - 2, blocks - 1):
                add_bias(dve, j, j % AHEAD, j // AHEAD)


def linear(nc, c, X, XN, GATE, SLOT, BESTP, HOT, w, ys):
    with ExitStack() as ctx:
        def sb(name, shape, dt=F32):
            return ctx.enter_context(nc.sbuf_tensor(f"ln_{name}", shape, dt))

        sem = semaphores(ctx, nc, "ln", False)

        def ps(name, shape):
            return ctx.enter_context(nc.psum_tensor(f"ln_{name}", shape, F32))

        wqkv, wo, wr = sb("wqkv", [P, 3 * D]), sb("wo", [P, D]), sb("wr", [P, E1])
        slot = [sb(f"slot{i}", [P, G * 2], I32) for i in range(2)]
        rows = [sb(f"rows{i}", [P, G * 2, D]) for i in range(2)]
        moe = sb("moe", [P, G, D])
        stats, mv, rstd, shift, xn, xT = ({k: sb(f"{n}_{k}", shape) for k in "ac"} for n, shape in (
            ("stats", [P, G, 6]), ("mv", [P, G, 2]), ("rstd", [P, G]), ("shift", [P, G]), ("xn", [P, G, D]), ("xT", [P, GT])))
        qk = [sb(f"qk{i}", [P, 2 * D]) for i in range(2)]
        v1 = [sb(f"v1_{i}", [P, D + 1]) for i in range(2)]
        qT = [sb(f"qT{i}", [P, P]) for i in range(2)]
        kv = [sb(f"kv{i}", [P, KV1 + D]) for i in range(2)]
        raw, state = sb("raw", [P, D + 1]), sb("state", [P, D + H1])
        own_head = sb("own_head", [P, D + H1])
        prod = sb("prod", [P, KV1 + D])
        num, den = sb("num", [P, D]), sb("den", [P, H1])
        o, oT = sb("o", [P, G, D]), sb("oT", [P, GT])
        top, total = sb("top", [P, G]), sb("total", [P, G])
        prob, best, at = sb("prob", [P, G, E1]), sb("best", [P, G, 8]), sb("at", [P, G, 8], U32)
        atf = sb("atf", [P, G])
        p_T, p_qkv = ps("p_T", [P, 512]), ps("p_qkv", [P, 512])
        p_cum = ps("p_cum", [P, 3, 512])
        p_prev, p_st, p_y = ps("p_prev", [P, 512]), ps("p_st", [P, 512]), ps("p_y", [P, G, D])
        S = {n: sem(n) for n in (
            "w_in", "ones", "mask", "x_a", "x_c", "stats_a", "stats_c", "var_a", "var_c", "root_a", "root_c",
            "rstd_a", "rstd_c", "xn_a", "xn_c", "pxT_a", "pxT_c", "xT_a", "xT_c", "qkv", "qk", "v", "pqT", "qT",
            "kc", "kv", "st", "raw", "state", "cum", "prev", "prod", "o", "poT", "oT", "y", "kept", "logits", "shift",
            "exp", "passed", "moe", "clip", "den", "num", "slots", "gated", "top", "router")}
        rows_in = [sem(f"rows_in{i}") for i in range(2)]
        passed = S["passed"]
        block = ctx.enter_context(nc.Block())

        def after(g, n=1):
            return g[0] + (g[1] + n) // 2, (g[1] + n) % 2

        def number(g):
            return g[0] * 2 + g[1]

        def exists(g):
            return not isinstance(number(g), int) or 0 <= number(g) < GROUPS

        def from_first(eng, name, value):
            if not (isinstance(value, int) and value <= 0):
                eng.wait_ge(S[name], value)

        def next_tile(g, t, n=1):
            return after(g, (t + n) // G), (t + n) % G

        def tile_number(g, t):
            return number(g) * G + t

        def prevs(b, tb):
            return b * (KT - 1) + (tb if tb >= 0 else tb + 1)

        def groups(eng, iteration):
            for g in range(-2, 2):
                iteration((g // 2, g % 2))
            with eng.Fori(0, B - 2) as r:
                for i in range(2):
                    iteration((r + 1, i))
            for g in range(GROUPS - 2, GROUPS + 2):
                iteration((g // 2, g % 2))

        def group_of(T_, g, width=D):
            return T_[:, bass.ds(number(g) * G * width, G * width)].rearrange("p (t d) -> p t d", t=G)

        @block.sync
        def _(sp):
            for dst, src in ((wqkv, w["WqkvT"]), (wo, w["Wo1T"]), (wr, w["routerT"])):
                sp.dma_start(dst[:, :], src).then_inc(S["w_in"], 16)
            sp.wait_ge(S["w_in"], 48)

        @block.gpsimd
        def _(pool):
            def masked(out, keys, reps):
                nc.gpsimd.memset(out, 1.0).then_inc(S["mask"], 1)
                pool.wait_ge(S["mask"], keys + 1)
                nc.gpsimd.affine_select(out=out, in_=out, compare_op=ALU.is_ge, fill=0.0, base=0,
                                        pattern=[[-DH1, H1], [0, reps]], channel_multiplier=1).then_inc(S["mask"], 1)
                pool.wait_ge(S["mask"], keys + 2)
                nc.gpsimd.affine_select(out=out, in_=out, compare_op=ALU.is_ge, fill=0.0, base=DH1 - 1,
                                        pattern=[[DH1, H1], [0, reps]], channel_multiplier=-1).then_inc(S["mask"], 1)

            masked(own_head[:, 0:D].rearrange("p (h m) -> p h m", h=H1), 0, DH1)
            masked(own_head[:, D:D + H1].rearrange("p (h m) -> p h m", h=H1), 3, 1)
            for i in range(2):
                nc.gpsimd.memset(v1[i][:, D:D + 1], 1.0).then_inc(S["ones"], 1)

            def take_slots(g):
                n, i = number(g), g[1]
                nc.gpsimd.tensor_copy(slot[i][:, :], SLOT[:, bass.ds(n * G * 2, G * 2)]).then_inc(S["slots"], 1)
                apart(pool, S["slots"], n + 1, passed)
                if not (isinstance(n, int) and n < 2):
                    apart(pool, S["moe"], n - 1, passed)

            def gather(g, t):
                i = g[1]
                for n in ((0, 1, 2), (3, 4, 5), (6, 7), ())[t]:
                    pool.indirect_dma_start(rows[i][:, n, :], None, ys[:, :],
                                            bass.IndirectOffsetOnAxis(ap=slot[i][:, n:n + 1], axis=0)).then_inc(rows_in[i], 16)

            def gate(g):
                b, i = g
                n = number(g)
                two = rows[i][:, :, :].rearrange("p (t k) d -> p t k d", k=2)
                apart(pool, rows_in[i], (b + 1) * G * 2 * 16, passed)
                nc.gpsimd.tensor_tensor(rows[i][:, :, :], rows[i][:, :, :],
                                        GATE[:, bass.ds(number(g) * G * 2, G * 2)].unsqueeze(2).broadcast_to([P, G * 2, D]),
                                        ALU.mult).then_inc(S["gated"], 1)
                pool.wait_ge(S["gated"], 2 * n + 1)
                nc.gpsimd.tensor_tensor(two[:, :, 0, :], two[:, :, 0, :], two[:, :, 1, :], ALU.add).then_inc(S["gated"], 1)
                if not (isinstance(n, int) and n == 0):
                    apart(pool, S["x_a"], n, passed)
                apart(pool, S["gated"], 2 * n + 2, passed)
                nc.gpsimd.tensor_tensor(moe[:, :, :], two[:, :, 0, :], group_of(XN, g), ALU.add).then_inc(S["moe"], 1)

            def keep_state(g, t):
                n = tile_number(g, t)
                apart(pool, S["raw"], n + 1, passed)
                if not (isinstance(n, int) and n == 0):
                    apart(pool, S["prev"], prevs(g[0], g[1] * G + t), passed)
                nc.gpsimd.tensor_tensor(state[:, 0:D], raw[:, 0:D], own_head[:, 0:D], ALU.mult).then_inc(S["state"], 1)
                nc.gpsimd.tensor_tensor(state[:, D:D + H1], own_head[:, D:D + H1], raw[:, D:D + 1].broadcast_to([P, H1]), ALU.mult).then_inc(S["state"], 1)

            def outer(g, t):
                n = tile_number(g, t)
                pool.wait_ge(S["v"], n + 1)
                from_first(pool, "cum", n - 1)
                shape = [P, H1, DH1, DH1]
                k = qk[t % 2][:, D:2 * D].rearrange("p (h d) -> p h d", h=H1)
                v = v1[t % 2][:, 0:D].rearrange("p (h m) -> p h m", h=H1)
                nc.gpsimd.tensor_tensor(kv[t % 2][:, 0:KV1].rearrange("p (h d m) -> p h d m", h=H1, d=DH1),
                                        k.unsqueeze(3).broadcast_to(shape), v.unsqueeze(2).broadcast_to(shape),
                                        ALU.mult).then_inc(S["kv"], 1)

            def iteration(g):
                for t in range(G):
                    nxt = next_tile(g, t)
                    if exists(g):
                        keep_state(g, t)
                    if exists(nxt[0]):
                        outer(*nxt)
                    if exists(after(g, 2)):
                        if t == 0:
                            take_slots(after(g, 2))
                        gather(after(g, 2), t)
                        if t == 3:
                            gate(after(g, 2))

            pool.wait_ge(S["mask"], 6)
            pool.sem_inc(passed, 1)
            groups(pool, iteration)

        @block.tensor
        def _(pe):
            def turned(src, done):
                for t in range(G):
                    mm = nc.tensor.transpose(p_T[:, t * P:(t + 1) * P], src[:, t, :], c["ident"][:, :])
                mm.then_inc(done, 1)

            def project_tile(g, t):
                n = tile_number(g, t)
                if t == 0:
                    pe.wait_ge(S["xT_a"], number(g) + 1)
                from_first(pe, "v", n)
                nc.tensor.matmul(p_qkv[:, 0:3 * D], xT["a"][:, t * P:(t + 1) * P], wqkv[:, :], start=True,
                                 stop=True).then_inc(S["qkv"], 1)

            def add_state(g, t):
                n, tb = tile_number(g, t), g[1] * G + t
                pe.wait_ge(S["v"], n + 1)
                from_first(pe, "raw", n)
                nc.tensor.matmul(p_st[:, 0:D + 1], qk[t % 2][:, D:2 * D], v1[t % 2][:, :], start=(tb == 0),
                                 stop=(tb == KT - 1), skip_group_check=True).then_inc(S["st"], 1)

            def turn_q(g, t):
                n = tile_number(g, t)
                from_first(pe, "qT", n)
                nc.tensor.transpose(p_T[:, 0:P], qk[t % 2][:, 0:D], c["ident"][:, :]).then_inc(S["pqT"], 1)

            def sums(g, t):
                n = tile_number(g, t)
                pe.wait_ge(S["kv"], n + 1)
                pe.wait_ge(S["kc"], n + 1)
                from_first(pe, "prod", 2 * n)
                for a in range(3):
                    z = min(512, KV1 + D - a * 512)
                    mm = nc.tensor.matmul(p_cum[:, a, 0:z], c["tri"][:, :], kv[t % 2][:, a * 512:a * 512 + z],
                                          start=True, stop=True)
                mm.then_inc(S["cum"], 1)

            def earlier(g, t):
                n = tile_number(g, t)
                if g[1] * G + t == 0:
                    return
                pe.wait_ge(S["qT"], n + 1)
                pe.wait_ge(S["state"], 2 * n)
                pe.wait_ge(S["o"], n)
                nc.tensor.matmul(p_prev[:, 0:D + H1], qT[t % 2][:, :], state[:, :], start=True,
                                 stop=True).then_inc(S["prev"], 1)

            def turn_output(g):
                n = number(g)
                pe.wait_ge(S["o"], n * G + G)
                pe.wait_ge(S["qT"], min(n * G + G + 1, NTOK // P) if isinstance(n, int) else n * G + G + 1)
                turned(o, S["poT"])

            def output_rows(g):
                n = number(g)
                pe.wait_ge(S["oT"], n + 1)
                from_first(pe, "shift", n)
                for t in range(G):
                    mm = nc.tensor.matmul(p_y[:, t, :], oT[:, t * P:(t + 1) * P], wo[:, :], start=True, stop=True)
                mm.then_inc(S["y"], 1)

            def turn_first(g):
                n = number(g)
                from_first(pe, "qT", n * G - 1)
                pe.wait_ge(S["xn_a"], n + 1)
                turned(xn["a"], S["pxT_a"])

            def turn_second(g):
                n = number(g)
                tiles = (n + 2) * G
                pe.wait_ge(S["qT"], min(tiles, NTOK // P) if isinstance(n, int) else tiles)
                pe.wait_ge(S["xn_c"], n + 1)
                turned(xn["c"], S["pxT_c"])

            def router(g):
                n = number(g)
                pe.wait_ge(S["xT_c"], n + 1)
                for t in range(G):
                    mm = nc.tensor.matmul(p_y[:, 0, t * E1:(t + 1) * E1], xT["c"][:, t * P:(t + 1) * P], wr[:, :], start=True, stop=True)
                mm.then_inc(S["logits"], 1)

            def iteration(g):
                before = after(g, -1)
                for t in range(G):
                    nxt, second = next_tile(g, t), next_tile(g, t, 2)
                    if t == 0 and exists(before):
                        turn_output(before)
                    if t == 2 and exists(after(g)):
                        turn_first(after(g))
                    if t == 3 and exists(before):
                        turn_second(before)
                    if exists(nxt[0]):
                        add_state(*nxt)
                    if exists(second[0]):
                        project_tile(*second)
                    if t == 0 and exists(before):
                        output_rows(before)
                    if t == 3 and exists(before):
                        router(before)
                    if exists(nxt[0]):
                        turn_q(*nxt)
                        sums(*nxt)
                        earlier(*nxt)

            pe.wait_ge(S["w_in"], 48)
            pe.wait_ge(S["ones"], 2)
            groups(pe, iteration)

        @block.scalar
        def _(act):
            def root(g, k):
                act.wait_ge(S[f"var_{k}"], number(g) + 1)
                nc.scalar.activation(rstd[k][:, :], rstd[k][:, :], ACT.Sqrt).then_inc(S[f"root_{k}"], 1)

            def keep_turned(g, k):
                n = number(g)
                act.wait_ge(S[f"pxT_{k}"], n + 1)
                from_first(act, *(("qkv", n * G) if k == "a" else ("logits", n)))
                nc.scalar.copy(xT[k][:, :], p_T[:, :]).then_inc(S[f"xT_{k}"], 1)

            def keep_rows(g):
                nc.scalar.copy(group_of(XN, g), xn["c"][:, :, :]).then_inc(S["kept"], 1)

            def keep_output(g):
                n = number(g)
                act.wait_ge(S["poT"], n + 1)
                from_first(act, "y", n)
                nc.scalar.copy(oT[:, :], p_T[:, :]).then_inc(S["oT"], 1)

            def keep_sums(g, t):
                n = tile_number(g, t)
                act.wait_ge(S["st"], n + 1)
                from_first(act, "state", 2 * n)
                nc.scalar.copy(raw[:, :], p_st[:, 0:D + 1]).then_inc(S["raw"], 1)

            def keep_values(g, t):
                n = tile_number(g, t)
                act.wait_ge(S["qk"], n + 1)
                from_first(act, "cum", n - 1)
                nc.scalar.copy(v1[t % 2][:, 0:D], p_qkv[:, 2 * D:3 * D]).then_inc(S["v"], 1)
                nc.scalar.copy(kv[t % 2][:, KV1:KV1 + D], qk[t % 2][:, D:2 * D]).then_inc(S["kc"], 1)

            def keep_queries(g, t):
                n, tb = tile_number(g, t), g[1] * G + t
                act.wait_ge(S["pqT"], n + 1)
                from_first(act, "prev", prevs(g[0], tb - 2))
                nc.scalar.copy(qT[t % 2][:, :], p_T[:, 0:P]).then_inc(S["qT"], 1)

            def exps(g):
                act.wait_ge(S["shift"], number(g) + 1)
                nc.scalar.activation(prob[:, :, :], prob[:, :, :], ACT.Exp).then_inc(S["exp"], 1)

            def normalise(g, k):
                n = number(g)
                apart(act, S[f"rstd_{k}"], 2 * n + 2, passed)
                if not (isinstance(n, int) and n == 0):
                    apart(act, S[f"pxT_{k}"], n, passed)
                    if k == "c":
                        apart(act, S["kept"], n, passed)
                for t in range(G):
                    last = nc.scalar.activation(xn[k][:, t, :], group_of(X, g)[:, t, :], ACT.Identity,
                                                bias=shift[k][:, t:t + 1], scale=rstd[k][:, t:t + 1])
                last.then_inc(S[f"xn_{k}"], 1)

            def iteration(g):
                before = after(g, -1)
                for t in range(G):
                    if exists(g):
                        keep_sums(g, t)
                    if exists(next_tile(g, t)[0]):
                        keep_values(*next_tile(g, t))
                    if t == 0 and exists(after(g, -2)):
                        exps(after(g, -2))
                    if t == 0 and exists(before):
                        keep_output(before)
                    if t == 1 and exists(after(g)):
                        root(after(g), "a")
                    if t == 2 and exists(after(g)):
                        keep_turned(after(g), "a")
                    if t == 2 and exists(before):
                        root(before, "c")
                    if t == 3 and exists(before):
                        keep_turned(before, "c")
                        keep_rows(before)
                    if exists(next_tile(g, t)[0]):
                        keep_queries(*next_tile(g, t))
                    if t == 1 and exists(after(g)):
                        normalise(after(g), "a")
                    if t == 2 and exists(before):
                        normalise(before, "c")

            groups(act, iteration)

        @block.vector
        def _(dve):
            def clip(g):
                dve.wait_ge(S["moe"], number(g) + 1)
                nc.vector.tensor_scalar(moe[:, :, :], moe[:, :, :], 100.0, -100.0, ALU.min, ALU.max).then_inc(S["clip"], 1)

            def add_moe(g):
                apart(dve, S["clip"], number(g) + 1, passed)
                nc.vector.tensor_tensor(group_of(X, g), group_of(X, g), moe[:, :, :], ALU.add).then_inc(S["x_a"], 1)

            def statistics(g, k):
                apart(dve, S[f"x_{k}"], number(g) + 1, passed)
                for t in range(G):
                    last = nc.vector.bn_stats(stats[k][:, t, :], group_of(X, g)[:, t, :])
                last.then_inc(S[f"stats_{k}"], 1)

            def moments(g, k):
                apart(dve, S[f"stats_{k}"], 2 * number(g) + 1, passed)
                for t in range(G):
                    last = nc.vector.bn_aggr(mv[k][:, t, :], stats[k][:, t, :])
                last.then_inc(S[f"stats_{k}"], 1)

            def variances(g, k):
                n = number(g)
                dve.wait_ge(S[f"stats_{k}"], 2 * n + 2)
                from_first(dve, f"xn_{k}", n)
                nc.vector.tensor_scalar(rstd[k][:, :], mv[k][:, :, 1], LN_EPS, None, ALU.add).then_inc(S[f"var_{k}"], 1)

            def scales(g, k):
                n = number(g)
                dve.wait_ge(S[f"root_{k}"], n + 1)
                nc.vector.reciprocal(rstd[k][:, :], rstd[k][:, :]).then_inc(S[f"rstd_{k}"], 1)
                dve.wait_ge(S[f"rstd_{k}"], 2 * n + 1)
                from_first(dve, f"xn_{k}", n)
                nc.vector.scalar_tensor_tensor(out=shift[k][:, :], in0=mv[k][:, :, 0], scalar=-1.0, in1=rstd[k][:, :],
                                               op0=ALU.mult, op1=ALU.mult).then_inc(S[f"rstd_{k}"], 1)

            def features(g, t):
                n, s = tile_number(g, t), t % 2
                dve.wait_ge(S["qkv"], n + 1)
                from_first(dve, "cum", n - 1)
                nc.vector.tensor_scalar(qk[s][:, :], p_qkv[:, 0:2 * D], 0.0, FEAT_EPS, ALU.max, ALU.add).then_inc(S["qk"], 1)

            def attend_tile(g, t):
                n, tb, s = tile_number(g, t), g[1] * G + t, t % 2
                q = qk[s][:, 0:D].rearrange("p (h d) -> p h d", h=H1)
                dve.wait_ge(S["cum"], n + 1)
                from_first(dve, "o", n)
                nc.vector.tensor_tensor(prod[:, KV1:KV1 + D], p_cum[:, 2, 0:D], qk[s][:, 0:D], ALU.mult).then_inc(S["prod"], 1)
                for a in range(2):
                    hs = slice(a * H1 // 2, (a + 1) * H1 // 2)
                    last = nc.vector.tensor_tensor(prod[:, a * 512:(a + 1) * 512].rearrange("p (h d m) -> p h d m", d=DH1, m=DH1),
                                                   p_cum[:, a, :].rearrange("p (h d m) -> p h d m", d=DH1, m=DH1),
                                                   q[:, hs, :].unsqueeze(3).broadcast_to([P, H1 // 2, DH1, DH1]), ALU.mult)
                last.then_inc(S["prod"], 1)
                dve.wait_ge(S["prod"], 2 * n + 1)
                nc.vector.tensor_reduce(den[:, :], prod[:, KV1:KV1 + D].rearrange("p (h d) -> p h d", h=H1), AX.X, ALU.add).then_inc(S["den"], 1)
                dve.wait_ge(S["prod"], 2 * n + 2)
                nc.vector.tensor_reduce(num[:, :].rearrange("p (h m) -> p h m", h=H1),
                                        prod[:, 0:KV1].rearrange("p (h d m) -> p h m d", h=H1, d=DH1), AX.X, ALU.add).then_inc(S["num"], 1)
                dve.wait_ge(S["den"], 3 * n + 1)
                if tb > 0:
                    dve.wait_ge(S["prev"], prevs(g[0], tb))
                    nc.vector.scalar_tensor_tensor(out=den[:, :], in0=den[:, :], scalar=FEAT_EPS,
                                                   in1=p_prev[:, D:D + H1], op0=ALU.add, op1=ALU.add).then_inc(S["den"], 1)
                    dve.wait_ge(S["num"], n + 1)
                    nc.vector.tensor_tensor(num[:, :], num[:, :], p_prev[:, 0:D], ALU.add)
                else:
                    nc.vector.tensor_scalar(den[:, :], den[:, :], FEAT_EPS, None, ALU.add).then_inc(S["den"], 1)
                dve.wait_ge(S["den"], 3 * n + 2)
                nc.vector.reciprocal(den[:, :], den[:, :]).then_inc(S["den"], 1)
                dve.wait_ge(S["den"], 3 * n + 3)
                if t == 0:
                    from_first(dve, "poT", number(g))
                nc.vector.tensor_tensor(o[:, t, :].rearrange("p (h m) -> p h m", h=H1), num[:, :].rearrange("p (h m) -> p h m", h=H1),
                                        den[:, :].unsqueeze(2).broadcast_to([P, H1, DH1]), ALU.mult).then_inc(S["o"], 1)

            def add_output(g):
                dve.wait_ge(S["y"], number(g) + 1)
                nc.vector.tensor_tensor(group_of(X, g), group_of(X, g), p_y[:, :, :], ALU.add).then_inc(S["x_c"], 1)

            wide = [P, G, E1]

            def shift_logits(g):
                n = number(g)
                logits = p_y[:, 0, 0:G * E1].rearrange("p (t e) -> p t e", e=E1)
                dve.wait_ge(S["logits"], n + 1)
                nc.vector.tensor_reduce(top[:, :], logits, AX.X, ALU.max).then_inc(S["top"], 1)
                dve.wait_ge(S["top"], n + 1)
                nc.vector.tensor_tensor(prob[:, :, :], logits, top[:, :].unsqueeze(2).broadcast_to(wide), ALU.subtract).then_inc(S["shift"], 1)

            def choose(g, step):
                n = number(g)
                if step == 0:
                    dve.wait_ge(S["exp"], n + 1)
                    nc.vector.tensor_reduce(total[:, :], prob[:, :, :], AX.X, ALU.add).then_inc(S["router"], 1)
                elif step == 1:
                    dve.wait_ge(S["router"], ROUTER * n + 1)
                    nc.vector.reciprocal(total[:, :], total[:, :]).then_inc(S["router"], 1)
                elif step == 2:
                    dve.wait_ge(S["router"], ROUTER * n + 2)
                    nc.vector.tensor_tensor(prob[:, :, :], prob[:, :, :], total[:, :].unsqueeze(2).broadcast_to(wide),
                                            ALU.mult).then_inc(S["router"], 1)
                elif step == 3:
                    apart(dve, S["router"], ROUTER * n + 3, passed)
                    for t in range(G):
                        last = nc.vector.max(best[:, t, :], prob[:, t, :])
                    last.then_inc(S["router"], 1)
                elif step == 4:
                    apart(dve, S["router"], ROUTER * n + 4, passed)
                    for t in range(G):
                        last = nc.vector.max_index(at[:, t, :], best[:, t, :], prob[:, t, :])
                    last.then_inc(S["router"], 1)
                elif step == 5:
                    dve.wait_ge(S["router"], ROUTER * n + 5)
                    nc.vector.tensor_copy(atf[:, :], at[:, :, 0]).then_inc(S["router"], 1)
                else:
                    dve.wait_ge(S["router"], ROUTER * n + 6)
                    nc.vector.tensor_tensor(HOT[:, :, bass.ds(n * G, G)].rearrange("p e t -> p t e"),
                                            c["iota"][:, 0:E1].unsqueeze(1).broadcast_to(wide),
                                            atf[:, :].unsqueeze(2).broadcast_to(wide), ALU.is_equal)
                    nc.vector.tensor_copy(BESTP[:, bass.ds(n * G, G)], best[:, :, 0]).then_inc(S["router"], 1)

            ROUTER = 7

            def iteration(g):
                before, coming, choosing = after(g, -1), after(g), after(g, -2)
                for t in range(G):
                    if exists(next_tile(g, t)[0]):
                        features(*next_tile(g, t))
                    if exists(g):
                        attend_tile(g, t)
                    if t == 0:
                        for first, step in ((clip, 0), (add_moe, 1), (None, 2), (statistics, 3), (moments, 4), (variances, 5), (None, 6)):
                            if first and exists(coming):
                                first(coming, *(("a",) if first in (statistics, moments, variances) else ()))
                            if exists(choosing):
                                choose(choosing, step)
                    if t == 1:
                        if exists(before):
                            add_output(before)
                        if exists(coming):
                            scales(coming, "a")
                        if exists(before):
                            statistics(before, "c")
                            moments(before, "c")
                            variances(before, "c")
                    if t == 2 and exists(before):
                        scales(before, "c")
                    if t == 3 and exists(before):
                        shift_logits(before)

            groups(dve, iteration)


BITS = 27

STEPS = 9

assert BITS % STEPS == 0


def capacity(nc, c, XN, BESTP, HOT, tabs, xs):
    with ExitStack() as ctx:
        def sb(name, shape, dt=F32):
            return ctx.enter_context(nc.sbuf_tensor(f"cp_{name}", shape, dt))

        sem = semaphores(ctx, nc, "cp", True)

        ET = [P, E1, TILES]
        p_of, cmp, equal, keep, place, tiles_before = (sb(n, ET) for n in ("p_of", "cmp", "equal", "keep", "place", "before"))
        count, level, trial, bit, rise, room, start, zero = (sb(n, [P, E1]) for n in
                                                             ("count", "level", "trial", "bit", "rise", "room", "start", "zero"))
        none = sb("none", [P, TILES])
        slotf, token = sb("slotf", [P, TILES]), sb("token", [P, TILES])
        R = 4
        xn = [sb(f"xn{s}", [P, G, D + 1]) for s in range(R)]
        slot = [sb(f"slot{s}", [P, G], I32) for s in range(R)]
        zeros = sb("zeros", [P, E1 + surplus_of(1, E1), BT // P, D + 1])
        p_count = ctx.enter_context(nc.psum_tensor("cp_p_count", [P, 512], F32))
        p_rank = ctx.enter_context(nc.psum_tensor("cp_p_rank", [P, E1, TILES], F32))
        p_tiles = ctx.enter_context(nc.psum_tensor("cp_p_tiles", [P, E1, TILES], F32))
        step_d, counted, total_d, loop_d, ranks, slots_d, copied, surplus_out, tails_out, passed = (
            sem(n) for n in ("step", "counted", "total", "loop", "ranks", "slots", "copied", "surplus_out", "tails_out", "passed"))
        tokens_d, sent = sem("tokens"), sem("sent")
        rows_out = [sem(f"rows_out{s}") for s in range(R)]
        SENT0 = R
        block = ctx.enter_context(nc.Block())
        wide = lambda a: a.unsqueeze(2).broadcast_to(ET)

        @block.tensor
        def _(pe):
            with pe.Fori(0, BITS // STEPS) as r:
                for m in range(STEPS):
                    pe.wait_ge(counted, r * STEPS + m + 1)
                    nc.tensor.matmul(p_count[:, 0:E1], c["ones"][:, :], count[:, :], start=True, stop=True).then_inc(total_d, 1)
            pe.wait_ge(counted, BITS + 1)
            nc.tensor.matmul(p_count[:, 0:E1], c["ones"][:, :], count[:, :], start=True, stop=True).then_inc(total_d, 1)
            for n, src in enumerate((equal, keep)):
                pe.wait_ge(counted, BITS + 2 + n)
                nc.tensor.matmul(p_rank[:, :, :], c["stri"][:, :], src[:, :, :], start=True, stop=True)
                nc.tensor.matmul(p_tiles[:, :, :], c["ones"][:, :], src[:, :, :], start=True, stop=True).then_inc(ranks, 1)

        @block.vector
        def _(dve):
            n = [0]

            def step(ins):
                n[0] += 1
                ins.then_inc(step_d, 1)
                dve.wait_ge(step_d, n[0])

            step(nc.vector.memset(zero[:, :], 0.0))
            step(nc.vector.memset(none[:, :], 0.0))
            step(nc.vector.tensor_scalar(start[:, :], c["iota"][:, 0:E1], float(REGION), None, ALU.mult))
            step(nc.vector.tensor_tensor(p_of[:, :, :], HOT[:, :, :], BESTP[:, :].unsqueeze(1).broadcast_to(ET), ALU.mult))
            step(nc.vector.tensor_tensor(p_of[:, :, :], p_of[:, :, :], HOT[:, :, :], ALU.add))
            step(nc.vector.tensor_scalar(p_of[:, :, :], p_of[:, :, :], -1.0, None, ALU.add))
            step(nc.vector.memset(level[:, :], 0.0))
            step(nc.vector.memset(trial[:, :], 0.5))
            step(nc.vector.memset(bit[:, :], 0.5))
            with dve.Fori(0, BITS // STEPS) as r:
                for m in range(STEPS):
                    k = r * STEPS + m
                    nc.vector.tensor_tensor(cmp[:, :, :], p_of[:, :, :], wide(trial[:, :]), ALU.is_ge).then_inc(loop_d, 1)
                    dve.wait_ge(loop_d, k * 4 + 1)
                    nc.vector.tensor_reduce(count[:, :], cmp[:, :, :], AX.X, ALU.add).then_inc(counted, 1)
                    dve.wait_ge(total_d, k + 1)
                    nc.vector.scalar_tensor_tensor(out=rise[:, :], in0=p_count[:, 0:E1], scalar=float(CAP1), in1=bit[:, :],
                                                   op0=ALU.is_ge, op1=ALU.mult).then_inc(loop_d, 1)
                    dve.wait_ge(loop_d, k * 4 + 2)
                    nc.vector.tensor_tensor(level[:, :], level[:, :], rise[:, :], ALU.add)
                    nc.vector.tensor_scalar(bit[:, :], bit[:, :], 0.5, None, ALU.mult).then_inc(loop_d, 1)
                    dve.wait_ge(loop_d, k * 4 + 3)
                    nc.vector.tensor_tensor(trial[:, :], level[:, :], bit[:, :], ALU.add).then_inc(loop_d, 1)
                    dve.wait_ge(loop_d, k * 4 + 4)
            step(nc.vector.tensor_tensor(keep[:, :, :], p_of[:, :, :], wide(level[:, :]), ALU.is_gt))
            nc.vector.tensor_reduce(count[:, :], keep[:, :, :], AX.X, ALU.add).then_inc(counted, 1)
            dve.wait_ge(total_d, BITS + 1)
            step(nc.vector.tensor_scalar(room[:, :], p_count[:, 0:E1], -1.0, float(CAP1), ALU.mult, ALU.add))
            nc.vector.tensor_tensor(equal[:, :, :], p_of[:, :, :], wide(level[:, :]), ALU.is_equal).then_inc(counted, 1)

            def rank(k):
                dve.wait_ge(ranks, k)
                for e in range(E1):
                    last = nc.vector.tensor_tensor_scan(tiles_before[:, e, :], p_tiles[:, e, :], none[:, :], 0.0, ALU.add, ALU.add)
                step(last)
                step(nc.vector.tensor_copy(count[:, :], tiles_before[:, :, TILES - 1]))
                step(nc.vector.tensor_tensor(tiles_before[:, :, :], tiles_before[:, :, :], p_tiles[:, :, :], ALU.subtract))
                step(nc.vector.tensor_tensor(place[:, :, :], tiles_before[:, :, :], p_rank[:, :, :], ALU.add))

            rank(1)
            step(nc.vector.tensor_tensor(cmp[:, :, :], place[:, :, :], wide(room[:, :]), ALU.is_lt))
            step(nc.vector.tensor_tensor(cmp[:, :, :], cmp[:, :, :], equal[:, :, :], ALU.mult))
            step(nc.vector.tensor_tensor(keep[:, :, :], keep[:, :, :], cmp[:, :, :], ALU.add))
            step(nc.vector.tensor_reduce(slotf[:, :], keep[:, 1:E1, :].rearrange("p e t -> p t e"), AX.X, ALU.add))
            nc.vector.tensor_scalar(keep[:, 0, :], slotf[:, :], -1.0, 1.0, ALU.mult, ALU.add).then_inc(counted, 1)
            rank(2)
            step(nc.vector.tensor_tensor(place[:, :, :], place[:, :, :], wide(start[:, :]), ALU.add))
            step(nc.vector.tensor_tensor(place[:, :, :], place[:, :, :], keep[:, :, :], ALU.mult))
            nc.vector.tensor_reduce(slotf[:, :], place[:, :, :].rearrange("p e t -> p t e"), AX.X, ALU.add).then_inc(slots_d, 1)
            block_table(nc, dve, c, count[:, :], E1, blocks_of(1, E1), tabs, slots_d, 1)

        @block.sync
        def _(sp):
            sp.wait_ge(tokens_d, 3)
            zero_surplus(sp, xs, lambda n: zeros[:, E1 + n], E1, surplus_of(1, E1), surplus_out)
            sp.wait_ge(slots_d, 1 + TAIL_STEPS)
            zero_tails(sp, xs, lambda e: zeros[:, e], tabs, range(E1), E1, tails_out)
            sp.wait_ge(surplus_out, surplus_of(1, E1) * 16)
            sp.wait_ge(tails_out, E1 * 16)

        @block.scalar
        def _(act):
            act.wait_ge(tokens_d, 1)
            act.sem_inc(passed, 1)
            act.wait_ge(slots_d, 1)
            act.sem_inc(passed, 1)
            with act.Fori(0, GROUPS // R) as r:
                for s in range(R):
                    g = r * R + s
                    apart(act, sent, SENT0 + g - R + 1, passed)
                    nc.scalar.copy(slot[s][:, :], slotf[:, bass.ds(g * G, G)])
                    nc.scalar.copy(xn[s][:, :, D], token[:, bass.ds(g * G, G)])
                    nc.scalar.copy(xn[s][:, :, 0:D], XN[:, bass.ds(g * GT, GT)].rearrange("p (t d) -> p t d", t=G)).then_inc(copied, 1)

        @block.gpsimd
        def _(pool):
            def scatter(r, s):
                apart(pool, copied, r * R + s + 1, passed)
                for t in range(G):
                    pool.indirect_dma_start(xs[:, :], bass.IndirectOffsetOnAxis(ap=slot[s][:, t:t + 1], axis=0),
                                            xn[s][:, t, :], None).then_inc(rows_out[s], 16)

            def scattered(r, s):
                apart(pool, rows_out[s], (r + 1) * G * 16, sent)

            nc.gpsimd.iota(token[:, :], pattern=[[P, TILES]], base=0, channel_multiplier=1,
                           allow_small_or_imprecise_dtypes=True).then_inc(tokens_d, 1)
            nc.gpsimd.memset(zeros[:, :, :, :], 0.0).then_inc(tokens_d, 1)
            pool.wait_ge(tokens_d, 2)
            nc.gpsimd.iota(zeros[:, :, :, D], pattern=[[BT, E1 + surplus_of(1, E1)], [1, BT // P]], base=NTOK,
                           channel_multiplier=BT // P, allow_small_or_imprecise_dtypes=True).then_inc(tokens_d, 1)
            pool.sem_inc(sent, SENT0)
            scatter(0, 0)
            with pool.Fori(0, GROUPS // R - 1) as r:
                for s in range(R):
                    scatter(r + (s + 1) // R, (s + 1) % R)
                    scattered(r, s)
            for s in range(R):
                if s + 1 < R:
                    scatter(GROUPS // R - 1, s + 1)
                scattered(GROUPS // R - 1, s)


def finish(nc, X, ys, out):
    with ExitStack() as ctx:
        R = 4
        rows = [ctx.enter_context(nc.sbuf_tensor(f"fi_rows{s}", [P, G, D], F32)) for s in range(R)]
        sem = semaphores(ctx, nc, "fi", True)
        rows_in = [sem(f"rows_in{s}") for s in range(R)]
        sum_d, out_d, passed = (sem(n) for n in ("sum", "out", "passed"))
        SUM0 = R
        block = ctx.enter_context(nc.Block())
        out_v = out.rearrange("b t d -> (b t) d").rearrange("(g t p) d -> p g t d", p=P, t=G)
        ys_v = ys[0:NTOK, :].rearrange("(g t p) d -> p g t d", p=P, t=G)

        @block.sync
        def _(sp):
            with sp.Fori(0, GROUPS // R) as r:
                for s in range(R):
                    g = r * R + s
                    apart(sp, sum_d, SUM0 + g - R + 1, passed)
                    sp.dma_start(rows[s][:, :, :], ys_v[:, bass.ds(g, 1)].rearrange("p o t d -> p (o t) d")).then_inc(rows_in[s], 16)

        @block.vector
        def _(dve):
            dve.sem_inc(sum_d, SUM0)
            with dve.Fori(0, GROUPS // R) as r:
                for s in range(R):
                    Xg = X[:, bass.ds((r * R + s) * GT, GT)].rearrange("p (t d) -> p t d", t=G)
                    dve.wait_ge(rows_in[s], (r + 1) * 16)
                    nc.vector.tensor_tensor(Xg, Xg, rows[s][:, :, :], ALU.add).then_inc(sum_d, 1)

        @block.scalar
        def _(act):
            with act.Fori(0, GROUPS) as g:
                apart(act, sum_d, SUM0 + g + 1, passed)
                act.dma_start(out_v[:, bass.ds(g, 1)].rearrange("p o t d -> p (o t) d"),
                              X[:, bass.ds(g * GT, GT)].rearrange("p (t d) -> p t d", t=G)).then_inc(out_d, 16)
            act.wait_ge(out_d, GROUPS * 16)


def program(nc, a, out, upto=99):
    with ExitStack() as ctx:
        def sb(n, shape, dt=F32):
            return ctx.enter_context(nc.sbuf_tensor(n, shape, dt))

        def dram(n, shape, dt=F32):
            return nc.dram_tensor(n, shape, dt, kind="Internal").ap()

        c = {n: sb(f"c_{n}", [P, P]) for n in ("ident", "tri", "stri", "ones", "iota")}
        X, XN = sb("X", [P, TILES * D]), sb("XN", [P, TILES * D])
        GATE, SLOT = sb("GATE", [P, TILES * 2]), sb("SLOT", [P, TILES * 2], I32)
        q3, k3 = dram("q3", [3, UNITS, DH0, T], BF16), dram("k3", [3, UNITS, DH0, T], BF16)
        v0, o0 = dram("v0", [UNITS, P, KT * DH0]), dram("o0", [UNITS, DH0, T])
        xs0, ys0 = dram("xs0", [E0 * REGION + surplus_of(2, E0) * BT, D]), dram("ys0", [blocks_of(2, E0) * BT, D])
        NB0 = blocks_of(2, E0)
        xs1, ys1 = dram("xs1", [E1 * REGION + surplus_of(1, E1) * BT, D + 1]), dram("ys1", [NTOK + (E1 + surplus_of(1, E1)) * BT, D])
        NB1 = blocks_of(1, E1)
        BESTP, HOT = sb("BESTP", [P, TILES]), sb("HOT", [P, E1, TILES])
        tabs1 = tables(ctx, nc, "t1", 1, E1)
        tabs0 = tables(ctx, nc, "t0", 2, E0)
        constants(nc, c)
        project(nc, c, X, a["x"], a, q3, k3, v0)
        if upto >= 2:
            attend(nc, c, q3, k3, v0, o0)
        if upto >= 3:
            route2(nc, c, X, XN, GATE, SLOT, tabs0, a, o0, xs0)
        if upto >= 4:
            experts(nc, c, "e0", True, E0, F0, ACT.Gelu, tabs0, NB0, surplus_of(2, E0), a["weights0"], a["b2"], xs0, ys0, False, SLOT[:, :])
        if upto >= 5:
            linear(nc, c, X, XN, GATE, SLOT, BESTP, HOT, a, ys0)
        if upto >= 6:
            capacity(nc, c, XN, BESTP, HOT, tabs1, xs1)
        if upto >= 7:
            experts(nc, c, "e1", False, E1, F1, ACT.Relu, tabs1, NB1, surplus_of(1, E1), a["weights1"], a["B2"], xs1, ys1, True)
        if upto >= 8:
            finish(nc, X, ys1, out)


def layout(d):
    import numpy as np
    t = lambda a: np.ascontiguousarray(np.swapaxes(a, -1, -2))

    def expert_rows(w1, b1, w2):
        E = w1.shape[0]
        return np.concatenate([w1, b1.reshape(E, -1, P).transpose(0, 2, 1),
                               w2.reshape(E, -1, P, D).transpose(0, 2, 1, 3).reshape(E, P, -1)], axis=2)

    return {"x": d["L0_attn_x"], "WqT": t(d["L0_attn_Wq"]), "WdT": t(d["L0_attn_Wkv_down"]),
            "WkuT": t(d["L0_attn_Wk_up"]), "WvuT": t(d["L0_attn_Wv_up"]), "WoT": t(d["L0_attn_Wo"]),
            "gateT": t(d["L0_ffn_gate_w"]), "b2": d["L0_ffn_b2"],
            "weights0": expert_rows(d["L0_ffn_w1"], d["L0_ffn_b1"], d["L0_ffn_w2"]),
            "WqkvT": np.concatenate([t(d["L1_attn_Wq"]), t(d["L1_attn_Wk"]), t(d["L1_attn_Wv"])], axis=1),
            "Wo1T": t(d["L1_attn_Wo"]), "routerT": t(d["L1_ffn_router_w"]), "B2": d["L1_ffn_b2"],
            "weights1": expert_rows(d["L1_ffn_W1"], d["L1_ffn_b1"], d["L1_ffn_W2"])}


def kernel(**inputs):
    import numpy as np
    import concourse.bacc as bacc
    from concourse.bass_utils import run_bass_kernel_spmd

    arrays = {k: np.ascontiguousarray(v) for k, v in layout({k: np.asarray(v) for k, v in inputs.items()}).items()}
    nc = bacc.Bacc("TRN2", target_bir_lowering=False, num_devices=1)
    a = {k: nc.dram_tensor(f"in_{k}", v.shape, mybir.dt.from_np(v.dtype), kind="ExternalInput").ap()
         for k, v in arrays.items()}
    out = nc.dram_tensor("out_0", (B, T, D), F32, kind="ExternalOutput").ap()
    program(nc, a, out)
    r = run_bass_kernel_spmd(nc, [{f"in_{k}": v for k, v in arrays.items()}], core_ids=[0])
    return r.results[0]["out_0"]
```
